# Optimizing a Trainium2 kernel written in Bass

```python
import numpy as np
import jax
import jax.numpy as jnp

def _softmax(x, axis=-1):
    return jax.nn.softmax(x, axis=axis)

def _gelu(x):
    return jax.nn.gelu(x, approximate=True)

def _silu(x):
    return jax.nn.silu(x)

def _sigmoid(x):
    return jax.nn.sigmoid(x)

def _layernorm(x, axis=-1, eps=1e-05):
    m = jnp.mean(x, axis=axis, keepdims=True)
    v = jnp.var(x, axis=axis, keepdims=True)
    return (x - m) / jnp.sqrt(v + eps)

def _scatter_add(tgt, idx, src, axis=0):
    return tgt.at[idx].add(src)

def _segment_sum(src, seg, n):
    return jax.ops.segment_sum(src, seg, n)
kernel_name = 'mk_decoder_postln_d1_seqx_r4_959c32'

def setup_inputs(seed: int=0):
    np.random.seed(seed)
    _w = jnp.asarray

    def _rec_inputs():
        import jax
        import jax.numpy as jnp
        _rk = jax.random.key(seed)
        x = -0.0002928 + 1 * jax.random.normal(jax.random.fold_in(_rk, 1), (64, 128, 256), jnp.float32)
        _lenS = 128 - jax.random.randint(jax.random.fold_in(_rk, 7), (64,), 0, max(1, 128 // 4) + 1, jnp.int32)
        _lenS2 = 128 - jax.random.randint(jax.random.fold_in(_rk, 8), (64,), 0, max(1, 128 // 4) + 1, jnp.int32)
        _ctx_1024P = jax.random.normal(jax.random.fold_in(_rk, 11), (64, 16, 256), jnp.float32)
        _ctx_1024c = jax.random.dirichlet(jax.random.fold_in(_rk, 511), 0.3 * jnp.ones((16,), jnp.float32), (64, 128))
        _ctx_1024t = jnp.einsum('bsk,bkd->bsd', _ctx_1024c, _ctx_1024P)
        _ctx_1024t = _ctx_1024t * jax.lax.rsqrt(jnp.mean(jnp.square(_ctx_1024t)) + 1e-12) * 0.953939
        ctx_1024 = -1.39393e-06 + 0.999914 * (_ctx_1024t + 0.3 * jax.random.normal(jax.random.fold_in(_rk, 611), (64, 128, 256), jnp.float32))
        _validS = jnp.arange(128)[None, :] < _lenS[:, None]
        _validS2 = jnp.arange(128)[None, :] < _lenS2[:, None]
        _causal = jnp.tril(jnp.ones((128, 128), dtype=bool))
        mask_Bx16xSxS2_ff0 = jnp.where(jnp.ones((64, 16, 128, 128), dtype=bool), 0.0, -1000000000.0).astype(jnp.float32)
        return (x, ctx_1024, mask_Bx16xSxS2_ff0)
    x, ctx_1024, mask_Bx16xSxS2_ff0 = _rec_inputs()

    def _L0_attn_setup():
        import jax, jax.numpy as jnp
        import numpy as np
        HIDDEN = 256
        N_HEADS = 16
        HEAD_DIM = HIDDEN // N_HEADS
        WINDOW = 64
        HALF_W = WINDOW // 2
        GLOBAL_TOKENS = (0,)

        def _longformer_mask(seq_len: int) -> jnp.ndarray:
            idx = jnp.arange(seq_len)
            mask = jnp.abs(idx[:, None] - idx[None, :]) <= HALF_W
            for g in GLOBAL_TOKENS:
                if 0 <= g < seq_len:
                    mask = mask.at[g, :].set(True)
                    mask = mask.at[:, g].set(True)
            return mask
        key = jax.random.key(seed)
        ks = jax.random.split(key, 5)
        B, S = (1, 1024)
        scale = 0.02
        return {'x': jax.random.normal(ks[0], (B, S, HIDDEN), dtype=jnp.float32), 'Wq': jax.random.normal(ks[1], (HIDDEN, HIDDEN), dtype=jnp.float32) * scale, 'Wk': jax.random.normal(ks[2], (HIDDEN, HIDDEN), dtype=jnp.float32) * scale, 'Wv': jax.random.normal(ks[3], (HIDDEN, HIDDEN), dtype=jnp.float32) * scale, 'Wo': jax.random.normal(ks[4], (HIDDEN, HIDDEN), dtype=jnp.float32) * scale}
    _L0_attn_all = _L0_attn_setup()
    _L0_attn_in = {k: v for k, v in _L0_attn_all.items() if k in ('Wq', 'Wk', 'Wv', 'Wo')}
    del _L0_attn_all

    def _L0_xattn_setup():
        import jax, jax.numpy as jnp
        import numpy as np
        B, S, D = (2, 512, 256)
        H = 16
        DH = D // H
        LAMBDA_INIT = 0.8
        EPS = 1e-05
        SCALE = 1.0 / np.sqrt(DH)
        key = jax.random.key(seed)
        ks = jax.random.split(key, 13)
        inp = {'query': jax.random.normal(ks[0], (B, S, D), jnp.float32), 'key': jax.random.normal(ks[1], (B, S, D), jnp.float32), 'value': jax.random.normal(ks[2], (B, S, D), jnp.float32), 'attn_mask': jnp.zeros((B, H, S, S), jnp.float32), 'W_q': jax.random.normal(ks[3], (D, 2 * DH * H), jnp.float32) * 0.02, 'W_k': jax.random.normal(ks[4], (D, 2 * DH * H), jnp.float32) * 0.02, 'W_v': jax.random.normal(ks[5], (D, DH * H), jnp.float32) * 0.02, 'W_o': jax.random.normal(ks[6], (DH * H, D), jnp.float32) * 0.02, 'lambda_q1': jax.random.normal(ks[7], (H, DH), jnp.float32) * 0.1, 'lambda_k1': jax.random.normal(ks[8], (H, DH), jnp.float32) * 0.1, 'lambda_q2': jax.random.normal(ks[9], (H, DH), jnp.float32) * 0.1, 'lambda_k2': jax.random.normal(ks[10], (H, DH), jnp.float32) * 0.1, 'rms_scale': jnp.ones((DH,), jnp.float32)}
        return inp
    _L0_xattn_all = _L0_xattn_setup()
    _L0_xattn_in = {k: v for k, v in _L0_xattn_all.items() if k in ('W_q', 'W_k', 'W_v', 'W_o', 'lambda_q1', 'lambda_k1', 'lambda_q2', 'lambda_k2', 'rms_scale')}
    del _L0_xattn_all

    def _L0_ffn_setup():
        import jax, jax.numpy as jnp
        import numpy as np
        B, M, D = (4, 512, 256)
        N, P = (64, 32)
        key = jax.random.key(seed)
        k1, k2, k3, k4 = jax.random.split(key, 4)
        x = jax.random.normal(k1, (B, M, D), dtype=jnp.float32)
        phi = jax.random.normal(k2, (D, N, P), dtype=jnp.float32) * (1.0 / np.sqrt(D))
        W = jax.random.normal(k3, (N, D, D), dtype=jnp.float32) * (1.0 / np.sqrt(D))
        b = jax.random.normal(k4, (N, D), dtype=jnp.float32) * 0.01
        return {'x': x, 'phi': phi, 'W': W, 'b': b}
    _L0_ffn_all = _L0_ffn_setup()
    _L0_ffn_in = {k: v for k, v in _L0_ffn_all.items() if k in ('phi', 'W', 'b')}
    del _L0_ffn_all
    return {'x': x, 'ctx_1024': ctx_1024, 'mask_Bx16xSxS2_ff0': mask_Bx16xSxS2_ff0, 'L0_attn_Wq': _L0_attn_in['Wq'], 'L0_attn_Wk': _L0_attn_in['Wk'], 'L0_attn_Wv': _L0_attn_in['Wv'], 'L0_attn_Wo': _L0_attn_in['Wo'], 'L0_xattn_W_q': _L0_xattn_in['W_q'], 'L0_xattn_W_k': _L0_xattn_in['W_k'], 'L0_xattn_W_v': _L0_xattn_in['W_v'], 'L0_xattn_W_o': _L0_xattn_in['W_o'], 'L0_xattn_lambda_q1': _L0_xattn_in['lambda_q1'], 'L0_xattn_lambda_k1': _L0_xattn_in['lambda_k1'], 'L0_xattn_lambda_q2': _L0_xattn_in['lambda_q2'], 'L0_xattn_lambda_k2': _L0_xattn_in['lambda_k2'], 'L0_xattn_rms_scale': _L0_xattn_in['rms_scale'], 'L0_ffn_phi': _L0_ffn_in['phi'], 'L0_ffn_W': _L0_ffn_in['W'], 'L0_ffn_b': _L0_ffn_in['b']}

def reference(x, ctx_1024, mask_Bx16xSxS2_ff0, L0_attn_Wq, L0_attn_Wk, L0_attn_Wv, L0_attn_Wo, L0_xattn_W_q, L0_xattn_W_k, L0_xattn_W_v, L0_xattn_W_o, L0_xattn_lambda_q1, L0_xattn_lambda_k1, L0_xattn_lambda_q2, L0_xattn_lambda_k2, L0_xattn_rms_scale, L0_ffn_phi, L0_ffn_W, L0_ffn_b):
    import jax
    import jax.numpy as jnp

    def _L0_attn_ref(x, Wq, Wk, Wv, Wo):
        import jax, jax.numpy as jnp
        import numpy as np
        HIDDEN = 256
        N_HEADS = 16
        HEAD_DIM = HIDDEN // N_HEADS
        WINDOW = 64
        HALF_W = WINDOW // 2
        GLOBAL_TOKENS = (0,)

        def _longformer_mask(seq_len: int) -> jnp.ndarray:
            idx = jnp.arange(seq_len)
            mask = jnp.abs(idx[:, None] - idx[None, :]) <= HALF_W
            for g in GLOBAL_TOKENS:
                if 0 <= g < seq_len:
                    mask = mask.at[g, :].set(True)
                    mask = mask.at[:, g].set(True)
            return mask
        B, S, H = x.shape
        scale = HEAD_DIM ** (-0.5)

        def proj(W):
            return jnp.einsum('bsh,oh->bso', x, W).reshape(B, S, N_HEADS, HEAD_DIM).transpose(0, 2, 1, 3)
        q, k, v = (proj(Wq), proj(Wk), proj(Wv))
        scores = jnp.einsum('bnsd,bntd->bnst', q, k) * scale
        mask = _longformer_mask(S)
        scores = jnp.where(mask[None, None], scores, jnp.float32(-jnp.inf))
        attn = jax.nn.softmax(scores, axis=-1)
        out = jnp.einsum('bnst,bntd->bnsd', attn, v)
        out = out.transpose(0, 2, 1, 3).reshape(B, S, H)
        return jnp.einsum('bsh,oh->bso', out, Wo)

    def _L0_xattn_ref(query, key, value, attn_mask, W_q, W_k, W_v, W_o, lambda_q1, lambda_k1, lambda_q2, lambda_k2, rms_scale):
        import jax, jax.numpy as jnp
        import numpy as np
        B, S, D = (2, 512, 256)
        H = 16
        DH = D // H
        LAMBDA_INIT = 0.8
        EPS = 1e-05
        SCALE = 1.0 / np.sqrt(DH)
        b, s, _ = value.shape
        q = (query @ W_q).reshape(b, s, H, 2 * DH).transpose(0, 2, 1, 3)
        k = (key @ W_k).reshape(b, s, H, 2 * DH).transpose(0, 2, 1, 3)
        v = (value @ W_v).reshape(b, s, H, DH).transpose(0, 2, 1, 3)
        q1, q2 = (q[..., :DH], q[..., DH:])
        k1, k2 = (k[..., :DH], k[..., DH:])
        lam = jnp.exp(jnp.sum(lambda_q1 * lambda_k1, -1)) - jnp.exp(jnp.sum(lambda_q2 * lambda_k2, -1)) + LAMBDA_INIT
        lam = lam[None, :, None, None]
        s1 = jnp.einsum('bhqd,bhkd->bhqk', q1, k1) * SCALE + attn_mask
        s2 = jnp.einsum('bhqd,bhkd->bhqk', q2, k2) * SCALE + attn_mask
        attn = jax.nn.softmax(s1, axis=-1) - lam * jax.nn.softmax(s2, axis=-1)
        out = jnp.einsum('bhqk,bhkd->bhqd', attn, v)
        rms = jnp.sqrt(jnp.mean(out * out, axis=-1, keepdims=True) + EPS)
        out = out / rms * rms_scale
        out = out * (1.0 - LAMBDA_INIT)
        out = out.transpose(0, 2, 1, 3).reshape(b, s, H * DH)
        return out @ W_o

    def _L0_ffn_ref(x, phi, W, b):
        import jax, jax.numpy as jnp
        import numpy as np
        B, M, D = (4, 512, 256)
        N, P = (64, 32)
        logits = jnp.einsum('bmd,dnp->bmnp', x, phi)
        dispatch = jax.nn.softmax(logits, axis=0)
        bsz, m, n, p = logits.shape
        combine = jax.nn.softmax(logits.reshape(bsz, m, n * p), axis=-1).reshape(bsz, m, n, p)
        slots = jnp.einsum('bmd,bmnp->bnpd', x, dispatch)
        y = jnp.einsum('bnpd,nde->bnpe', slots, W) + b[None, :, None, :]
        out = jnp.einsum('bnpd,bmnp->bmd', y, combine)
        return out
    x = _layernorm(x + _L0_attn_ref(x, L0_attn_Wq, L0_attn_Wk, L0_attn_Wv, L0_attn_Wo), axis=-1)
    x = _layernorm(x + _L0_xattn_ref(x, ctx_1024, ctx_1024, mask_Bx16xSxS2_ff0, L0_xattn_W_q, L0_xattn_W_k, L0_xattn_W_v, L0_xattn_W_o, L0_xattn_lambda_q1, L0_xattn_lambda_k1, L0_xattn_lambda_q2, L0_xattn_lambda_k2, L0_xattn_rms_scale), axis=-1)
    x = _layernorm(x + _L0_ffn_ref(x, L0_ffn_phi, L0_ffn_W, L0_ffn_b), axis=-1)
    return x

_drawn_inputs = setup_inputs


def setup_inputs(seed=0):
    import zlib

    import numpy as np

    out = dict(_drawn_inputs(seed))
    spreads = {'L0_xattn_rms_scale': (1.0, 0.6)}
    factors = {'L0_attn_Wq': 8.0,
     'L0_attn_Wk': 8.0,
     'L0_attn_Wv': 3.984,
     'L0_attn_Wo': 4.058,
     'L0_xattn_W_q': 3.176,
     'L0_xattn_W_k': 3.185,
     'L0_xattn_lambda_q1': 8.0,
     'L0_xattn_lambda_k1': 8.0,
     'L0_xattn_lambda_q2': 8.0,
     'L0_xattn_lambda_k2': 8.0,
     'L0_ffn_phi': 4.714,
     'L0_ffn_b': 8.0}
    for name, (base, spread) in spreads.items():
        noise = np.random.default_rng([zlib.crc32(name.encode()), seed]).standard_normal(out[name].shape)
        drawn = base * np.exp(spread * noise) if base else spread * noise
        out[name] = jnp.asarray(drawn.astype(out[name].dtype))
    for name, factor in factors.items():
        out[name] = (out[name] * factor).astype(out[name].dtype)
    return out
```

```python
import numpy as np
import concourse.bass as bass
from concourse import mybir
from contextlib import ExitStack

HI, LO = 0, 1
PASSES = ((HI, HI), (HI, LO), (LO, HI))


def decoder_layer(nc, x, ctx_in, mask, w_all, w_scale, lambdas, phi, w_ffn, b_ffn, ident_in, band_in, block_in, out):
    F32, F16 = mybir.dt.float32, mybir.dt.float16
    ALU, ACT, AX = mybir.AluOpType, mybir.ActivationFunctionType, mybir.AxisListType

    B, S, D = x.shape
    H = mask.shape[1]
    DH = D // H
    P = 128
    DT = D // P
    NP = phi.shape[2]
    E = w_ffn.shape[0]
    SP_E = NP // E
    EC = P // SP_E
    NCH = NP // P
    Q4 = 4
    NQ = B // Q4
    LN_EPS, RMS_EPS = 1e-5, 1e-5
    LAMBDA_INIT = 0.8
    OUT_SCALE = 1.0 - LAMBDA_INIT
    SCORE_SCALE = 1.0 / float(np.sqrt(DH))
    VW = DH + 1
    SQ, SK, SV, SO, CQ, CK, CV, CO, W_END = (int(c) for c in np.cumsum([0, D, D, D, D, 2 * D, 2 * D, D, D]))

    scratch_x2 = nc.dram_tensor("scratch_x2", [B, S, D], F32).ap()
    scratch_x2_parts = nc.dram_tensor("scratch_x2_parts", [B, S, 2 * D], F16).ap()

    es = ExitStack()
    with es:
        def sb(name, shape, dt=F32):
            return es.enter_context(nc.sbuf_tensor(name, shape, dt))

        def sem(name):
            return es.enter_context(nc.semaphore(name))

        bank = {n: es.enter_context(nc.psum_tensor(f"bank_{n}", [P, 512], F32))
                for n in ("turn", "proj", "score0", "score1", "prob0", "prob1", "s_value", "c_value")}

        xT = sb("xT", [P, 2, DT, B * S], F16)
        ident = sb("ident", [P, P])
        ARENA = (207 * 1024 - 2 * DT * B * S * 2 - P * 4) // 4
        arena = sb("arena", [P, ARENA])
        used = [0]

        def carve(shape, dt=F32):
            n = int(np.prod(shape))
            words = n if dt == F32 else (n + 1) // 2
            part = arena[:, used[0]:used[0] + words]
            used[0] += words
            assert used[0] <= ARENA, (used[0], ARENA)
            if dt != F32:
                part = part.bitcast(dt)
            if len(shape) > 1:
                names = "abcd"[:len(shape)]
                part = part.rearrange(f"p ({' '.join(names)}) -> p {' '.join(names)}", **dict(zip(names, shape)))
            return part

        w_parts = carve([2, DT, W_END], F16)
        c_mask = carve([H, S])
        c_prob = carve([2 * H, S])
        s_prob = carve([H, S])
        w_stage = c_prob.rearrange("p a b -> p (a b)")
        band = carve([S])
        blocks = carve([8])
        lam_in = carve([4, H, DH])
        lam_prod = carve([2, H, DH])
        lam_sum = carve([2, H])
        lam_exp = carve([2, H])
        lam_dif = carve([H])
        neg_lam = carve([H])
        w_rows = carve([DT])
        w_rows2 = carve([DT])
        s_kbd = carve([2, DT, 8, S], F16)
        c_kbd = carve([2, 2 * DT, 8, S], F16)
        s_in, s_res, c_in = carve([D]), carve([D]), carve([D])
        s_xT, s_oT, c_xT, c_cT, c_oT = (carve([2, DT, S], F16) for _ in range(5))
        s_qk = carve([2, 4, S], F16)
        c_q, c_k = carve([2, 4, S], F16), carve([2, 4, S], F16)
        s_v, c_v = carve([2, H, VW], F16), carve([2, H, DH], F16)
        s_pT, c_pT = carve([2, 2, Q4, S], F16), carve([2, 2, Q4, S], F16)
        s_max, c_max, c_negmax = carve([H]), carve([2 * H]), carve([2 * H])
        c_sum = carve([2 * H])
        s_rsum, c_rsum, c_r2, c_ratio, c_blend = (carve([H]) for _ in range(5))
        s_o, c_o, c_oraw, c_sq = carve([D]), carve([D]), carve([D]), carve([D])
        c_ss, c_ms, c_rms = carve([H]), carve([H]), carve([H])
        s_sum, c_sumx = carve([D]), carve([D])
        s_total, c_total, s_negmean, c_negmean, s_sq, c_sqx = (carve([1]) for _ in range(6))
        s_junk, c_junk = carve([D]), carve([D])
        s_veps, c_veps, s_rstd, c_rstd = carve([1]), carve([1]), carve([1]), carve([1])
        x1, x2 = carve([D]), carve([D])
        X1_RING = 4
        x1_ring = carve([X1_RING, D])
        x2_parts = carve([2, D], F16)
        fence = carve([3])
        minus_half = carve([H])

        LAG = {"s_pre": 0, "s_core": 1, "s_tail": 2, "c_pre": 2, "c_core": 3, "c_tail": 4}
        STEPS = B + max(LAG.values())
        FIRST_FULL = max(LAG.values()) + 1
        UNITS = range(H // Q4)

        def units(*of):
            return [e for u in UNITS for e in ((f"{k}{u}", part) for k, part in of)]

        C, T = "c_core", "c_tail"
        ORDER = {
            "turn": [("c_oT", T), ("c_v", C), ("s_v", "s_core"), ("s_oT", "s_tail"), ("c_wo", T), ("s_wo", "s_tail"),
                     ("x2T", T), ("x1T", "s_tail"), ("s_xT", "s_pre"), ("c_cT", "c_pre")],
            "turn_hi": [("c_oT", T), ("c_v", C), ("s_v", "s_core"), ("s_oT", "s_tail"),
                        ("x2T", T), ("x1T", "s_tail"), ("s_xT", "s_pre"), ("c_cT", "c_pre")],
            "proj": [("s_qk", "s_core"), ("c_q", C), ("c_k", C)],
            "score": units(("ca", C), ("cb", C), ("s", "s_core")),
            "exp_s": units(("s", "s_core")),
            "exp_c": units(("ca", C), ("cb", C)),
            "blend": units(("c", C)),
            "prob": units(("c", C), ("s", "s_core")),
            "s_value": units(("s", "s_core")), "c_value": units(("c", C)),
        }

        class Step:

            def __init__(self, t):
                self.t = t

            def on(self, part):
                return not isinstance(self.t, int) or 0 <= self.t - LAG[part] < B

            def b(self, part):
                return self.t - LAG[part]

            def slot(self, order, use):
                live = [u for u, part in ORDER[order] if self.on(part)]
                return live.index(use)

            def count(self, order, use):
                parts = [part for _, part in ORDER[order]]
                if isinstance(self.t, int):
                    before = sum(min(max(self.t - LAG[p], 0), B) for p in parts)
                else:
                    before = self.t * len(parts) - sum(LAG[p] for p in parts)
                return before + self.slot(order, use) + 1

            def last(self):
                return Step(self.t - 1)

        def steps(e, body):
            for t in range(min(FIRST_FULL, STEPS)):
                body(Step(t))
            if FIRST_FULL < B:
                with e.Fori(FIRST_FULL, B) as t:
                    body(Step(t))
            for t in range(max(B, FIRST_FULL), STEPS):
                body(Step(t))

        sig = {name: sem(name) for name in '''
            constants_in weights_in s_in s_res c_in c_mask0 c_mask1 c_mask2 c_mask3 x2_stored x2_parts_stored
            lam_prod lam_sum lam_exp lam_dif neg_lam w_rows2 weights_scaled weights_hi weights_lo zeros
            turn_written turn_hi turn_read proj_written proj_hi proj_read score_written score_read
            prob_written prob_hi prob_read s_value_written c_value_written c_value_read
            s_kbd c_kbd s_max c_max c_negmax s_shifted s_exp c_exp c_r2 c_ratio c_blend blended
            s_rsum s_o c_rsum c_sq c_ss c_ms c_rms c_o s_summed s_squares s_veps s_rstd x1 x1_kept
            c_summed c_squares c_veps c_rstd x2 x2_hi x2_parts
            f_cleared f_zero f_ones f_bias_in f_phi_in f_phi_hi f_phi_lo f_w_in f_w_hi f_w_lo f_x0 f_x1 f_x2 f_x3
            f_logits f_logits_read f_max4 f_max4_reset f_chunkmax f_max f_newmax f_rowmax f_diff f_keep
            f_shifted f_sum_exp f_sum4 f_sum4_reset f_sum f_rsum f_d_shifted f_d_exp f_dispatch f_dispatch_hi f_dispatch_lo
            f_slots0 f_slots1 f_slots2 f_slots3 f_slots_hi f_slots_lo f_c_shifted f_combine f_cT_psum f_cT_hi f_cT_lo
            f_yT_psum f_yT f_y_psum f_y_hi f_y_lo f_out f_acc
            f_res0 f_res1 f_res2 f_res3 f_n_rsum f_added f_negmean f_squares f_veps f_rstd f_normed out_stored'''.split()}

        def later(n):
            return not isinstance(n, int) or n > 0

        def in3(ap, a):
            return ap.rearrange("p (a n) -> p a n", a=a)

        def spread(ap, n):
            return ap.unsqueeze(2).broadcast_to([P, ap.shape[1], n])

        def batch(dram, b):
            return dram[bass.ds(b, 1), :, :].rearrange("o s d -> (o s) d")

        PIECE = D
        NPIECE = W_END // PIECE
        DMA = 16


        used[0] = 0
        YW = D + 2
        acc = carve([B, D + 1])
        logits = carve([B, S])
        f_w_stage = carve([DT, D])
        f_w = carve([2, DT, EC, D], F16)
        f_phi_stage = carve([DT, P])
        f_phi = carve([2, DT, P], F16)
        f_bias = carve([DT, NCH * EC])
        f_x = carve([Q4, 2, D], F16)
        f_dp = carve([2, Q4, P], F16)
        f_pair = carve([2, Q4, P])
        f_cT = carve([2, 2, Q4, S], F16)
        f_slT = carve([2, DT, Q4, P], F16)
        f_yT = carve([DT, Q4, P])
        f_y = carve([2, Q4, YW], F16)
        f_max4, f_sum4 = carve([Q4, P]), carve([Q4, P])
        f_max, f_sum, f_rsum = carve([P]), carve([P]), carve([P])
        f_chunkmax, f_rowmax, f_newmax, f_diff, f_keep = (carve([B]) for _ in range(5))
        n_half = carve([16])
        F_LAST = NQ + 3

        class Quad:

            def __init__(self, c, k):
                self.c, self.k = c, k

            def on(self, lag):
                return not isinstance(self.k, int) or 0 <= self.k - lag < NQ

            def done(self, lag, each=1):
                return self.c * (NQ * each) + (self.k - lag + 1) * each

        def quads(e, c, body):
            for k in range(min(3, F_LAST)):
                body(Quad(c, k))
            if NQ > 3:
                with e.Fori(3, NQ) as k:
                    body(Quad(c, k))
            for k in range(max(NQ, 3), F_LAST):
                body(Quad(c, k))

        def chunks(e, body):
            if NCH > 1:
                with e.Fori(0, NCH - 1) as c:
                    body(c, True)
            body(NCH - 1, False)

        def one(ap):
            return ap.rearrange("p o n -> p (o n)")

        def one4(ap):
            return ap.rearrange("p o a b -> p (o a) b")

        DISPATCH, COMBINE = 0, 1
        used[0] = B * (D + 1)
        res_ring = carve([4, Q4, D])
        norm_junk = carve([2, D])
        n_rsum, n_total, n_negmean, n_squares, n_veps, n_rstd = (carve([B]) for _ in range(6))
        NORM_GROUP = 16

        block = es.enter_context(nc.Block())

        @block.sync
        def _(sp):
            for dst, src in ((ident[:, :], ident_in), (band, band_in), (blocks, block_in), (w_rows, w_scale),
                             (lam_in.rearrange("p a b c -> p (a b c)"), lambdas)):
                sp.dma_start(dst, src).then_inc(sig["constants_in"], DMA)
            for i in range(NPIECE):
                if i:
                    sp.wait_ge(sig["weights_lo"], i)
                sp.dma_start(in3(w_stage[:, 0:DT * PIECE], DT), w_all[:, :, i * PIECE:(i + 1) * PIECE]).then_inc(sig["weights_in"], DMA)

            def body(st):
                if st.on("s_pre"):
                    b = st.b("s_pre")
                    if later(b):
                        sp.wait_ge(sig["turn_written"], st.last().count("turn", "s_xT"))
                    sp.dma_start(s_in, batch(x, b)).then_inc(sig["s_in"], DMA)
                if st.on("c_pre"):
                    b = st.b("c_pre")
                    if later(b):
                        sp.wait_ge(sig["turn_written"], st.last().count("turn", "c_cT"))
                    sp.dma_start(c_in, batch(ctx_in, b)).then_inc(sig["c_in"], DMA)
                if st.on("s_tail"):
                    b = st.b("s_tail")
                    if later(b):
                        sp.wait_ge(sig["s_summed"], b)
                    sp.dma_start(s_res, batch(x, b)).then_inc(sig["s_res"], DMA)
                if st.on("c_core"):
                    b = st.b("c_core")
                    for u in UNITS:
                        if later(b):
                            sp.wait_ge(sig["score_read"], st.last().count("score", f"cb{u}"))
                        sp.dma_start(c_mask[:, u * Q4:(u + 1) * Q4, :],
                                         mask[bass.ds(b, 1), u * Q4:(u + 1) * Q4, :, :].rearrange("o h q k -> q (o h) k")).then_inc(sig[f"c_mask{u}"], DMA)
                if st.on("c_tail"):
                    b = st.b("c_tail")
                    sp.wait_ge(sig["x2"], b + 1)
                    sp.dma_start(batch(scratch_x2, b), x2).then_inc(sig["x2_stored"], DMA)
                    sp.wait_ge(sig["x2_parts"], b + 1)
                    sp.dma_start(batch(scratch_x2_parts, b), x2_parts.rearrange("p a d -> p (a d)")).then_inc(sig["x2_parts_stored"], DMA)

            steps(sp, body)
            sp.wait_ge(sig["x2_stored"], DMA * B)
            sp.wait_ge(sig["x2_parts_stored"], DMA * B)

            sp.wait_ge(sig["f_cleared"], 3)
            sp.dma_start(f_bias, b_ffn).then_inc(sig["f_bias_in"], DMA)
            sp.dma_start(f_phi_stage, phi[:, :, 0:P]).then_inc(sig["f_phi_in"], DMA)

            def load_expert(n):
                sp.dma_start(f_w_stage, w_ffn[bass.ds(n, 1), :, :, :].rearrange("o p k e -> p (o k) e")).then_inc(sig["f_w_in"], DMA)

            def load_x(b, j):
                sp.dma_start(f_x[:, j].rearrange("p a d -> p (a d)"), batch(scratch_x2_parts, b)).then_inc(sig[f"f_x{j}"], DMA)

            load_expert(0)
            for j in range(Q4):
                load_x(j, j)

            def sp_chunk(c, more):
                if more:
                    sp.wait_ge(sig["f_phi_lo"], c + 1)
                    sp.dma_start(f_phi_stage, phi[:, :, bass.ds((c + 1) * P, P)]).then_inc(sig["f_phi_in"], DMA)
                for j in range(EC if more else EC - 1):
                    sp.wait_ge(sig["f_w_lo"], c * EC + j + 1)
                    load_expert(c * EC + j + 1)
                with sp.Fori(0, NQ if more else NQ - 1) as g:
                    for j in range(Q4):
                        sp.wait_ge(sig[f"f_slots{j}"], c * NQ + g + 1)
                        load_x((g + 1) % NQ * Q4 + j, j)

            chunks(sp, sp_chunk)
            sp.wait_ge(sig["f_acc"], NCH * B + 1)
            for g in range(NQ):
                if g >= 4:
                    sp.wait_ge(sig["f_added"], Q4 * (g - 3))
                sp.dma_start(res_ring[:, g % 4], scratch_x2[g * Q4:(g + 1) * Q4].rearrange("b s d -> s b d")).then_inc(sig[f"f_res{g % 4}"], DMA)
            for g in range(B // NORM_GROUP):
                sp.wait_ge(sig["f_normed"], NORM_GROUP * (g + 1))
                sp.dma_start(out[g * NORM_GROUP:(g + 1) * NORM_GROUP].rearrange("b s d -> s b d"),
                                 acc[:, g * NORM_GROUP:(g + 1) * NORM_GROUP, 0:D]).then_inc(sig["out_stored"], DMA)
            sp.wait_ge(sig["out_stored"], DMA * (B // NORM_GROUP))

        @block.tensor
        def _(pe):
            pe.wait_ge(sig["weights_lo"], NPIECE)
            pe.wait_ge(sig["zeros"], 4)

            def body(st):
                def take(order, use, names):
                    others = st.count(order, use) - len(names)
                    if later(others):
                        pe.wait_ge(sig[f"{order}_read"], others)
                    return bank[names[st.slot(order, use) % len(names)]]

                def turn(use, src):
                    dst = take("turn", use, ["turn"])
                    for k in range(DT):
                        last = nc.tensor.transpose(dst[:, k * P:(k + 1) * P], src[:, k * P:(k + 1) * P], ident[:, :])
                    last.then_inc(sig["turn_written"], 1)

                def project_T(use, col, src):
                    dst = take("proj", use, ["proj"])
                    for o in range(4):
                        for k in range(DT):
                            for n, (a, c) in enumerate(PASSES):
                                last = nc.tensor.matmul(dst[:, o * S:(o + 1) * S], w_parts[:, a, k, col + o * P:col + (o + 1) * P],
                                                        src[:, c, k, :], start=k + n == 0, stop=k == DT - 1 and n == 2)
                    last.then_inc(sig["proj_written"], 1)

                def project(use, col, src):
                    dst = take("turn", use, ["turn"])
                    for k in range(DT):
                        for n, (a, c) in enumerate(PASSES):
                            last = nc.tensor.matmul(dst[:, 0:D], src[:, a, k, :], w_parts[:, c, k, col:col + D],
                                                    start=k + n == 0, stop=k == DT - 1 and n == 2)
                    last.then_inc(sig["turn_written"], 1)

                def scores(use, g, q, kbd):
                    dst = take("score", use, ["score0", "score1"])
                    tile, r = g // 2, 4 * (g % 2)
                    for n, (a, c) in enumerate(PASSES):
                        last = nc.tensor.matmul(dst[:, :], q[:, a, tile, :], kbd[:, c, tile, r:r + 4, :].rearrange("p r k -> p (r k)"),
                                                start=n == 0, stop=n == 2)
                    last.then_inc(sig["score_written"], 1)

                def turn_probs(use, u, src, stride):
                    dst = take("prob", use, ["prob0", "prob1"])
                    for j in range(Q4):
                        last = nc.tensor.transpose(dst[:, j * S:(j + 1) * S], src[:, (u * Q4 + j) * stride, :], ident[:, :])
                    last.then_inc(sig["prob_written"], 1)

                def values(use, u, name, pT, v, w):
                    for j in range(Q4):
                        h = u * Q4 + j
                        for n, (a, c) in enumerate(PASSES):
                            last = nc.tensor.matmul(bank[name][:, h * w:(h + 1) * w], pT[:, u % 2, a, j, :], v[:, c, h, :],
                                                    start=n == 0, stop=n == 2)
                    last.then_inc(sig[f"{name}_written"], 1)

                s, c, st_, ct = (st.on(p) for p in ("s_core", "c_core", "s_tail", "c_tail"))
                sb_, cb, stb, ctb = (st.b(p) for p in ("s_core", "c_core", "s_tail", "c_tail"))

                def score_unit(u):
                    if c:
                        if u == 0:
                            pe.wait_ge(sig["c_kbd"], cb + 1)
                        scores(f"ca{u}", 2 * u, c_q, c_kbd)
                        scores(f"cb{u}", 2 * u + 1, c_q, c_kbd)
                    if s:
                        if u == 0:
                            pe.wait_ge(sig["s_kbd"], sb_ + 1)
                        scores(f"s{u}", u, s_qk, s_kbd)

                def turn_unit(u):
                    if c:
                        pe.wait_ge(sig["blended"], st.count("blend", f"c{u}"))
                        turn_probs(f"c{u}", u, c_prob, 2)
                    if s:
                        pe.wait_ge(sig["s_exp"], st.count("exp_s", f"s{u}"))
                        turn_probs(f"s{u}", u, s_prob, 1)

                def value_unit(u):
                    if c:
                        if u == 0:
                            if later(cb):
                                pe.wait_ge(sig["c_value_read"], cb)
                        pe.wait_ge(sig["prob_read"], st.count("prob", f"c{u}"))
                        values(f"c{u}", u, "c_value", c_pT, c_v, DH)
                    if s:
                        if u == 0:
                            if later(sb_):
                                pe.wait_ge(sig["s_o"], sb_)
                        pe.wait_ge(sig["prob_read"], st.count("prob", f"s{u}"))
                        values(f"s{u}", u, "s_value", s_pT, s_v, VW)

                if s:
                    pe.wait_ge(sig["turn_read"], st.last().count("turn", "s_xT"))
                    project_T("s_qk", SQ, s_xT)
                if ct:
                    pe.wait_ge(sig["c_o"], ctb + 1)
                    turn("c_oT", c_o)
                if c:
                    pe.wait_ge(sig["turn_read"], st.last().count("turn", "x1T"))
                    project_T("c_q", CQ, c_xT)
                    pe.wait_ge(sig["turn_read"], st.last().count("turn", "c_cT"))
                    project("c_v", CV, c_cT)
                    project_T("c_k", CK, c_cT)
                if s:
                    project("s_v", SV, s_xT)
                if st_:
                    pe.wait_ge(sig["s_o"], stb + 1)
                    turn("s_oT", s_o)
                score_unit(0)
                if ct:
                    pe.wait_ge(sig["turn_read"], st.count("turn", "c_oT"))
                    project("c_wo", CO, c_oT)
                score_unit(1)
                turn_unit(0)
                if st_:
                    pe.wait_ge(sig["turn_read"], st.count("turn", "s_oT"))
                    project("s_wo", SO, s_oT)
                score_unit(2)
                turn_unit(1)
                value_unit(0)
                if ct:
                    pe.wait_ge(sig["x2"], ctb + 1)
                    turn("x2T", x2)
                score_unit(3)
                turn_unit(2)
                value_unit(1)
                if st_:
                    pe.wait_ge(sig["x1"], stb + 1)
                    turn("x1T", x1)
                turn_unit(3)
                value_unit(2)
                if st.on("s_pre"):
                    pe.wait_ge(sig["s_in"], DMA * (st.b("s_pre") + 1))
                    turn("s_xT", s_in)
                if st.on("c_pre"):
                    pe.wait_ge(sig["c_in"], DMA * (st.b("c_pre") + 1))
                    turn("c_cT", c_in)
                value_unit(3)

            steps(pe, body)

            FB = [bank[n] for n in ("turn", "proj", "score0", "score1", "prob0", "prob1", "s_value", "c_value")]
            b_turn, b_slots, b_yT, b_y, b_out = FB[0], FB[1:3], FB[3:5], FB[5:7], FB[7]
            mm = nc.tensor.matmul
            pe.wait_ge(sig["f_cleared"], 3)

            def pe_logits(g, js):
                for j in js:
                    for k in range(DT):
                        for n, (a, c_) in enumerate(PASSES):
                            last = mm(b_turn[:, j * P:(j + 1) * P], xT[:, a, k, bass.ds((g * Q4 + j) * S, S)], f_phi[:, c_, k, :],
                                      start=k + n == 0, stop=k == DT - 1 and n == 2)
                return last

            pe.wait_ge(sig["f_phi_lo"], 1)
            pe_logits(0, range(Q4)).then_inc(sig["f_logits"], 1)
            with pe.Fori(1, NQ) as g:
                pe.wait_ge(sig["f_logits_read"], g)
                pe_logits(g, range(Q4)).then_inc(sig["f_logits"], 1)

            def pe_chunk(c, more):
                pe.wait_ge(sig["f_w_lo"], c * EC + EC)
                if more:
                    pe.wait_ge(sig["f_phi_lo"], c + 2)

                def body(st):
                    k = st.k

                    def out_product(j):
                        if not st.on(3):
                            return
                        if j == 0:
                            pe.wait_ge(sig["f_y_lo"], st.done(3, 2))
                            pe.wait_ge(sig["f_cT_lo"], st.done(3))
                        pe.wait_ge(sig["f_acc"], (c * NQ + k - 3) * Q4 + j + 1)
                        slot = bass.ds((k - 3) % 2, 1)
                        for n, (a, c_) in enumerate(PASSES):
                            last = mm(b_out[:, 0:D + 1], one(f_cT[:, slot, a, j, :]), f_y[:, c_, j, 0:D + 1], start=n == 0, stop=n == 2)
                        last.then_inc(sig["f_out"], 1)

                    out_product(0)
                    if st.on(2):
                        pe.wait_ge(sig["f_combine"], st.done(2))
                        before = k - 3 if not isinstance(k, int) else max(k - 3, 0)
                        pe.wait_ge(sig["f_logits_read"], (c + 1) * NQ + (before if more else 0))
                        for j in range(Q4):
                            last = nc.tensor.transpose(b_turn[:, j * S:(j + 1) * S], f_pair[:, COMBINE, j, :], ident[:, :])
                        last.then_inc(sig["f_cT_psum"], 1)
                    out_product(1)
                    if st.on(3) and more:
                        done = min(k - 2 + 1, NQ) if isinstance(k, int) else k - 2 + 1
                        pe.wait_ge(sig["f_cT_lo"], c * NQ + done)
                        pe_logits(k - 3, (0, 1))
                    out_product(2)
                    if st.on(3) and more:
                        pe_logits(k - 3, (2, 3)).then_inc(sig["f_logits"], 1)
                    out_product(3)
                    if st.on(2):
                        pe.wait_ge(sig["f_yT"], st.done(2, 2))
                        for half in range(2):
                            for j in (2 * half, 2 * half + 1):
                                for e in range(DT):
                                    col = (j % 2) * D + e * P
                                    last = nc.tensor.transpose(b_y[half][:, col:col + P], f_yT[:, e, j, :], ident[:, :])
                            last.then_inc(sig["f_y_psum"], 1)
                    if st.on(1):
                        pe.wait_ge(sig["f_slots_lo"], st.done(1, 2))
                        for e in range(DT):
                            for x_ in range(EC):
                                for kk in range(DT):
                                    for n, (a, c_) in enumerate(PASSES):
                                        last = mm(b_yT[e][:, :].rearrange("p (b s) -> p b s", b=Q4)[:, :, x_ * SP_E:(x_ + 1) * SP_E],
                                                  f_w[:, a, kk, x_, e * P:(e + 1) * P], f_slT[:, c_, kk, :, x_ * SP_E:(x_ + 1) * SP_E],
                                                  start=kk + n == 0, stop=kk == DT - 1 and n == 2)
                            last.then_inc(sig["f_yT_psum"], 1)
                    if st.on(0):
                        pe.wait_ge(sig["f_dispatch_lo"], st.done(0))
                        for e in range(DT):
                            for j in range(Q4):
                                if e == 0:
                                    pe.wait_ge(sig[f"f_x{j}"], DMA * st.done(0))
                                for n, (a, c_) in enumerate(PASSES):
                                    last = mm(b_slots[e][:, j * P:(j + 1) * P], f_x[:, j, a, e * P:(e + 1) * P], f_dp[:, c_, j, :],
                                              start=n == 0, stop=n == 2)
                                if e == DT - 1:
                                    last.then_inc(sig[f"f_slots{j}"], 1)
                quads(pe, c, body)

            chunks(pe, pe_chunk)

        @block.scalar
        def _(act):
            act.wait_ge(sig["constants_in"], DMA * 5)
            act.wait_ge(sig["lam_sum"], 1)
            nc.scalar.activation(lam_exp.rearrange("p a b -> p (a b)"), lam_sum.rearrange("p a b -> p (a b)"), ACT.Exp).then_inc(sig["lam_exp"], 1)
            for i in range(NPIECE):
                act.wait_ge(sig["weights_scaled"], i + 1)
                nc.scalar.activation(w_parts[:, HI, :, i * PIECE:(i + 1) * PIECE], in3(w_stage[:, 0:DT * PIECE], DT), ACT.Copy).then_inc(sig["weights_hi"], 1)

            def body(st):
                def hi(order, use, name, dst, src):
                    act.wait_ge(sig[f"{order}_written"], st.count(order, use))
                    nc.scalar.activation(dst, src, ACT.Copy).then_inc(sig[name], 1)

                def hi_turn(use, dst):
                    hi("turn", use, "turn_hi", dst, in3(bank["turn"][:, 0:D], dst.shape[1]))

                def hi_proj(use, dst):
                    hi("proj", use, "proj_hi", dst, in3(bank["proj"][:, :], 4))

                def squares(part, b, junk, summed, negmean, total):
                    act.wait_ge(sig[f"{part}_summed"], b + 1)
                    nc.scalar.activation(junk, summed, ACT.Square, bias=negmean, accum_out=total).then_inc(sig[f"{part}_squares"], 1)

                def exps(u):
                    if st.on("c_core"):
                        for g, use in ((2 * u, f"ca{u}"), (2 * u + 1, f"cb{u}")):
                            act.wait_ge(sig["c_negmax"], st.count("exp_c", use))
                            for r in range(4 * g, 4 * g + 4):
                                last = nc.scalar.activation(c_prob[:, r, :], c_prob[:, r, :], ACT.Exp,
                                                            bias=c_negmax[:, r:r + 1], accum_out=c_sum[:, r:r + 1])
                            last.then_inc(sig["c_exp"], 1)
                    if st.on("s_core"):
                        act.wait_ge(sig["s_shifted"], st.count("exp_s", f"s{u}"))
                        part = s_prob[:, u * Q4:(u + 1) * Q4, :].rearrange("p a b -> p (a b)")
                        nc.scalar.activation(part, part, ACT.Exp).then_inc(sig["s_exp"], 1)

                def prob_hi(u):
                    for use, part, pT in ((f"c{u}", "c_core", c_pT), (f"s{u}", "s_core", s_pT)):
                        if st.on(part):
                            name = ["prob0", "prob1"][st.slot("prob", use) % 2]
                            hi("prob", use, "prob_hi", pT[:, u % 2, HI, :, :], in3(bank[name][:, :], Q4))

                if st.on("s_core"):
                    hi_proj("s_qk", s_qk[:, HI])
                if st.on("c_tail"):
                    hi_turn("c_oT", c_oT[:, HI])
                if st.on("c_core"):
                    hi_proj("c_q", c_q[:, HI])
                    hi_turn("c_v", c_v[:, HI])
                    hi_proj("c_k", c_k[:, HI])
                if st.on("s_core"):
                    hi_turn("s_v", s_v[:, HI, :, 0:DH])
                if st.on("s_tail"):
                    hi_turn("s_oT", s_oT[:, HI])
                exps(0)
                if st.on("c_tail"):
                    squares("c", st.b("c_tail"), c_junk, c_sumx, c_negmean, c_sqx)
                exps(1)
                prob_hi(0)
                if st.on("s_tail"):
                    squares("s", st.b("s_tail"), s_junk, s_sum, s_negmean, s_sq)
                exps(2)
                if st.on("c_tail"):
                    b = st.b("c_tail")
                    act.wait_ge(sig["x2"], b + 1)
                    if later(b):
                        act.wait_ge(sig["x2_parts_stored"], DMA * b)
                    nc.scalar.activation(x2_parts[:, HI, :], x2, ACT.Copy).then_inc(sig["x2_hi"], 1)
                    hi_turn("x2T", xT[:, HI, :, bass.ds(st.b("c_tail") * S, S)])
                prob_hi(1)
                exps(3)
                if st.on("s_tail"):
                    b = st.b("s_tail")
                    act.wait_ge(sig["x1"], b + 1)
                    nc.scalar.activation(x1_ring[:, bass.ds(b % X1_RING, 1), :].rearrange("p o d -> p (o d)"), x1, ACT.Copy).then_inc(sig["x1_kept"], 1)
                    hi_turn("x1T", c_xT[:, HI])
                prob_hi(2)
                if st.on("s_pre"):
                    hi_turn("s_xT", s_xT[:, HI])
                if st.on("c_pre"):
                    hi_turn("c_cT", c_cT[:, HI])
                prob_hi(3)

            steps(act, body)

            EXP, COPY = ACT.Exp, ACT.Copy
            nc.scalar.activation(fence[:, 0:1], neg_lam[:, 0:1], COPY).then_inc(sig["f_cleared"], 1)

            def flat(ap):
                return ap.rearrange("p a b -> p (a b)")

            def act_phi(n):
                act.wait_ge(sig["f_phi_in"], DMA * n)
                nc.scalar.activation(f_phi[:, HI], f_phi_stage, COPY).then_inc(sig["f_phi_hi"], 1)

            def act_logits(g, n):
                act.wait_ge(sig["f_logits"], n)
                nc.scalar.activation(logits[:, bass.ds(g * Q4, Q4), :], in3(FBV[0][:, :], Q4), COPY).then_inc(sig["f_logits_read"], 1)

            FBV = [bank[n] for n in ("turn", "proj", "score0", "score1", "prob0", "prob1", "s_value", "c_value")]
            act.wait_ge(sig["f_cleared"], 3)
            act_phi(1)
            with act.Fori(0, NQ) as g:
                act_logits(g, g + 1)

            def act_chunk(c, more):
                act.wait_ge(sig["f_diff"], c + 1)
                nc.scalar.activation(f_keep, f_diff, EXP).then_inc(sig["f_keep"], 1)
                with act.Fori(0, NQ) as g:
                    act.wait_ge(sig["f_shifted"], c * NQ + g + 1)
                    part = f_pair[:, bass.ds(g % 2, 1), :, :].rearrange("p o a b -> p (o a b)")
                    nc.scalar.activation(part, part, EXP).then_inc(sig["f_sum_exp"], 1)
                for j in range(EC):
                    act.wait_ge(sig["f_w_in"], DMA * (c * EC + j + 1))
                    nc.scalar.activation(f_w[:, HI, :, j, :], f_w_stage, COPY).then_inc(sig["f_w_hi"], 1)
                if more:
                    act_phi(c + 2)

                def body(st):
                    k = st.k
                    if st.on(0):
                        act.wait_ge(sig["f_d_shifted"], st.done(0))
                        nc.scalar.activation(flat(f_pair[:, DISPATCH]), flat(f_pair[:, DISPATCH]), EXP).then_inc(sig["f_d_exp"], 1)
                    if st.on(2):
                        act.wait_ge(sig["f_cT_psum"], st.done(2))
                        nc.scalar.activation(f_cT[:, bass.ds((k - 2) % 2, 1), HI, :, :].rearrange("p o a b -> p (o a b)"), FBV[0][:, :], COPY).then_inc(sig["f_cT_hi"], 1)
                    if st.on(3) and more:
                        act_logits(k - 3, (c + 1) * NQ + k - 2)
                    if st.on(0):
                        act.wait_ge(sig["f_dispatch"], st.done(0))
                        if later(k):
                            act.wait_ge(sig["f_slots3"], st.done(1))
                        nc.scalar.activation(f_dp[:, HI], f_pair[:, DISPATCH], COPY).then_inc(sig["f_dispatch_hi"], 1)
                    if st.on(1):
                        act.wait_ge(sig["f_c_shifted"], st.done(1))
                        nc.scalar.activation(flat(f_pair[:, COMBINE]), flat(f_pair[:, COMBINE]), EXP).then_inc(sig["f_combine"], 1)
                    if st.on(2):
                        for half in range(2):
                            act.wait_ge(sig["f_y_psum"], st.done(2, 2) - 1 + half)
                            nc.scalar.activation(f_y[:, HI, 2 * half:2 * half + 2, 0:D], in3(FBV[5 + half][:, :], 2), COPY).then_inc(sig["f_y_hi"], 1)
                    if st.on(0):
                        act.wait_ge(sig["f_slots3"], st.done(0))
                        for e in range(DT):
                            nc.scalar.activation(f_slT[:, HI, e], in3(FBV[1 + e][:, :], Q4), COPY).then_inc(sig["f_slots_hi"], 1)
                quads(act, c, body)

            chunks(act, act_chunk)
            for g in range(B // NORM_GROUP):
                act.wait_ge(sig["f_negmean"], g + 1)
                for b in range(g * NORM_GROUP, (g + 1) * NORM_GROUP):
                    if b:
                        act.wait_ge(sig["f_squares"], b)
                    nc.scalar.activation(norm_junk[:, b % 2], acc[:, b, 0:D], ACT.Square, bias=n_negmean[:, b:b + 1],
                                             accum_out=n_squares[:, b:b + 1]).then_inc(sig["f_squares"], 1)

        @block.vector
        def _(dve):
            dve.wait_ge(sig["constants_in"], DMA * 5)
            pairs = lam_in.rearrange("p (i two) b c -> p i two b c", two=2)
            nc.vector.tensor_tensor(lam_prod, pairs[:, :, 0], pairs[:, :, 1], ALU.mult).then_inc(sig["lam_prod"], 1)
            dve.wait_ge(sig["lam_prod"], 1)
            nc.vector.reduce_sum(lam_sum, lam_prod, AX.X).then_inc(sig["lam_sum"], 1)
            dve.wait_ge(sig["lam_exp"], 1)
            nc.vector.tensor_tensor(lam_dif, lam_exp[:, 1, :], lam_exp[:, 0, :], ALU.subtract).then_inc(sig["lam_dif"], 1)
            dve.wait_ge(sig["lam_dif"], 1)
            nc.vector.tensor_scalar(neg_lam, lam_dif, -LAMBDA_INIT, None, ALU.add).then_inc(sig["neg_lam"], 1)
            nc.vector.tensor_scalar(w_rows2, w_rows, OUT_SCALE, None, ALU.mult).then_inc(sig["w_rows2"], 1)
            dve.wait_ge(sig["neg_lam"], 1)
            dve.wait_ge(sig["w_rows2"], 1)
            for i in range(NPIECE):
                dve.wait_ge(sig["weights_in"], DMA * (i + 1))
                col, stage = i * PIECE, in3(w_stage[:, 0:DT * PIECE], DT)
                scale = SCORE_SCALE if SQ <= col < SK or CQ <= col < CK else 1.0
                for k in range(DT):
                    if CO <= col:
                        last = nc.vector.tensor_scalar(stage[:, k], stage[:, k], w_rows2[:, k:k + 1], None, ALU.mult)
                    else:
                        last = nc.vector.tensor_scalar(stage[:, k], stage[:, k], scale, None, ALU.mult)
                last.then_inc(sig["weights_scaled"], 1)
                dve.wait_ge(sig["weights_hi"], i + 1)
                nc.vector.tensor_tensor(w_parts[:, LO, :, col:col + PIECE], stage, w_parts[:, HI, :, col:col + PIECE], ALU.subtract).then_inc(sig["weights_lo"], 1)

            def body(st):
                def lo(order, use, dst, src, hi):
                    dve.wait_ge(sig[f"{order}_hi"], st.count("turn_hi" if order == "turn" else order, use))
                    nc.vector.tensor_tensor(dst, src, hi, ALU.subtract).then_inc(sig[f"{order}_read"], 1)

                def lo_turn(use, parts):
                    lo("turn", use, parts[:, LO], in3(bank["turn"][:, 0:D], parts.shape[2]), parts[:, HI])

                def lo_proj(use, parts):
                    lo("proj", use, parts[:, LO], in3(bank["proj"][:, :], 4), parts[:, HI])

                def block_diagonal(name, kbd, k_parts):
                    for r in range(8):
                        for part in (HI, LO):
                            last = nc.vector.tensor_scalar(kbd[:, part, :, r, :], k_parts[:, part], blocks[:, r:r + 1], None, ALU.mult)
                    last.then_inc(sig[name], 1)

                def masked(use, part, g, prob, bias, maxima):
                    dve.wait_ge(sig["score_written"], st.count("score", use))
                    name = ["score0", "score1"][st.slot("score", use) % 2]
                    block_, cols = prob[:, 4 * g:4 * g + 4, :], maxima[:, 4 * g:4 * g + 4]
                    src = in3(bank[name][:, :], 4)
                    if part == "c":
                        src, dst = src.rearrange("p (h i) k -> p h i k", i=2), block_.rearrange("p (h i) k -> p h i k", i=2)
                    else:
                        dst = block_
                    nc.vector.tensor_tensor(dst, src, bias, ALU.add).then_inc(sig["score_read"], 1)
                    dve.wait_ge(sig["score_read"], st.count("score", use))
                    nc.vector.reduce_max(cols, block_, AX.X).then_inc(sig[f"{part}_max"], 1)

                def mask_unit(u):
                    if st.on("c_core"):
                        b = st.b("c_core")
                        dve.wait_ge(sig[f"c_mask{u}"], DMA * (b + 1))
                        for i, use in enumerate((f"ca{u}", f"cb{u}")):
                            g = 2 * u + i
                            heads = c_mask[:, 2 * g:2 * g + 2, :].unsqueeze(2).broadcast_to([P, 2, 2, S])
                            masked(use, "c", g, c_prob, heads, c_max)
                            dve.wait_ge(sig["c_max"], st.count("exp_c", use))
                            nc.vector.tensor_scalar(c_negmax[:, 4 * g:4 * g + 4], c_max[:, 4 * g:4 * g + 4], -1.0, None, ALU.mult).then_inc(sig["c_negmax"], 1)
                    if st.on("s_core"):
                        masked(f"s{u}", "s", u, s_prob, band.unsqueeze(1).broadcast_to([P, Q4, S]), s_max)

                def blend_unit(u):
                    if not st.on("c_core"):
                        return
                    dve.wait_ge(sig["c_exp"], st.count("exp_c", f"cb{u}"))
                    n = st.count("blend", f"c{u}")
                    heads = slice(u * Q4, (u + 1) * Q4)
                    sums = c_sum.rearrange("p (h i) -> p h i", i=2)
                    nc.vector.reciprocal(c_r2[:, heads], sums[:, heads, 1]).then_inc(sig["c_r2"], 1)
                    dve.wait_ge(sig["c_r2"], n)
                    nc.vector.tensor_tensor(c_ratio[:, heads], c_r2[:, heads], sums[:, heads, 0], ALU.mult).then_inc(sig["c_ratio"], 1)
                    dve.wait_ge(sig["c_ratio"], n)
                    nc.vector.tensor_tensor(c_blend[:, heads], c_ratio[:, heads], neg_lam[:, heads], ALU.mult).then_inc(sig["c_blend"], 1)
                    dve.wait_ge(sig["c_blend"], n)
                    for h in range(u * Q4, (u + 1) * Q4):
                        last = nc.vector.scalar_tensor_tensor(c_prob[:, 2 * h, :], c_prob[:, 2 * h + 1, :], c_blend[:, h:h + 1],
                                                              c_prob[:, 2 * h, :], ALU.mult, ALU.add)
                    last.then_inc(sig["blended"], 1)

                def prob_lo(u):
                    for use, part, pT in ((f"c{u}", "c_core", c_pT), (f"s{u}", "s_core", s_pT)):
                        if st.on(part):
                            name = ["prob0", "prob1"][st.slot("prob", use) % 2]
                            lo("prob", use, pT[:, u % 2, LO], in3(bank[name][:, :], Q4), pT[:, u % 2, HI])

                def norm_mean(part, b, use, res, summed, total, negmean):
                    dve.wait_ge(sig["turn_written"], st.count("turn", use))
                    nc.vector.scalar_tensor_tensor(summed, bank["turn"][:, 0:D], 1.0, res, ALU.mult, ALU.add, accum_out=total).then_inc(sig["turn_read"], 1)
                    dve.wait_ge(sig["turn_read"], st.count("turn", use))
                    nc.vector.tensor_scalar(negmean, total, -1.0 / D, None, ALU.mult).then_inc(sig[f"{part}_summed"], 1)

                def norm_variance(part, b, squares, veps):
                    dve.wait_ge(sig[f"{part}_squares"], b + 1)
                    nc.vector.tensor_scalar(veps, squares, 1.0 / D, LN_EPS, ALU.mult, ALU.add).then_inc(sig[f"{part}_veps"], 1)

                def norm_apply(part, b, summed, negmean, rstd, dst, name):
                    dve.wait_ge(sig[f"{part}_rstd"], b + 1)
                    nc.vector.tensor_scalar(dst, summed, negmean, rstd, ALU.add, ALU.mult).then_inc(sig[name], 1)

                s, c, s_t, ct = (st.on(p) for p in ("s_core", "c_core", "s_tail", "c_tail"))
                sb_, cb, stb, ctb = (st.b(p) for p in ("s_core", "c_core", "s_tail", "c_tail"))
                if ct:
                    dve.wait_ge(sig["c_rms"], ctb + 1)
                    nc.vector.tensor_tensor(in3(c_o, H), in3(c_oraw, H), spread(c_rms, DH), ALU.mult).then_inc(sig["c_o"], 1)
                if s:
                    lo_proj("s_qk", s_qk)
                    dve.wait_ge(sig["proj_read"], st.count("proj", "s_qk"))
                    block_diagonal("s_kbd", s_kbd, s_qk[:, :, 2:4, :])
                if ct:
                    lo_turn("c_oT", c_oT)
                if c:
                    lo_proj("c_q", c_q)
                    lo_turn("c_v", c_v)
                    lo_proj("c_k", c_k)
                    dve.wait_ge(sig["proj_read"], st.count("proj", "c_k"))
                    block_diagonal("c_kbd", c_kbd, c_k)
                if s:
                    lo_turn("s_v", s_v[:, :, :, 0:DH])
                if s_t:
                    lo_turn("s_oT", s_oT)
                mask_unit(0)
                if ct:
                    dve.wait_ge(sig["x1_kept"], ctb + 1)
                    norm_mean("c", ctb, "c_wo", x1_ring[:, bass.ds(ctb % X1_RING, 1), :].rearrange("p o d -> p (o d)"), c_sumx, c_total, c_negmean)
                mask_unit(1)
                if ct:
                    norm_variance("c", ctb, c_sqx, c_veps)
                blend_unit(0)
                if ct:
                    if later(ctb):
                        dve.wait_ge(sig["x2_stored"], DMA * ctb)
                        dve.wait_ge(sig["x2_parts"], ctb)
                    norm_apply("c", ctb, c_sumx, c_negmean, c_rstd, x2, "x2")
                if s_t:
                    dve.wait_ge(sig["s_res"], DMA * (stb + 1))
                    norm_mean("s", stb, "s_wo", s_res, s_sum, s_total, s_negmean)
                mask_unit(2)
                prob_lo(0)
                if s_t:
                    norm_variance("s", stb, s_sq, s_veps)
                blend_unit(1)
                if s_t:
                    if later(stb):
                        dve.wait_ge(sig["x1_kept"], stb)
                    norm_apply("s", stb, s_sum, s_negmean, s_rstd, x1, "x1")
                if ct:
                    lo_turn("x2T", xT[:, :, :, bass.ds(ctb * S, S)])
                mask_unit(3)
                prob_lo(1)
                blend_unit(2)
                if s_t:
                    lo_turn("x1T", c_xT)
                prob_lo(2)
                blend_unit(3)
                if st.on("s_pre"):
                    lo_turn("s_xT", s_xT)
                if st.on("c_pre"):
                    lo_turn("c_cT", c_cT)
                prob_lo(3)
                if s:
                    acc = bank["s_value"][:, 0:H * VW].rearrange("p (h w) -> p h w", w=VW)
                    dve.wait_ge(sig["s_value_written"], st.count("s_value", "s3"))
                    nc.vector.reciprocal(s_rsum, acc[:, :, DH]).then_inc(sig["s_rsum"], 1)
                    dve.wait_ge(sig["s_rsum"], sb_ + 1)
                    nc.vector.tensor_tensor(in3(s_o, H), acc[:, :, 0:DH], spread(s_rsum, DH), ALU.mult).then_inc(sig["s_o"], 1)
                if c:
                    acc = in3(bank["c_value"][:, 0:D], H)
                    nc.vector.reciprocal(c_rsum, c_sum.rearrange("p (h i) -> p h i", i=2)[:, :, 0]).then_inc(sig["c_rsum"], 1)
                    dve.wait_ge(sig["c_value_written"], st.count("c_value", "c3"))
                    dve.wait_ge(sig["c_rsum"], cb + 1)
                    nc.vector.tensor_tensor(in3(c_oraw, H), acc, spread(c_rsum, DH), ALU.mult).then_inc(sig["c_value_read"], 1)
                    dve.wait_ge(sig["c_value_read"], cb + 1)
                    nc.vector.tensor_tensor(c_sq, c_oraw, c_oraw, ALU.mult).then_inc(sig["c_sq"], 1)
                    dve.wait_ge(sig["c_sq"], cb + 1)
                    nc.vector.reduce_sum(c_ss, in3(c_sq, H), AX.X).then_inc(sig["c_ss"], 1)
                    dve.wait_ge(sig["c_ss"], cb + 1)
                    nc.vector.tensor_scalar(c_ms, c_ss, 1.0 / DH, RMS_EPS, ALU.mult, ALU.add).then_inc(sig["c_ms"], 1)

            steps(dve, body)

            FBV = [bank[n] for n in ("turn", "proj", "score0", "score1", "prob0", "prob1", "s_value", "c_value")]
            nc.vector.memset(fence[:, 1:2], 0.0).then_inc(sig["f_cleared"], 1)
            dve.wait_ge(sig["f_cleared"], 3)
            dve.wait_ge(sig["x2_parts_stored"], DMA * B)
            dve.wait_ge(sig["x2_stored"], DMA * B)
            nc.vector.memset(acc[:, 0:B // 2, :], 0.0).then_inc(sig["f_acc"], 1)
            nc.vector.memset(f_rowmax, -1e30).then_inc(sig["f_zero"], 1)
            nc.vector.memset(f_max4, -3e38).then_inc(sig["f_zero"], 1)

            def dve_phi(n):
                dve.wait_ge(sig["f_phi_hi"], n)
                nc.vector.tensor_tensor(f_phi[:, LO], f_phi_stage, f_phi[:, HI], ALU.subtract).then_inc(sig["f_phi_lo"], 1)

            def dve_maxima(g, n):
                dve.wait_ge(sig["f_logits_read"], n)
                dve.wait_ge(sig["f_max4"], n - 1)
                part = logits[:, bass.ds(g * Q4, Q4), :]
                nc.vector.tensor_tensor(f_max4, f_max4, part, ALU.max).then_inc(sig["f_max4"], 1)
                nc.vector.reduce_max(f_chunkmax[:, bass.ds(g * Q4, Q4)], part, AX.X).then_inc(sig["f_chunkmax"], 1)

            dve_phi(1)
            dve.wait_ge(sig["f_zero"], 3)
            dve.wait_ge(sig["f_logits_read"], 1)
            nc.vector.tensor_tensor(f_max4, f_max4, logits[:, 0:Q4, :], ALU.max).then_inc(sig["f_max4"], 1)
            nc.vector.reduce_max(f_chunkmax[:, 0:Q4], logits[:, 0:Q4, :], AX.X).then_inc(sig["f_chunkmax"], 1)
            with dve.Fori(1, NQ) as g:
                dve_maxima(g, g + 1)

            def dve_chunk(c, more):
                dve.wait_ge(sig["f_max4"], (c + 1) * NQ)
                nc.vector.reduce_max(f_max, f_max4.rearrange("p q n -> p n q"), AX.X).then_inc(sig["f_max"], 1)
                dve.wait_ge(sig["f_chunkmax"], (c + 1) * NQ)
                nc.vector.tensor_tensor(f_newmax, f_rowmax, f_chunkmax, ALU.max).then_inc(sig["f_newmax"], 1)
                dve.wait_ge(sig["f_newmax"], c + 1)
                nc.vector.tensor_tensor(f_diff, f_rowmax, f_newmax, ALU.subtract).then_inc(sig["f_diff"], 1)
                dve.wait_ge(sig["f_diff"], c + 1)
                nc.vector.tensor_copy(f_rowmax, f_newmax).then_inc(sig["f_rowmax"], 1)
                dve.wait_ge(sig["f_max"], c + 1)
                nc.vector.memset(f_max4, -3e38).then_inc(sig["f_max4_reset"], 1)
                nc.vector.memset(f_sum4, 0.0).then_inc(sig["f_sum4_reset"], 1)
                dve.wait_ge(sig["f_sum4_reset"], c + 1)
                dve.wait_ge(sig["f_sum_exp"], c * NQ + 1)
                nc.vector.tensor_tensor(f_sum4, f_sum4, f_pair[:, 0], ALU.add).then_inc(sig["f_sum4"], 1)
                with dve.Fori(1, NQ) as g:
                    dve.wait_ge(sig["f_sum_exp"], c * NQ + g + 1)
                    dve.wait_ge(sig["f_sum4"], c * NQ + g)
                    nc.vector.tensor_tensor(f_sum4, f_sum4, one4(f_pair[:, bass.ds(g % 2, 1), :, :]), ALU.add).then_inc(sig["f_sum4"], 1)
                dve.wait_ge(sig["f_sum4"], (c + 1) * NQ)
                nc.vector.reduce_sum(f_sum, f_sum4.rearrange("p q n -> p n q"), AX.X).then_inc(sig["f_sum"], 1)
                dve.wait_ge(sig["f_sum"], c + 1)
                nc.vector.reciprocal(f_rsum, f_sum).then_inc(sig["f_rsum"], 1)
                for j in range(EC):
                    dve.wait_ge(sig["f_w_hi"], c * EC + j + 1)
                    nc.vector.tensor_tensor(f_w[:, LO, :, j, :], f_w_stage, f_w[:, HI, :, j, :], ALU.subtract).then_inc(sig["f_w_lo"], 1)
                if more:
                    dve_phi(c + 2)
                dve.wait_ge(sig["f_keep"], c + 1)
                dve.wait_ge(sig["f_rowmax"], c + 1)
                dve.wait_ge(sig["f_max4_reset"], c + 1)

                def body(st):
                    k = st.k

                    def accumulate(j):
                        if st.on(3):
                            dve.wait_ge(sig["f_out"], (c * NQ + k - 3) * Q4 + j + 1)
                            b = bass.ds((k - 3) * Q4 + j, 1)
                            nc.vector.scalar_tensor_tensor(one(acc[:, b, :]), one(acc[:, b, :]), f_keep[:, b], FBV[7][:, 0:D + 1],
                                                               ALU.mult, ALU.add).then_inc(sig["f_acc"], 1)

                    accumulate(0)
                    if st.on(2):
                        dve.wait_ge(sig["f_cT_hi"], st.done(2))
                        slot = bass.ds((k - 2) % 2, 1)
                        nc.vector.tensor_tensor(f_cT[:, slot, LO, :, :].rearrange("p o a b -> p (o a b)"), FBV[0][:, :],
                                                    f_cT[:, slot, HI, :, :].rearrange("p o a b -> p (o a b)"), ALU.subtract).then_inc(sig["f_cT_lo"], 1)
                    accumulate(1)
                    accumulate(2)
                    accumulate(3)
                    if st.on(3) and more:
                        dve_maxima(k - 3, (c + 1) * NQ + k - 2)
                    if st.on(1):
                        if later(k - 1):
                            dve.wait_ge(sig["f_cT_psum"], st.done(2))
                        b = bass.ds((k - 1) * Q4, Q4)
                        nc.vector.tensor_tensor(f_pair[:, COMBINE], logits[:, b, :], spread(f_rowmax[:, b], P), ALU.subtract).then_inc(sig["f_c_shifted"], 1)
                    if st.on(2):
                        for half in range(2):
                            dve.wait_ge(sig["f_y_hi"], st.done(2, 2) - 1 + half)
                            part = slice(2 * half, 2 * half + 2)
                            nc.vector.tensor_tensor(f_y[:, LO, part, 0:D], in3(FBV[5 + half][:, :], 2), f_y[:, HI, part, 0:D], ALU.subtract).then_inc(sig["f_y_lo"], 1)
                    if st.on(1):
                        for e in range(DT):
                            dve.wait_ge(sig["f_yT_psum"], st.done(1, 2) - 1 + e)
                            bias = f_bias[:, e, bass.ds(c * EC, EC)].unsqueeze(1).unsqueeze(3).broadcast_to([P, Q4, EC, SP_E])
                            nc.vector.tensor_tensor(f_yT[:, e].rearrange("p b (x s) -> p b x s", x=EC),
                                                        FBV[3 + e][:, :].rearrange("p (b x s) -> p b x s", b=Q4, x=EC), bias, ALU.add).then_inc(sig["f_yT"], 1)
                    if st.on(0):
                        for e in range(DT):
                            dve.wait_ge(sig["f_slots_hi"], st.done(0, 2) - 1 + e)
                            nc.vector.tensor_tensor(f_slT[:, LO, e], in3(FBV[1 + e][:, :], Q4), f_slT[:, HI, e], ALU.subtract).then_inc(sig["f_slots_lo"], 1)
                quads(dve, c, body)

            dve.wait_ge(sig["f_bias_in"], DMA)
            chunks(dve, dve_chunk)
            dve.wait_ge(sig["f_acc"], NCH * B + 1)
            nc.vector.reciprocal(n_rsum, acc[:, :, D]).then_inc(sig["f_n_rsum"], 1)
            dve.wait_ge(sig["f_n_rsum"], 1)
            for g in range(NQ):
                dve.wait_ge(sig[f"f_res{g % 4}"], DMA * (g // 4 + 1))
                for b in range(g * Q4, (g + 1) * Q4):
                    nc.vector.scalar_tensor_tensor(acc[:, b, 0:D], acc[:, b, 0:D], n_rsum[:, b:b + 1], res_ring[:, g % 4, b % Q4],
                                                       ALU.mult, ALU.add, accum_out=n_total[:, b:b + 1]).then_inc(sig["f_added"], 1)
            dve.wait_ge(sig["f_added"], B)
            for g in range(B // NORM_GROUP):
                cols = slice(g * NORM_GROUP, (g + 1) * NORM_GROUP)
                nc.vector.tensor_scalar(n_negmean[:, cols], n_total[:, cols], -1.0 / D, None, ALU.mult).then_inc(sig["f_negmean"], 1)
            for g in range(B // NORM_GROUP):
                cols = slice(g * NORM_GROUP, (g + 1) * NORM_GROUP)
                dve.wait_ge(sig["f_squares"], NORM_GROUP * (g + 1))
                nc.vector.tensor_scalar(n_veps[:, cols], n_squares[:, cols], 1.0 / D, LN_EPS, ALU.mult, ALU.add).then_inc(sig["f_veps"], 1)
            for g in range(B // NORM_GROUP):
                dve.wait_ge(sig["f_rstd"], g + 1)
                with dve.Fori(g * NORM_GROUP, (g + 1) * NORM_GROUP) as b:
                    b1 = bass.ds(b, 1)
                    nc.vector.tensor_scalar(one(acc[:, b1, 0:D]), one(acc[:, b1, 0:D]), n_negmean[:, b1], n_rstd[:, b1], ALU.add, ALU.mult).then_inc(sig["f_normed"], 1)

        @block.gpsimd
        def _(pool):
            pool.memset(s_v[:, HI, :, DH:VW], 1.0).then_inc(sig["zeros"], 1)
            pool.memset(s_v[:, LO, :, DH:VW], 0.0).then_inc(sig["zeros"], 1)
            pool.memset(minus_half, -0.5).then_inc(sig["zeros"], 1)
            pool.memset(c_rms, 0.0).then_inc(sig["zeros"], 1)
            pool.wait_ge(sig["zeros"], 4)

            def body(st):
                def reciprocal_root(name, ready, b, dst, src):
                    pool.wait_ge(sig[ready], b + 1)
                    pool.tensor_tensor(dst, src, minus_half[:, 0:src.shape[1]], ALU.pow).then_inc(sig[name], 1)

                def shift(u):
                    if st.on("s_core"):
                        pool.wait_ge(sig["s_max"], st.count("exp_s", f"s{u}"))
                        part = s_prob[:, u * Q4:(u + 1) * Q4, :]
                        pool.tensor_tensor(part, part, spread(s_max[:, u * Q4:(u + 1) * Q4], S), ALU.subtract).then_inc(sig["s_shifted"], 1)

                shift(0)
                if st.on("c_tail"):
                    reciprocal_root("c_rstd", "c_veps", st.b("c_tail"), c_rstd, c_veps)
                shift(1)
                shift(2)
                if st.on("s_tail"):
                    reciprocal_root("s_rstd", "s_veps", st.b("s_tail"), s_rstd, s_veps)
                if st.on("c_tail"):
                    b = st.b("c_tail")
                    pool.wait_ge(sig["x2_hi"], b + 1)
                    if later(b):
                        pool.wait_ge(sig["x2_parts_stored"], DMA * b)
                    pool.tensor_tensor(x2_parts[:, LO, :], x2, x2_parts[:, HI, :], ALU.subtract).then_inc(sig["x2_parts"], 1)
                shift(3)
                if st.on("c_core"):
                    reciprocal_root("c_rms", "c_ms", st.b("c_core"), c_rms, c_ms)

            steps(pool, body)

            pool.memset(fence[:, 2:3], 0.0).then_inc(sig["f_cleared"], 1)
            pool.wait_ge(sig["f_cleared"], 3)
            pool.wait_ge(sig["x2_parts_stored"], DMA * B)
            pool.wait_ge(sig["x2_stored"], DMA * B)
            pool.memset(acc[:, B // 2:B, :], 0.0).then_inc(sig["f_zero"], 1)
            pool.memset(f_y[:, HI, :, D:YW], 1.0).then_inc(sig["f_ones"], 1)
            pool.memset(f_y[:, LO, :, D:YW], 0.0).then_inc(sig["f_ones"], 1)
            pool.memset(n_half, -0.5).then_inc(sig["f_ones"], 1)

            pool.wait_ge(sig["f_ones"], 3)

            def pool_chunk(c, more):
                f_max_b = f_max.unsqueeze(1).broadcast_to([P, Q4, P])
                f_rsum_b = f_rsum.unsqueeze(1).broadcast_to([P, Q4, P])
                pool.wait_ge(sig["f_max"], c + 1)
                for g in range(2):
                    pool.tensor_tensor(f_pair[:, g], logits[:, g * Q4:(g + 1) * Q4, :], f_max_b, ALU.subtract).then_inc(sig["f_shifted"], 1)
                with pool.Fori(2, NQ) as g:
                    pool.wait_ge(sig["f_sum4"], c * NQ + g - 1)
                    pool.tensor_tensor(one4(f_pair[:, bass.ds(g % 2, 1), :, :]), logits[:, bass.ds(g * Q4, Q4), :], f_max_b, ALU.subtract).then_inc(sig["f_shifted"], 1)
                pool.wait_ge(sig["f_rsum"], c + 1)

                def body(st):
                    k = st.k
                    if st.on(0):
                        if later(k):
                            pool.wait_ge(sig["f_dispatch_lo"], st.done(1))
                        pool.tensor_tensor(f_pair[:, DISPATCH], logits[:, bass.ds(k * Q4, Q4), :], f_max_b, ALU.subtract).then_inc(sig["f_d_shifted"], 1)
                        pool.wait_ge(sig["f_d_exp"], st.done(0))
                        pool.tensor_tensor(f_pair[:, DISPATCH], f_pair[:, DISPATCH], f_rsum_b, ALU.mult).then_inc(sig["f_dispatch"], 1)
                        pool.wait_ge(sig["f_dispatch_hi"], st.done(0))
                        pool.tensor_tensor(f_dp[:, LO], f_pair[:, DISPATCH], f_dp[:, HI], ALU.subtract).then_inc(sig["f_dispatch_lo"], 1)
                quads(pool, c, body)

            chunks(pool, pool_chunk)
            for g in range(B // NORM_GROUP):
                cols = slice(g * NORM_GROUP, (g + 1) * NORM_GROUP)
                pool.wait_ge(sig["f_veps"], g + 1)
                pool.tensor_tensor(n_rstd[:, cols], n_veps[:, cols], n_half, ALU.pow).then_inc(sig["f_rstd"], 1)


def _layout(inputs):
    a = {k: np.asarray(v) for k, v in inputs.items()}
    d = a["x"].shape[2]
    s = a["x"].shape[1]
    p = 128
    weights = np.concatenate([a["L0_attn_Wq"].T, a["L0_attn_Wk"].T, a["L0_attn_Wv"].T, a["L0_attn_Wo"].T,
                              a["L0_xattn_W_q"], a["L0_xattn_W_k"], a["L0_xattn_W_v"], a["L0_xattn_W_o"]], axis=1)
    heads = a["L0_xattn_lambda_q1"].shape[0]
    lambdas = np.stack([a[f"L0_xattn_lambda_{n}"] for n in ("q1", "k1", "q2", "k2")]).reshape(1, -1)
    idx = np.arange(s)
    seen = np.abs(idx[:, None] - idx[None, :]) <= 32
    seen[0, :] = True
    seen[:, 0] = True
    return {
        "x": a["x"], "ctx": a["ctx_1024"], "mask": a["mask_Bx16xSxS2_ff0"],
        "w_all": weights.reshape(d // p, p, -1).transpose(1, 0, 2),
        "w_scale": np.tile(a["L0_xattn_rms_scale"], heads).reshape(d // p, p).T,
        "lambdas": np.broadcast_to(lambdas, (p, lambdas.size)),
        "phi": a["L0_ffn_phi"].reshape(d // p, p, -1).transpose(1, 0, 2),
        "w_ffn": a["L0_ffn_W"].reshape(-1, d // p, p, d).transpose(0, 2, 1, 3),
        "b_ffn": a["L0_ffn_b"].T.reshape(d // p, p, -1).transpose(1, 0, 2),
        "ident": np.eye(p, dtype=np.float32),
        "band": np.where(seen, np.float32(0), np.float32(-1e30)).astype(np.float32),
        "blocks": (np.arange(p)[:, None] // 16 == np.arange(8)[None, :]).astype(np.float32),
    }


def kernel(**inputs):
    import concourse.bacc as _bacc
    from concourse.bass_utils import run_bass_kernel_spmd as _run

    nc = _bacc.Bacc("TRN2", target_bir_lowering=False, num_devices=1)
    arrays, args = {}, []
    for name, a in _layout(inputs).items():
        a = np.ascontiguousarray(a)
        arrays[f"in_{name}_dram"] = a
        args.append(nc.dram_tensor(f"in_{name}_dram", a.shape, mybir.dt.from_np(a.dtype), kind="ExternalInput").ap())
    out = nc.dram_tensor("out_dram", inputs["x"].shape, mybir.dt.float32, kind="ExternalOutput").ap()
    decoder_layer(nc, *args, out)
    return _run(nc, [arrays], core_ids=[0]).results[0]["out_dram"]
```

```python
import numpy as np
import concourse.bass as bass
from concourse import mybir
from contextlib import ExitStack

HI, LO = 0, 1
PASSES = ((HI, HI), (HI, LO), (LO, HI))


def decoder_layer(nc, x, ctx_in, mask, w_all, w_scale, lambdas, phi, w_ffn, b_ffn, ident_in, band_in, out):
    F32, F16 = mybir.dt.float32, mybir.dt.float16
    ALU, ACT, AX = mybir.AluOpType, mybir.ActivationFunctionType, mybir.AxisListType

    B, S, D = x.shape
    H = mask.shape[1]
    DH = D // H
    P = 128
    DT = D // P
    NP = phi.shape[2]
    E = w_ffn.shape[0]
    SP_E = NP // E
    EC = P // SP_E
    NCH = NP // P
    Q4 = 4
    NQ = B // Q4
    LOWEST = -3e38
    LN_EPS, RMS_EPS = 1e-5, 1e-5
    LAMBDA_INIT = 0.8
    OUT_SCALE = 1.0 - LAMBDA_INIT
    FAR = 32768.0
    SCORE_SCALE = 1.0 / float(np.sqrt(DH))
    SQ, SK, SV, SO, CQ, CK, CV, CO, W_END = (int(c) for c in np.cumsum([0, D, D, D, D, 2 * D, 2 * D, D, D]))

    scratch_x2 = nc.dram_tensor("scratch_x2", [B, S, D], F32).ap()
    scratch_x2_parts = nc.dram_tensor("scratch_x2_parts", [B, S, 2 * D], F16).ap()

    es = ExitStack()
    with es:
        def sb(name, shape, dt=F32):
            return es.enter_context(nc.sbuf_tensor(name, shape, dt))

        def sem(name):
            return es.enter_context(nc.semaphore(name))

        bank = {n: es.enter_context(nc.psum_tensor(f"bank_{n}", [P, 512], F32))
                for n in ("turn0", "turn1", "score_a", "score_b", "score_s", "prob_c", "prob_s", "value")}

        xT = sb("xT", [P, 2, DT, B * S], F16)
        ident = sb("ident", [P, P])
        ARENA = (207 * 1024 - 2 * DT * B * S * 2 - P * 4) // 4
        arena = sb("arena", [P, ARENA])
        used = [0]

        def carve(shape, dt=F32):
            n = int(np.prod(shape))
            words = n if dt == F32 else (n + 1) // 2
            part = arena[:, used[0]:used[0] + words]
            used[0] += words
            assert used[0] <= ARENA, (used[0], ARENA)
            if dt != F32:
                part = part.bitcast(dt)
            if len(shape) > 1:
                names = "abcdef"[:len(shape)]
                part = part.rearrange(f"p ({' '.join(names)}) -> p {' '.join(names)}", **dict(zip(names, shape)))
            return part

        w_parts = carve([2, DT, W_END], F16)
        c_mask = carve([H, S])
        c_prob = carve([2 * H, S])
        s_prob = carve([H, S])
        w_stage = c_prob.rearrange("p a b -> p (a b)")
        band = carve([S])
        far16 = carve([S], F16)
        far_ident = carve([P], F16)
        lam_in = carve([4, H, DH])
        lam_prod = carve([2, H, DH])
        lam_sum = carve([2, H])
        lam_exp = carve([2, H])
        lam_dif = carve([H])
        neg_lam = carve([H])
        w_rows = carve([DT])
        w_rows2 = carve([DT])
        s_kbd = carve([2, 8, DT, 2, S], F16)
        c_kbd = carve([8, 2 * DT, 2, S], F16)
        s_in, s_res, c_in = carve([D]), carve([D]), carve([D])
        s_xT, s_oT, c_xT, c_cT, c_oT = (carve([DT, 2, S], F16) for _ in range(5))
        s_qk = carve([2, 4, 2, S], F16)
        c_q, c_k = carve([2, 4, 2, S], F16), carve([4, 2, S], F16)
        s_v, c_v = carve([2, 2, D], F16), carve([2, 2, D], F16)
        s_pT, c_pT = carve([2, 2, Q4, S], F16), carve([2, 2, Q4, S], F16)
        s_negmax, c_max, c_negmax = carve([H]), carve([2 * H]), carve([2 * H])
        c_sum, s_expsum = carve([2, 2 * H]), carve([2, H])
        s_rsum, c_rsum, c_r2, c_ratio, c_blend = (carve([H]) for _ in range(5))
        s_o, c_o, c_oraw, c_sq = carve([D]), carve([D]), carve([D]), carve([D])
        c_ss, c_ms, c_rms = carve([H]), carve([H]), carve([H])
        s_sum, c_sumx = carve([D]), carve([D])
        s_total, c_total, s_negmean, c_negmean, s_sq, c_sqx = (carve([1]) for _ in range(6))
        s_junk, c_junk = carve([D]), carve([D])
        s_veps, c_veps, s_rstd, c_rstd = carve([1]), carve([1]), carve([1]), carve([1])
        x1, x2 = carve([D]), carve([D])
        X1_RING = 8
        x1_ring = carve([X1_RING, D])
        x2_parts = carve([2, D], F16)
        fence = carve([3])
        minus_half = carve([H])

        LAG = {"s_pre": 0, "s_proj": 1, "s_core": 2, "s_late": 3, "s_tail": 4,
               "c_pre": 4, "c_proj": 5, "c_core": 6, "c_late": 7, "c_tail": 8}
        STEPS = B + max(LAG.values())
        FIRST_FULL = max(LAG.values()) + 1
        UNITS = range(H // Q4)
        assert len(UNITS) == 4

        def earlier(slot, back):
            return (slot - back, "core") if slot >= back else (slot - back + 4, "late")

        def in_slots(back, *kinds):
            return [(f"{a}{earlier(i, back)[0]}", f"{a[0]}_{earlier(i, back)[1]}") for i in range(4) for a in kinds]

        TURN = [("s_oT", "s_tail"), ("c_oT", "c_tail"), ("s_qk", "s_proj"),
                ("s_wo", "s_tail"), ("c_wo", "c_tail"), ("c_q", "c_proj"),
                ("c_k", "c_proj"), ("s_v", "s_proj"), ("c_v", "c_proj"),
                ("s_xT", "s_pre"), ("c_cT", "c_pre"), ("x1T", "s_tail"), ("x2T", "c_tail")]
        ORDER = {
            "turn": TURN,
            "turn_hi": [e for e in TURN if e[0] not in ("s_wo", "c_wo")],
            "c_score": [(f"c{h}{u}", "c_core") for u in UNITS for h in "ab"],
            "s_score": in_slots(0, "s"),
            "blend": in_slots(1, "c"),
            "c_prob": in_slots(2, "c"),
            "s_prob": in_slots(2, "s"),
            "value": in_slots(3, "c", "s"),
        }

        class Step:

            def __init__(self, t):
                self.t = t

            def on(self, part):
                return not isinstance(self.t, int) or 0 <= self.t - LAG[part] < B

            def b(self, part):
                return self.t - LAG[part]

            def slot(self, order, use):
                live = [u for u, part in ORDER[order] if self.on(part)]
                return live.index(use)

            def before(self, order, use, ring):
                uses = [u for u, _ in ORDER[order]]
                place = uses.index(use) % ring
                step = self
                ahead = uses[:uses.index(use)]
                while True:
                    live = [u for u, part in ORDER[order] if u in ahead and uses.index(u) % ring == place and step.on(part)]
                    if live:
                        return step.count(order, live[-1])
                    if isinstance(step.t, int) and step.t <= 0:
                        return 0
                    step, ahead = step.last(), uses

            def count(self, order, use):
                parts = [part for _, part in ORDER[order]]
                if isinstance(self.t, int):
                    before = sum(min(max(self.t - LAG[p], 0), B) for p in parts)
                else:
                    before = self.t * len(parts) - sum(LAG[p] for p in parts)
                return before + self.slot(order, use) + 1

            def slot_of(self, part):
                b = self.b(part)
                return bass.ds(b % 2, 1)

            def made(self, order, use, kind):
                same = dict(ORDER[order])[use].endswith(kind)
                return (self if same else self.last()).count(order, use)

            def last(self):
                return Step(self.t - 1)

        def steps(e, body):
            for t in range(min(FIRST_FULL, STEPS)):
                body(Step(t))
            if FIRST_FULL < B:
                with e.Fori(FIRST_FULL, B) as t:
                    body(Step(t))
            for t in range(max(B, FIRST_FULL), STEPS):
                body(Step(t))

        sig = {name: sem(name) for name in '''
            constants_in weights_in s_in s_res c_in c_mask0 c_mask1 c_mask2 c_mask3 far_ident far16 x2_stored x2_parts_stored
            lam_prod lam_sum lam_exp lam_dif neg_lam w_rows2 weights_scaled weights_hi weights_lo zeros
            turn_written turn_hi turn_read c_score_written c_score_read s_score_written
            c_prob_written c_prob_hi c_prob_read s_prob_written s_prob_hi s_prob_read value_written c_value_read
            s_kbd_zero c_kbd_zero s_kbd c_kbd0 c_kbd1 s_max c_max c_negmax s_exp c_exp c_r2 c_ratio c_blend blended
            s_rsum s_o c_rsum c_sq c_ss c_ms c_rms c_o s_summed s_squares s_veps s_rstd x1 x1_kept
            c_summed c_squares c_veps c_rstd x2 x2_hi x2_parts
            f_cleared f_zero f_ones f_bias_in f_phi_in f_phi_hi f_phi_lo f_w_in f_w_hi f_w_lo f_x0 f_x1 f_x2 f_x3
            f_logits f_logits_read f_max4 f_max4_reset f_chunkmax f_max f_newmax f_rowmax f_diff f_keep
            f_shifted f_sum_exp f_sum4 f_sum4_reset f_sum f_rsum f_d_shifted f_d_exp f_dispatch f_dispatch_hi f_dispatch_lo
            f_slots0 f_slots1 f_slots2 f_slots3 f_slots_hi f_slots_lo f_c_shifted f_combine f_cT_psum f_cT_hi f_cT_lo
            f_yT_psum f_yT f_y_psum f_y_hi f_y_lo f_out f_acc
            f_res0 f_res1 f_res2 f_res3 f_n_rsum f_added f_negmean f_squares f_veps f_rstd f_normed out_stored'''.split()}

        def later(n):
            return not isinstance(n, int) or n > 0

        def in3(ap, a):
            return ap.rearrange("p (a n) -> p a n", a=a)

        def spread(ap, n):
            return ap.unsqueeze(2).broadcast_to([P, ap.shape[1], n])

        def batch(dram, b):
            return dram[bass.ds(b, 1), :, :].rearrange("o s d -> (o s) d")

        PIECE = D
        NPIECE = W_END // PIECE
        DMA = 16


        used[0] = 0
        YW = D + 2
        acc = carve([B, D + 1])
        logits = carve([B, S])
        f_w_stage = carve([DT, D])
        f_w = carve([2, DT, EC, D], F16)
        f_phi_stage = carve([DT, P])
        f_phi = carve([2, DT, P], F16)
        f_bias = carve([DT, NCH * EC])
        f_x = carve([Q4, 2, D], F16)
        f_dp = carve([2, Q4, P], F16)
        f_pair = carve([2, Q4, P])
        f_cT = carve([2, 2, Q4, S], F16)
        f_slT = carve([2, DT, Q4, P], F16)
        f_yT = carve([DT, Q4, P])
        f_y = carve([2, Q4, YW], F16)
        f_max4, f_sum4 = carve([Q4, P]), carve([Q4, P])
        f_max, f_sum, f_rsum = carve([P]), carve([P]), carve([P])
        f_chunkmax, f_rowmax, f_newmax, f_diff, f_keep = (carve([B]) for _ in range(5))
        n_half = carve([16])
        F_LAST = NQ + 3

        class Quad:

            def __init__(self, c, k):
                self.c, self.k = c, k

            def on(self, lag):
                return not isinstance(self.k, int) or 0 <= self.k - lag < NQ

            def done(self, lag, each=1):
                return self.c * (NQ * each) + (self.k - lag + 1) * each

        def quads(e, c, body):
            for k in range(min(3, F_LAST)):
                body(Quad(c, k))
            if NQ > 3:
                with e.Fori(3, NQ) as k:
                    body(Quad(c, k))
            for k in range(max(NQ, 3), F_LAST):
                body(Quad(c, k))

        def chunks(e, body):
            if NCH > 1:
                with e.Fori(0, NCH - 1) as c:
                    body(c, True)
            body(NCH - 1, False)

        def one(ap):
            return ap.rearrange("p o n -> p (o n)")

        def one4(ap):
            return ap.rearrange("p o a b -> p (o a) b")

        DISPATCH, COMBINE = 0, 1
        used[0] = B * (D + 1)
        res_ring = carve([4, Q4, D])
        norm_junk = carve([2, D])
        n_rsum, n_total, n_negmean, n_squares, n_veps, n_rstd = (carve([B]) for _ in range(6))
        NORM_GROUP = 16

        block = es.enter_context(nc.Block())

        @block.sync
        def _(sp):
            for dst, src in ((ident[:, :], ident_in), (band, band_in), (w_rows, w_scale),
                             (lam_in.rearrange("p a b c -> p (a b c)"), lambdas)):
                sp.dma_start(dst, src).then_inc(sig["constants_in"], DMA)
            for i in range(NPIECE):
                if i:
                    sp.wait_ge(sig["weights_lo"], i)
                sp.dma_start(in3(w_stage[:, 0:DT * PIECE], DT), w_all[:, :, i * PIECE:(i + 1) * PIECE]).then_inc(sig["weights_in"], DMA)

            sp.wait_ge(sig["s_kbd_zero"], 1)
            sp.wait_ge(sig["c_kbd_zero"], 1)

            def load_mask(st, u):
                if st.on("c_proj"):
                    b = st.b("c_proj")
                    if later(b):
                        sp.wait_ge(sig["c_score_read"], st.count("c_score", f"cb{u}"))
                    sp.dma_start(c_mask[:, u * Q4:(u + 1) * Q4, :],
                                     mask[bass.ds(b, 1), u * Q4:(u + 1) * Q4, :, :].rearrange("o h q k -> q (o h) k")).then_inc(sig[f"c_mask{u}"], DMA)

            def cross_keys(half):
                tiles = slice(2 * half, 2 * half + 2)
                for r in range(8):
                    rows = slice(r * P // 8, (r + 1) * P // 8)
                    sp.dma_start(c_kbd[rows, r, tiles].rearrange("p a b s -> p (a b s)"),
                                     c_k[rows, tiles].rearrange("p a b s -> p (a b s)")).then_inc(sig[f"c_kbd{half}"], DMA)

            def body(st):
                if st.on("s_pre"):
                    b = st.b("s_pre")
                    if later(b):
                        sp.wait_ge(sig["turn_written"], st.last().count("turn", "s_xT"))
                    sp.dma_start(s_in, batch(x, b)).then_inc(sig["s_in"], DMA)
                if st.on("c_pre"):
                    b = st.b("c_pre")
                    if later(b):
                        sp.wait_ge(sig["turn_written"], st.last().count("turn", "c_cT"))
                    sp.dma_start(c_in, batch(ctx_in, b)).then_inc(sig["c_in"], DMA)
                if st.on("s_tail"):
                    b = st.b("s_tail")
                    if later(b):
                        sp.wait_ge(sig["s_summed"], b)
                    sp.dma_start(s_res, batch(x, b)).then_inc(sig["s_res"], DMA)
                load_mask(st, 0)
                if st.on("s_proj"):
                    sp.wait_ge(sig["turn_read"], st.count("turn", "s_qk"))
                    for r in range(8):
                        rows = slice(r * P // 8, (r + 1) * P // 8)
                        sp.dma_start(s_kbd[rows, st.slot_of("s_proj"), r].rearrange("p o a b s -> p (o a b s)"),
                                         s_qk[rows, st.slot_of("s_proj"), 2:4].rearrange("p o a b s -> p (o a b s)")).then_inc(sig["s_kbd"], DMA)
                load_mask(st, 1)
                if st.on("c_proj"):
                    sp.wait_ge(sig["turn_read"], st.count("turn", "c_k"))
                    cross_keys(0)
                load_mask(st, 2)
                if st.on("c_proj"):
                    if st.on("s_pre"):
                        sp.wait_ge(sig["turn_written"], st.count("turn", "s_xT"))
                    elif st.on("c_core"):
                        sp.wait_ge(sig["c_score_written"], st.count("c_score", "cb3"))
                    cross_keys(1)
                if st.on("c_tail"):
                    b = st.b("c_tail")
                    sp.wait_ge(sig["x2"], b + 1)
                    sp.dma_start(batch(scratch_x2, b), x2).then_inc(sig["x2_stored"], DMA)
                    sp.wait_ge(sig["x2_parts"], b + 1)
                    sp.dma_start(batch(scratch_x2_parts, b), x2_parts.rearrange("p a d -> p (a d)")).then_inc(sig["x2_parts_stored"], DMA)
                load_mask(st, 3)

            steps(sp, body)
            sp.wait_ge(sig["x2_stored"], DMA * B)
            sp.wait_ge(sig["x2_parts_stored"], DMA * B)

            sp.wait_ge(sig["f_cleared"], 3)
            sp.dma_start(f_bias, b_ffn).then_inc(sig["f_bias_in"], DMA)
            sp.dma_start(f_phi_stage, phi[:, :, 0:P]).then_inc(sig["f_phi_in"], DMA)

            def load_expert(n):
                sp.dma_start(f_w_stage, w_ffn[bass.ds(n, 1), :, :, :].rearrange("o p k e -> p (o k) e")).then_inc(sig["f_w_in"], DMA)

            def load_x(b, j):
                sp.dma_start(f_x[:, j].rearrange("p a d -> p (a d)"), batch(scratch_x2_parts, b)).then_inc(sig[f"f_x{j}"], DMA)

            load_expert(0)
            for j in range(Q4):
                load_x(j, j)

            def sp_chunk(c, more):
                if more:
                    sp.wait_ge(sig["f_phi_lo"], c + 1)
                    sp.dma_start(f_phi_stage, phi[:, :, bass.ds((c + 1) * P, P)]).then_inc(sig["f_phi_in"], DMA)
                for j in range(EC if more else EC - 1):
                    sp.wait_ge(sig["f_w_lo"], c * EC + j + 1)
                    load_expert(c * EC + j + 1)
                with sp.Fori(0, NQ if more else NQ - 1) as g:
                    for j in range(Q4):
                        sp.wait_ge(sig[f"f_slots{j}"], c * NQ + g + 1)
                        load_x((g + 1) % NQ * Q4 + j, j)

            chunks(sp, sp_chunk)
            sp.wait_ge(sig["f_acc"], NCH * B + 1)
            for g in range(NQ):
                if g >= 4:
                    sp.wait_ge(sig["f_added"], Q4 * (g - 3))
                sp.dma_start(res_ring[:, g % 4], scratch_x2[g * Q4:(g + 1) * Q4].rearrange("b s d -> s b d")).then_inc(sig[f"f_res{g % 4}"], DMA)
            for g in range(B // NORM_GROUP):
                sp.wait_ge(sig["f_normed"], NORM_GROUP * (g + 1))
                sp.dma_start(out[g * NORM_GROUP:(g + 1) * NORM_GROUP].rearrange("b s d -> s b d"),
                                 acc[:, g * NORM_GROUP:(g + 1) * NORM_GROUP, 0:D]).then_inc(sig["out_stored"], DMA)
            sp.wait_ge(sig["out_stored"], DMA * (B // NORM_GROUP))

        @block.tensor
        def _(pe):
            pe.wait_ge(sig["weights_lo"], NPIECE)
            pe.wait_ge(sig["zeros"], 2)
            pe.wait_ge(sig["far_ident"], 1)
            pe.wait_ge(sig["far16"], 1)

            def body(st):
                s, c = "s", "c"

                def turn_bank(use):
                    others = st.before("turn", use, 2)
                    if later(others):
                        pe.wait_ge(sig["turn_read"], others)
                    return bank[f"turn{[u for u, _ in TURN].index(use) % 2}"]

                def turn(use, src):
                    dst = turn_bank(use)
                    for k in range(DT):
                        last = nc.tensor.transpose(dst[:, k * P:(k + 1) * P], src[:, k * P:(k + 1) * P], ident[:, :])
                    last.then_inc(sig["turn_written"], 1)

                def project_T(use, col, src):
                    dst = turn_bank(use)
                    for o in range(4):
                        for k in range(DT):
                            for n, (a, p) in enumerate(PASSES):
                                last = nc.tensor.matmul(dst[:, o * S:(o + 1) * S], w_parts[:, a, k, col + o * P:col + (o + 1) * P],
                                                        src[:, k, p, :], start=k + n == 0, stop=k == DT - 1 and n == 2)
                    last.then_inc(sig["turn_written"], 1)

                def project(use, col, src):
                    dst = turn_bank(use)
                    for k in range(DT):
                        for n, (a, p) in enumerate(PASSES):
                            last = nc.tensor.matmul(dst[:, 0:D], src[:, k, a, :], w_parts[:, p, k, col:col + D],
                                                    start=k + n == 0, stop=k == DT - 1 and n == 2)
                    last.then_inc(sig["turn_written"], 1)

                def self_scores(u):
                    if not st.on("s_core"):
                        return
                    before = st.before("s_score", f"s{u}", 1)
                    if later(before):
                        pe.wait_ge(sig["s_exp"], before)
                    if u == 0:
                        pe.wait_ge(sig["s_kbd"], 8 * DMA * (st.b("s_core") + 1))
                    slot, tile, r = st.slot_of("s_core"), u // 2, 4 * (u % 2)
                    for n, (a, p) in enumerate(PASSES):
                        nc.tensor.matmul(bank["score_s"][:, :], s_qk[:, slot, tile, a, :].rearrange("p o s -> p (o s)"),
                                         s_kbd[:, slot, r:r + 4, tile, p, :].rearrange("p o r k -> p (o r) k"), start=n == 0, stop=False)
                    nc.tensor.matmul(in3(bank["score_s"][:, :], Q4), far_ident, far16.unsqueeze(1).broadcast_to([P, Q4, S]),
                                     start=False, stop=True).then_inc(sig["s_score_written"], 1)

                def cross_scores(u, half):
                    if not st.on("c_core"):
                        return
                    use, name = (f"ca{u}", "score_a") if half == 0 else (f"cb{u}", "score_b")
                    before = st.before("c_score", use, 2)
                    if later(before):
                        pe.wait_ge(sig["c_score_read"], before)
                    if half == 0 and u % 2 == 0:
                        pe.wait_ge(sig[f"c_kbd{u // 2}"], 8 * DMA * (st.b("c_core") + 1))
                    for n, (a, p) in enumerate(PASSES):
                        last = nc.tensor.matmul(bank[name][:, :], c_q[:, st.slot_of("c_core"), u, a, :].rearrange("p o s -> p (o s)"),
                                                c_kbd[:, 4 * half:4 * half + 4, u, p, :], start=n == 0, stop=n == 2)
                    last.then_inc(sig["c_score_written"], 1)

                def turn_probs(which, slot):
                    u, kind = earlier(slot, 2)
                    if not st.on(f"{which}_{kind}"):
                        return
                    use = f"{which}{u}"
                    before = st.count(f"{which}_prob", use) - 1
                    if later(before):
                        pe.wait_ge(sig[f"{which}_prob_read"], before)
                    if which == c:
                        pe.wait_ge(sig["blended"], st.made("blend", use, kind))
                        src, stride = c_prob, 2
                    else:
                        pe.wait_ge(sig["s_exp"], st.made("s_score", use, kind))
                        src, stride = s_prob, 1
                    for j in range(Q4):
                        last = nc.tensor.transpose(bank[f"prob_{which}"][:, j * S:(j + 1) * S], src[:, (u * Q4 + j) * stride, :], ident[:, :])
                    last.then_inc(sig[f"{which}_prob_written"], 1)

                def values(slot):
                    u, kind = earlier(slot, 3)
                    if u == 0:
                        if st.on("c_late"):
                            pe.wait_ge(sig["c_value_read"], st.b("c_late") + 1)
                        if st.on("s_late"):
                            pe.wait_ge(sig["s_o"], st.b("s_late") + 1)
                    for which, pT, v, col in ((c, c_pT, c_v, 0), (s, s_pT, s_v, D)):
                        if not st.on(f"{which}_{kind}"):
                            continue
                        pe.wait_ge(sig[f"{which}_prob_read"], st.made(f"{which}_prob", f"{which}{u}", kind))
                        place = st.slot_of(f"{which}_{kind}")
                        for j in range(Q4):
                            h = u * Q4 + j
                            for n, (a, p) in enumerate(PASSES):
                                last = nc.tensor.matmul(bank["value"][:, col + h * DH:col + (h + 1) * DH], pT[:, u % 2, a, j, :],
                                                        v[:, place, p, h * DH:(h + 1) * DH].rearrange("p o d -> p (o d)"), start=n == 0, stop=n == 2)
                        last.then_inc(sig["value_written"], 1)

                def slot_start(u):
                    turn_probs(c, u)
                    turn_probs(s, u)

                def first_scores(u):
                    self_scores(u)
                    cross_scores(u, 0)

                first_scores(0)
                slot_start(0)
                if st.on("s_tail"):
                    pe.wait_ge(sig["s_o"], st.b("s_tail") + 1)
                    turn("s_oT", s_o)
                cross_scores(0, 1)
                values(0)
                first_scores(1)
                if st.on("c_tail"):
                    pe.wait_ge(sig["c_o"], st.b("c_tail") + 1)
                    turn("c_oT", c_o)
                if st.on("s_proj"):
                    pe.wait_ge(sig["turn_read"], st.last().count("turn", "s_xT"))
                    project_T("s_qk", SQ, s_xT)
                slot_start(1)
                if st.on("s_tail"):
                    pe.wait_ge(sig["turn_read"], st.count("turn", "s_oT"))
                    project("s_wo", SO, s_oT)
                cross_scores(1, 1)
                values(1)
                first_scores(2)
                if st.on("c_tail"):
                    pe.wait_ge(sig["turn_read"], st.count("turn", "c_oT"))
                    project("c_wo", CO, c_oT)
                if st.on("c_proj"):
                    pe.wait_ge(sig["turn_read"], st.last().count("turn", "x1T"))
                    project_T("c_q", CQ, c_xT)
                slot_start(2)
                if st.on("c_proj"):
                    pe.wait_ge(sig["turn_read"], st.last().count("turn", "c_cT"))
                    project_T("c_k", CK, c_cT)
                cross_scores(2, 1)
                values(2)
                first_scores(3)
                if st.on("s_proj"):
                    project("s_v", SV, s_xT)
                if st.on("c_proj"):
                    project("c_v", CV, c_cT)
                slot_start(3)
                cross_scores(3, 1)
                if st.on("s_pre"):
                    pe.wait_ge(sig["s_in"], DMA * (st.b("s_pre") + 1))
                    turn("s_xT", s_in)
                if st.on("c_pre"):
                    pe.wait_ge(sig["c_in"], DMA * (st.b("c_pre") + 1))
                    turn("c_cT", c_in)
                values(3)
                if st.on("s_tail"):
                    pe.wait_ge(sig["x1"], st.b("s_tail") + 1)
                    turn("x1T", x1)
                if st.on("c_tail"):
                    pe.wait_ge(sig["x2"], st.b("c_tail") + 1)
                    turn("x2T", x2)

            steps(pe, body)

            FB = [bank[n] for n in ("turn0", "turn1", "score_a", "score_b", "score_s", "prob_c", "prob_s", "value")]
            b_turn, b_slots, b_yT, b_y, b_out = FB[0], FB[1:3], FB[3:5], FB[5:7], FB[7]
            mm = nc.tensor.matmul
            pe.wait_ge(sig["f_cleared"], 3)

            def pe_logits(g, js):
                for j in js:
                    for k in range(DT):
                        for n, (a, c_) in enumerate(PASSES):
                            last = mm(b_turn[:, j * P:(j + 1) * P], xT[:, a, k, bass.ds((g * Q4 + j) * S, S)], f_phi[:, c_, k, :],
                                      start=k + n == 0, stop=k == DT - 1 and n == 2)
                return last

            pe.wait_ge(sig["f_phi_lo"], 1)
            pe_logits(0, range(Q4)).then_inc(sig["f_logits"], 1)
            with pe.Fori(1, NQ) as g:
                pe.wait_ge(sig["f_logits_read"], g)
                pe_logits(g, range(Q4)).then_inc(sig["f_logits"], 1)

            def pe_chunk(c, more):
                pe.wait_ge(sig["f_w_lo"], c * EC + EC)
                if more:
                    pe.wait_ge(sig["f_phi_lo"], c + 2)

                def body(st):
                    k = st.k

                    def out_product(j):
                        if not st.on(3):
                            return
                        if j == 0:
                            pe.wait_ge(sig["f_y_lo"], st.done(3, 2))
                            pe.wait_ge(sig["f_cT_lo"], st.done(3))
                        pe.wait_ge(sig["f_acc"], (c * NQ + k - 3) * Q4 + j + 1)
                        slot = bass.ds((k - 3) % 2, 1)
                        for n, (a, c_) in enumerate(PASSES):
                            last = mm(b_out[:, 0:D + 1], one(f_cT[:, slot, a, j, :]), f_y[:, c_, j, 0:D + 1], start=n == 0, stop=n == 2)
                        last.then_inc(sig["f_out"], 1)

                    out_product(0)
                    if st.on(2):
                        pe.wait_ge(sig["f_combine"], st.done(2))
                        before = k - 3 if not isinstance(k, int) else max(k - 3, 0)
                        pe.wait_ge(sig["f_logits_read"], (c + 1) * NQ + (before if more else 0))
                        for j in range(Q4):
                            last = nc.tensor.transpose(b_turn[:, j * S:(j + 1) * S], f_pair[:, COMBINE, j, :], ident[:, :])
                        last.then_inc(sig["f_cT_psum"], 1)
                    out_product(1)
                    if st.on(3) and more:
                        done = min(k - 2 + 1, NQ) if isinstance(k, int) else k - 2 + 1
                        pe.wait_ge(sig["f_cT_lo"], c * NQ + done)
                        pe_logits(k - 3, (0, 1))
                    out_product(2)
                    if st.on(3) and more:
                        pe_logits(k - 3, (2, 3)).then_inc(sig["f_logits"], 1)
                    out_product(3)
                    if st.on(2):
                        pe.wait_ge(sig["f_yT"], st.done(2, 2))
                        for half in range(2):
                            for j in (2 * half, 2 * half + 1):
                                for e in range(DT):
                                    col = (j % 2) * D + e * P
                                    last = nc.tensor.transpose(b_y[half][:, col:col + P], f_yT[:, e, j, :], ident[:, :])
                            last.then_inc(sig["f_y_psum"], 1)
                    if st.on(1):
                        pe.wait_ge(sig["f_slots_lo"], st.done(1, 2))
                        for e in range(DT):
                            for x_ in range(EC):
                                for kk in range(DT):
                                    for n, (a, c_) in enumerate(PASSES):
                                        last = mm(b_yT[e][:, :].rearrange("p (b s) -> p b s", b=Q4)[:, :, x_ * SP_E:(x_ + 1) * SP_E],
                                                  f_w[:, a, kk, x_, e * P:(e + 1) * P], f_slT[:, c_, kk, :, x_ * SP_E:(x_ + 1) * SP_E],
                                                  start=kk + n == 0, stop=kk == DT - 1 and n == 2)
                            last.then_inc(sig["f_yT_psum"], 1)
                    if st.on(0):
                        pe.wait_ge(sig["f_dispatch_lo"], st.done(0))
                        for e in range(DT):
                            for j in range(Q4):
                                if e == 0:
                                    pe.wait_ge(sig[f"f_x{j}"], DMA * st.done(0))
                                for n, (a, c_) in enumerate(PASSES):
                                    last = mm(b_slots[e][:, j * P:(j + 1) * P], f_x[:, j, a, e * P:(e + 1) * P], f_dp[:, c_, j, :],
                                              start=n == 0, stop=n == 2)
                                if e == DT - 1:
                                    last.then_inc(sig[f"f_slots{j}"], 1)
                quads(pe, c, body)

            chunks(pe, pe_chunk)

        @block.scalar
        def _(act):
            act.wait_ge(sig["constants_in"], DMA * 4)
            act.wait_ge(sig["lam_sum"], 1)
            nc.scalar.activation(lam_exp.rearrange("p a b -> p (a b)"), lam_sum.rearrange("p a b -> p (a b)"), ACT.Exp).then_inc(sig["lam_exp"], 1)
            for i in range(NPIECE):
                act.wait_ge(sig["weights_scaled"], i + 1)
                nc.scalar.activation(w_parts[:, HI, :, i * PIECE:(i + 1) * PIECE], in3(w_stage[:, 0:DT * PIECE], DT), ACT.Copy).then_inc(sig["weights_hi"], 1)

            def body(st):
                def hi_turn(use, dst, tiles):
                    src = bank[f"turn{[u for u, _ in TURN].index(use) % 2}"]
                    act.wait_ge(sig["turn_written"], st.count("turn", use))
                    nc.scalar.activation(dst, in3(src[:, 0:tiles * P], tiles), ACT.Copy).then_inc(sig["turn_hi"], 1)

                def squares(part, b, junk, summed, negmean, total):
                    act.wait_ge(sig[f"{part}_summed"], b + 1)
                    nc.scalar.activation(junk, summed, ACT.Square, bias=negmean, accum_out=total).then_inc(sig[f"{part}_squares"], 1)

                def cross_exps(u, half):
                    if st.on("c_core"):
                        act.wait_ge(sig["c_negmax"], st.count("c_score", f"c{'ab'[half]}{u}"))
                        g = 2 * u + half
                        for r in range(4 * g, 4 * g + 4):
                            last = nc.scalar.activation(c_prob[:, r, :], c_prob[:, r, :], ACT.Exp,
                                                        bias=c_negmax[:, r:r + 1], accum_out=one(c_sum[:, st.slot_of("c_core"), r:r + 1]))
                        last.then_inc(sig["c_exp"], 1)

                def self_exps(u):
                    if st.on("s_core"):
                        act.wait_ge(sig["s_max"], st.count("s_score", f"s{u}"))
                        for j in range(Q4):
                            h = u * Q4 + j
                            last = nc.scalar.activation(s_prob[:, h, :], bank["score_s"][:, j * S:(j + 1) * S], ACT.Exp,
                                                        bias=s_negmax[:, h:h + 1], accum_out=one(s_expsum[:, st.slot_of("s_core"), h:h + 1]))
                        last.then_inc(sig["s_exp"], 1)

                def prob_hi(which, slot):
                    u, kind = earlier(slot, 2)
                    if st.on(f"{which}_{kind}"):
                        pT = c_pT if which == "c" else s_pT
                        act.wait_ge(sig[f"{which}_prob_written"], st.count(f"{which}_prob", f"{which}{u}"))
                        nc.scalar.activation(pT[:, u % 2, HI, :, :], in3(bank[f"prob_{which}"][:, :], Q4), ACT.Copy).then_inc(sig[f"{which}_prob_hi"], 1)

                def q_like(buf, part):
                    return buf[:, st.slot_of(part), :, HI, :].rearrange("p o a s -> p (o a) s")

                def v_like(buf, part):
                    return in3(buf[:, st.slot_of(part), HI, :].rearrange("p o d -> p (o d)"), DT)

                def slot_start(u):
                    prob_hi("c", u)
                    self_exps(u)
                    prob_hi("s", u)
                    cross_exps(u, 0)

                slot_start(0)
                if st.on("s_tail"):
                    hi_turn("s_oT", s_oT[:, :, HI], DT)
                cross_exps(0, 1)
                if st.on("c_tail"):
                    hi_turn("c_oT", c_oT[:, :, HI], DT)
                if st.on("s_proj"):
                    hi_turn("s_qk", q_like(s_qk, "s_proj"), 4)
                slot_start(1)
                if st.on("s_tail"):
                    squares("s", st.b("s_tail"), s_junk, s_sum, s_negmean, s_sq)
                cross_exps(1, 1)
                if st.on("c_proj"):
                    hi_turn("c_q", q_like(c_q, "c_proj"), 4)
                if st.on("c_tail"):
                    squares("c", st.b("c_tail"), c_junk, c_sumx, c_negmean, c_sqx)
                slot_start(2)
                if st.on("c_proj"):
                    hi_turn("c_k", c_k[:, :, HI], 4)
                if st.on("s_tail"):
                    b = st.b("s_tail")
                    act.wait_ge(sig["x1"], b + 1)
                    nc.scalar.activation(x1_ring[:, bass.ds(b % X1_RING, 1), :].rearrange("p o d -> p (o d)"), x1, ACT.Copy).then_inc(sig["x1_kept"], 1)
                cross_exps(2, 1)
                if st.on("s_proj"):
                    hi_turn("s_v", v_like(s_v, "s_proj"), DT)
                if st.on("c_proj"):
                    hi_turn("c_v", v_like(c_v, "c_proj"), DT)
                slot_start(3)
                if st.on("s_pre"):
                    hi_turn("s_xT", s_xT[:, :, HI], DT)
                if st.on("c_pre"):
                    hi_turn("c_cT", c_cT[:, :, HI], DT)
                if st.on("c_tail"):
                    b = st.b("c_tail")
                    act.wait_ge(sig["x2"], b + 1)
                    if later(b):
                        act.wait_ge(sig["x2_parts_stored"], DMA * b)
                    nc.scalar.activation(x2_parts[:, HI, :], x2, ACT.Copy).then_inc(sig["x2_hi"], 1)
                cross_exps(3, 1)
                if st.on("s_tail"):
                    hi_turn("x1T", c_xT[:, :, HI], DT)
                if st.on("c_tail"):
                    hi_turn("x2T", xT[:, HI, :, bass.ds(st.b("c_tail") * S, S)], DT)

            steps(act, body)

            EXP, COPY = ACT.Exp, ACT.Copy
            nc.scalar.activation(fence[:, 0:1], neg_lam[:, 0:1], COPY).then_inc(sig["f_cleared"], 1)

            def flat(ap):
                return ap.rearrange("p a b -> p (a b)")

            def act_phi(n):
                act.wait_ge(sig["f_phi_in"], DMA * n)
                nc.scalar.activation(f_phi[:, HI], f_phi_stage, COPY).then_inc(sig["f_phi_hi"], 1)

            def act_logits(g, n):
                act.wait_ge(sig["f_logits"], n)
                nc.scalar.activation(logits[:, bass.ds(g * Q4, Q4), :], in3(FBV[0][:, :], Q4), COPY).then_inc(sig["f_logits_read"], 1)

            FBV = [bank[n] for n in ("turn0", "turn1", "score_a", "score_b", "score_s", "prob_c", "prob_s", "value")]
            act.wait_ge(sig["f_cleared"], 3)
            act_phi(1)
            with act.Fori(0, NQ) as g:
                act_logits(g, g + 1)

            def act_chunk(c, more):
                act.wait_ge(sig["f_diff"], c + 1)
                nc.scalar.activation(f_keep, f_diff, EXP).then_inc(sig["f_keep"], 1)
                with act.Fori(0, NQ) as g:
                    act.wait_ge(sig["f_shifted"], c * NQ + g + 1)
                    part = f_pair[:, bass.ds(g % 2, 1), :, :].rearrange("p o a b -> p (o a b)")
                    nc.scalar.activation(part, part, EXP).then_inc(sig["f_sum_exp"], 1)
                for j in range(EC):
                    act.wait_ge(sig["f_w_in"], DMA * (c * EC + j + 1))
                    nc.scalar.activation(f_w[:, HI, :, j, :], f_w_stage, COPY).then_inc(sig["f_w_hi"], 1)
                if more:
                    act_phi(c + 2)

                def body(st):
                    k = st.k
                    if st.on(0):
                        act.wait_ge(sig["f_d_shifted"], st.done(0))
                        nc.scalar.activation(flat(f_pair[:, DISPATCH]), flat(f_pair[:, DISPATCH]), EXP).then_inc(sig["f_d_exp"], 1)
                    if st.on(2):
                        act.wait_ge(sig["f_cT_psum"], st.done(2))
                        nc.scalar.activation(f_cT[:, bass.ds((k - 2) % 2, 1), HI, :, :].rearrange("p o a b -> p (o a b)"), FBV[0][:, :], COPY).then_inc(sig["f_cT_hi"], 1)
                    if st.on(3) and more:
                        act_logits(k - 3, (c + 1) * NQ + k - 2)
                    if st.on(0):
                        act.wait_ge(sig["f_dispatch"], st.done(0))
                        if later(k):
                            act.wait_ge(sig["f_slots3"], st.done(1))
                        nc.scalar.activation(f_dp[:, HI], f_pair[:, DISPATCH], COPY).then_inc(sig["f_dispatch_hi"], 1)
                    if st.on(1):
                        act.wait_ge(sig["f_c_shifted"], st.done(1))
                        nc.scalar.activation(flat(f_pair[:, COMBINE]), flat(f_pair[:, COMBINE]), EXP).then_inc(sig["f_combine"], 1)
                    if st.on(2):
                        for half in range(2):
                            act.wait_ge(sig["f_y_psum"], st.done(2, 2) - 1 + half)
                            nc.scalar.activation(f_y[:, HI, 2 * half:2 * half + 2, 0:D], in3(FBV[5 + half][:, :], 2), COPY).then_inc(sig["f_y_hi"], 1)
                    if st.on(0):
                        act.wait_ge(sig["f_slots3"], st.done(0))
                        for e in range(DT):
                            nc.scalar.activation(f_slT[:, HI, e], in3(FBV[1 + e][:, :], Q4), COPY).then_inc(sig["f_slots_hi"], 1)
                quads(act, c, body)

            chunks(act, act_chunk)
            for g in range(B // NORM_GROUP):
                act.wait_ge(sig["f_negmean"], g + 1)
                for b in range(g * NORM_GROUP, (g + 1) * NORM_GROUP):
                    if b:
                        act.wait_ge(sig["f_squares"], b)
                    nc.scalar.activation(norm_junk[:, b % 2], acc[:, b, 0:D], ACT.Square, bias=n_negmean[:, b:b + 1],
                                             accum_out=n_squares[:, b:b + 1]).then_inc(sig["f_squares"], 1)

        @block.vector
        def _(dve):
            dve.wait_ge(sig["constants_in"], DMA * 4)
            nc.vector.tensor_scalar(far_ident, ident[:, :], FAR, None, ALU.mult).then_inc(sig["far_ident"], 1)
            nc.vector.tensor_scalar(far16, band, FAR, None, ALU.mult).then_inc(sig["far16"], 1)
            pairs = lam_in.rearrange("p (i two) b c -> p i two b c", two=2)
            nc.vector.tensor_tensor(lam_prod, pairs[:, :, 0], pairs[:, :, 1], ALU.mult).then_inc(sig["lam_prod"], 1)
            dve.wait_ge(sig["lam_prod"], 1)
            nc.vector.reduce_sum(lam_sum, lam_prod, AX.X).then_inc(sig["lam_sum"], 1)
            dve.wait_ge(sig["lam_exp"], 1)
            nc.vector.tensor_tensor(lam_dif, lam_exp[:, 1, :], lam_exp[:, 0, :], ALU.subtract).then_inc(sig["lam_dif"], 1)
            dve.wait_ge(sig["lam_dif"], 1)
            nc.vector.tensor_scalar(neg_lam, lam_dif, -LAMBDA_INIT, None, ALU.add).then_inc(sig["neg_lam"], 1)
            nc.vector.tensor_scalar(w_rows2, w_rows, OUT_SCALE, None, ALU.mult).then_inc(sig["w_rows2"], 1)
            dve.wait_ge(sig["neg_lam"], 1)
            dve.wait_ge(sig["w_rows2"], 1)
            for i in range(NPIECE):
                dve.wait_ge(sig["weights_in"], DMA * (i + 1))
                col, stage = i * PIECE, in3(w_stage[:, 0:DT * PIECE], DT)
                scale = SCORE_SCALE if SQ <= col < SK or CQ <= col < CK else 1.0
                for k in range(DT):
                    if CO <= col:
                        last = nc.vector.tensor_scalar(stage[:, k], stage[:, k], w_rows2[:, k:k + 1], None, ALU.mult)
                    else:
                        last = nc.vector.tensor_scalar(stage[:, k], stage[:, k], scale, None, ALU.mult)
                last.then_inc(sig["weights_scaled"], 1)
                dve.wait_ge(sig["weights_hi"], i + 1)
                nc.vector.tensor_tensor(w_parts[:, LO, :, col:col + PIECE], stage, w_parts[:, HI, :, col:col + PIECE], ALU.subtract).then_inc(sig["weights_lo"], 1)

            def body(st):
                def lo_turn(use, dst, hi, tiles):
                    src = bank[f"turn{[u for u, _ in TURN].index(use) % 2}"]
                    dve.wait_ge(sig["turn_hi"], st.count("turn_hi", use))
                    nc.vector.tensor_tensor(dst, in3(src[:, 0:tiles * P], tiles), hi, ALU.subtract).then_inc(sig["turn_read"], 1)

                def lo_T(use, parts):
                    lo_turn(use, parts[:, :, LO], parts[:, :, HI], parts.shape[1])

                def lo_q(use, buf, part):
                    at = [buf[:, st.slot_of(part), :, p, :].rearrange("p o a s -> p (o a) s") for p in (HI, LO)]
                    lo_turn(use, at[LO], at[HI], 4)

                def lo_v(use, buf, part):
                    at = [in3(buf[:, st.slot_of(part), p, :].rearrange("p o d -> p (o d)"), DT) for p in (HI, LO)]
                    lo_turn(use, at[LO], at[HI], DT)

                def self_max(u):
                    if st.on("s_core"):
                        n = st.count("s_score", f"s{u}")
                        dve.wait_ge(sig["s_score_written"], n)
                        nc.vector.reduce_max(s_negmax[:, u * Q4:(u + 1) * Q4], in3(bank["score_s"][:, :], Q4), AX.X, negate=True).then_inc(sig["s_max"], 1)

                def add_mask(g):
                    name = ["score_a", "score_b"][g % 2]
                    for i in range(4):
                        last = nc.vector.tensor_tensor_reduce(c_prob[:, 4 * g + i, :], bank[name][:, i * S:(i + 1) * S], c_mask[:, 2 * g + i // 2, :],
                                                              1.0, LOWEST, ALU.add, ALU.max, c_max[:, 4 * g + i:4 * g + i + 1])
                    last.then_inc(sig["c_score_read"], 1)

                def negate_max(u, half):
                    g = 2 * u + half
                    dve.wait_ge(sig["c_score_read"], st.count("c_score", f"c{'ab'[half]}{u}"))
                    nc.vector.tensor_scalar(c_negmax[:, 4 * g:4 * g + 4], c_max[:, 4 * g:4 * g + 4], -1.0, None, ALU.mult).then_inc(sig["c_negmax"], 1)

                def slot_start(slot):
                    if st.on("c_core"):
                        dve.wait_ge(sig[f"c_mask{slot}"], DMA * (st.b("c_core") + 1))
                        dve.wait_ge(sig["c_score_written"], st.count("c_score", f"ca{slot}"))
                    self_max(slot)
                    if st.on("c_core"):
                        add_mask(2 * slot)
                        negate_max(slot, 0)

                def slot_middle(slot):
                    v, kind = earlier(slot, 1)
                    core, blend = st.on("c_core"), st.on(f"c_{kind}")
                    heads = slice(v * Q4, (v + 1) * Q4)
                    if blend:
                        n = st.count("blend", f"c{v}")
                        sums = one(c_sum[:, st.slot_of(f"c_{kind}"), :]).rearrange("p (h i) -> p h i", i=2)
                        dve.wait_ge(sig["c_exp"], st.made("c_score", f"cb{v}", kind))
                        nc.vector.reciprocal(c_r2[:, heads], sums[:, heads, 1]).then_inc(sig["c_r2"], 1)
                    prob_lo("c", slot)
                    if core:
                        dve.wait_ge(sig["c_score_written"], st.count("c_score", f"cb{slot}"))
                    if blend:
                        dve.wait_ge(sig["c_r2"], n)
                        nc.vector.tensor_tensor(c_ratio[:, heads], c_r2[:, heads], sums[:, heads, 0], ALU.mult).then_inc(sig["c_ratio"], 1)
                    if core:
                        add_mask(2 * slot + 1)
                    if blend:
                        dve.wait_ge(sig["c_ratio"], n)
                        nc.vector.tensor_tensor(c_blend[:, heads], c_ratio[:, heads], neg_lam[:, heads], ALU.mult).then_inc(sig["c_blend"], 1)
                    if core:
                        negate_max(slot, 1)
                    prob_lo("s", slot)

                def blend_unit(slot):
                    v, kind = earlier(slot, 1)
                    if not st.on(f"c_{kind}"):
                        return
                    dve.wait_ge(sig["c_blend"], st.count("blend", f"c{v}"))
                    for h in range(v * Q4, (v + 1) * Q4):
                        last = nc.vector.scalar_tensor_tensor(c_prob[:, 2 * h, :], c_prob[:, 2 * h + 1, :], c_blend[:, h:h + 1],
                                                              c_prob[:, 2 * h, :], ALU.mult, ALU.add)
                    last.then_inc(sig["blended"], 1)

                def prob_lo(which, slot):
                    u, kind = earlier(slot, 2)
                    if st.on(f"{which}_{kind}"):
                        pT = c_pT if which == "c" else s_pT
                        dve.wait_ge(sig[f"{which}_prob_hi"], st.count(f"{which}_prob", f"{which}{u}"))
                        nc.vector.tensor_tensor(pT[:, u % 2, LO], in3(bank[f"prob_{which}"][:, :], Q4), pT[:, u % 2, HI], ALU.subtract).then_inc(sig[f"{which}_prob_read"], 1)

                def norm_mean(part, use, res, summed, total, negmean):
                    dve.wait_ge(sig["turn_written"], st.count("turn", use))
                    nc.vector.scalar_tensor_tensor(summed, bank[f"turn{[u for u, _ in TURN].index(use) % 2}"][:, 0:D], 1.0, res, ALU.mult, ALU.add,
                                                   accum_out=total).then_inc(sig["turn_read"], 1)
                    dve.wait_ge(sig["turn_read"], st.count("turn", use))
                    nc.vector.tensor_scalar(negmean, total, -1.0 / D, None, ALU.mult).then_inc(sig[f"{part}_summed"], 1)

                def norm_variance(part, b, squares, veps):
                    dve.wait_ge(sig[f"{part}_squares"], b + 1)
                    nc.vector.tensor_scalar(veps, squares, 1.0 / D, LN_EPS, ALU.mult, ALU.add).then_inc(sig[f"{part}_veps"], 1)

                def norm_apply(part, b, summed, negmean, rstd, dst, name):
                    dve.wait_ge(sig[f"{part}_rstd"], b + 1)
                    nc.vector.tensor_scalar(dst, summed, negmean, rstd, ALU.add, ALU.mult).then_inc(sig[name], 1)

                slot_start(0)
                if st.on("c_tail"):
                    dve.wait_ge(sig["c_rms"], st.b("c_tail") + 1)
                    nc.vector.tensor_tensor(in3(c_o, H), in3(c_oraw, H), spread(c_rms, DH), ALU.mult).then_inc(sig["c_o"], 1)
                slot_middle(0)
                if st.on("s_tail"):
                    lo_T("s_oT", s_oT)
                blend_unit(0)
                if st.on("c_tail"):
                    lo_T("c_oT", c_oT)
                if st.on("s_proj"):
                    lo_q("s_qk", s_qk, "s_proj")
                slot_start(1)
                if st.on("s_tail"):
                    dve.wait_ge(sig["s_res"], DMA * (st.b("s_tail") + 1))
                    norm_mean("s", "s_wo", s_res, s_sum, s_total, s_negmean)
                slot_middle(1)
                if st.on("c_tail"):
                    ctb = st.b("c_tail")
                    dve.wait_ge(sig["x1_kept"], ctb + 1)
                    norm_mean("c", "c_wo", x1_ring[:, bass.ds(ctb % X1_RING, 1), :].rearrange("p o d -> p (o d)"), c_sumx, c_total, c_negmean)
                blend_unit(1)
                if st.on("s_tail"):
                    norm_variance("s", st.b("s_tail"), s_sq, s_veps)
                if st.on("c_proj"):
                    lo_q("c_q", c_q, "c_proj")
                slot_start(2)
                if st.on("s_tail"):
                    if later(st.b("s_tail")):
                        dve.wait_ge(sig["x1_kept"], st.b("s_tail"))
                    norm_apply("s", st.b("s_tail"), s_sum, s_negmean, s_rstd, x1, "x1")
                if st.on("c_tail"):
                    norm_variance("c", st.b("c_tail"), c_sqx, c_veps)
                slot_middle(2)
                if st.on("c_proj"):
                    lo_T("c_k", c_k)
                blend_unit(2)
                if st.on("s_proj"):
                    lo_v("s_v", s_v, "s_proj")
                if st.on("s_late"):
                    b = st.b("s_late")
                    nc.vector.reciprocal(s_rsum, one(s_expsum[:, st.slot_of("s_late"), :])).then_inc(sig["s_rsum"], 1)
                if st.on("c_late"):
                    b = st.b("c_late")
                    sums = one(c_sum[:, st.slot_of("c_late"), :]).rearrange("p (h i) -> p h i", i=2)
                    nc.vector.reciprocal(c_rsum, sums[:, :, 0]).then_inc(sig["c_rsum"], 1)
                    dve.wait_ge(sig["value_written"], st.count("value", "s3" if st.on("s_late") else "c3"))
                    dve.wait_ge(sig["c_rsum"], b + 1)
                    nc.vector.tensor_tensor(in3(c_oraw, H), in3(bank["value"][:, 0:D], H), spread(c_rsum, DH), ALU.mult).then_inc(sig["c_value_read"], 1)
                if st.on("s_late"):
                    b = st.b("s_late")
                    dve.wait_ge(sig["value_written"], st.count("value", "s3"))
                    dve.wait_ge(sig["s_rsum"], b + 1)
                    nc.vector.tensor_tensor(in3(s_o, H), in3(bank["value"][:, D:2 * D], H), spread(s_rsum, DH), ALU.mult).then_inc(sig["s_o"], 1)
                if st.on("c_proj"):
                    lo_v("c_v", c_v, "c_proj")
                slot_start(3)
                if st.on("c_tail"):
                    ctb = st.b("c_tail")
                    if later(ctb):
                        dve.wait_ge(sig["x2_stored"], DMA * ctb)
                        dve.wait_ge(sig["x2_parts"], ctb)
                    norm_apply("c", ctb, c_sumx, c_negmean, c_rstd, x2, "x2")
                slot_middle(3)
                if st.on("c_late"):
                    b = st.b("c_late")
                    dve.wait_ge(sig["c_sq"], b + 1)
                    nc.vector.reduce_sum(c_ss, in3(c_sq, H), AX.X).then_inc(sig["c_ss"], 1)
                if st.on("s_pre"):
                    lo_T("s_xT", s_xT)
                if st.on("c_late"):
                    dve.wait_ge(sig["c_ss"], b + 1)
                    nc.vector.tensor_scalar(c_ms, c_ss, 1.0 / DH, RMS_EPS, ALU.mult, ALU.add).then_inc(sig["c_ms"], 1)
                if st.on("c_pre"):
                    lo_T("c_cT", c_cT)
                blend_unit(3)
                if st.on("s_tail"):
                    lo_T("x1T", c_xT)
                if st.on("c_tail"):
                    at = xT[:, :, :, bass.ds(st.b("c_tail") * S, S)]
                    lo_turn("x2T", at[:, LO], at[:, HI], DT)

            steps(dve, body)

            FBV = [bank[n] for n in ("turn0", "turn1", "score_a", "score_b", "score_s", "prob_c", "prob_s", "value")]
            nc.vector.memset(fence[:, 1:2], 0.0).then_inc(sig["f_cleared"], 1)
            dve.wait_ge(sig["f_cleared"], 3)
            dve.wait_ge(sig["x2_parts_stored"], DMA * B)
            dve.wait_ge(sig["x2_stored"], DMA * B)
            nc.vector.memset(acc[:, 0:B // 2, :], 0.0).then_inc(sig["f_acc"], 1)
            nc.vector.memset(f_rowmax, -1e30).then_inc(sig["f_zero"], 1)
            nc.vector.memset(f_max4, -3e38).then_inc(sig["f_zero"], 1)

            def dve_phi(n):
                dve.wait_ge(sig["f_phi_hi"], n)
                nc.vector.tensor_tensor(f_phi[:, LO], f_phi_stage, f_phi[:, HI], ALU.subtract).then_inc(sig["f_phi_lo"], 1)

            def dve_maxima(g, n):
                dve.wait_ge(sig["f_logits_read"], n)
                dve.wait_ge(sig["f_max4"], n - 1)
                part = logits[:, bass.ds(g * Q4, Q4), :]
                nc.vector.tensor_tensor(f_max4, f_max4, part, ALU.max).then_inc(sig["f_max4"], 1)
                nc.vector.reduce_max(f_chunkmax[:, bass.ds(g * Q4, Q4)], part, AX.X).then_inc(sig["f_chunkmax"], 1)

            dve_phi(1)
            dve.wait_ge(sig["f_zero"], 3)
            dve.wait_ge(sig["f_logits_read"], 1)
            nc.vector.tensor_tensor(f_max4, f_max4, logits[:, 0:Q4, :], ALU.max).then_inc(sig["f_max4"], 1)
            nc.vector.reduce_max(f_chunkmax[:, 0:Q4], logits[:, 0:Q4, :], AX.X).then_inc(sig["f_chunkmax"], 1)
            with dve.Fori(1, NQ) as g:
                dve_maxima(g, g + 1)

            def dve_chunk(c, more):
                dve.wait_ge(sig["f_max4"], (c + 1) * NQ)
                nc.vector.reduce_max(f_max, f_max4.rearrange("p q n -> p n q"), AX.X).then_inc(sig["f_max"], 1)
                dve.wait_ge(sig["f_chunkmax"], (c + 1) * NQ)
                nc.vector.tensor_tensor(f_newmax, f_rowmax, f_chunkmax, ALU.max).then_inc(sig["f_newmax"], 1)
                dve.wait_ge(sig["f_newmax"], c + 1)
                nc.vector.tensor_tensor(f_diff, f_rowmax, f_newmax, ALU.subtract).then_inc(sig["f_diff"], 1)
                dve.wait_ge(sig["f_diff"], c + 1)
                nc.vector.tensor_copy(f_rowmax, f_newmax).then_inc(sig["f_rowmax"], 1)
                dve.wait_ge(sig["f_max"], c + 1)
                nc.vector.memset(f_max4, -3e38).then_inc(sig["f_max4_reset"], 1)
                nc.vector.memset(f_sum4, 0.0).then_inc(sig["f_sum4_reset"], 1)
                dve.wait_ge(sig["f_sum4_reset"], c + 1)
                dve.wait_ge(sig["f_sum_exp"], c * NQ + 1)
                nc.vector.tensor_tensor(f_sum4, f_sum4, f_pair[:, 0], ALU.add).then_inc(sig["f_sum4"], 1)
                with dve.Fori(1, NQ) as g:
                    dve.wait_ge(sig["f_sum_exp"], c * NQ + g + 1)
                    dve.wait_ge(sig["f_sum4"], c * NQ + g)
                    nc.vector.tensor_tensor(f_sum4, f_sum4, one4(f_pair[:, bass.ds(g % 2, 1), :, :]), ALU.add).then_inc(sig["f_sum4"], 1)
                dve.wait_ge(sig["f_sum4"], (c + 1) * NQ)
                nc.vector.reduce_sum(f_sum, f_sum4.rearrange("p q n -> p n q"), AX.X).then_inc(sig["f_sum"], 1)
                dve.wait_ge(sig["f_sum"], c + 1)
                nc.vector.reciprocal(f_rsum, f_sum).then_inc(sig["f_rsum"], 1)
                for j in range(EC):
                    dve.wait_ge(sig["f_w_hi"], c * EC + j + 1)
                    nc.vector.tensor_tensor(f_w[:, LO, :, j, :], f_w_stage, f_w[:, HI, :, j, :], ALU.subtract).then_inc(sig["f_w_lo"], 1)
                if more:
                    dve_phi(c + 2)
                dve.wait_ge(sig["f_keep"], c + 1)
                dve.wait_ge(sig["f_rowmax"], c + 1)
                dve.wait_ge(sig["f_max4_reset"], c + 1)

                def body(st):
                    k = st.k

                    def accumulate(j):
                        if st.on(3):
                            dve.wait_ge(sig["f_out"], (c * NQ + k - 3) * Q4 + j + 1)
                            b = bass.ds((k - 3) * Q4 + j, 1)
                            nc.vector.scalar_tensor_tensor(one(acc[:, b, :]), one(acc[:, b, :]), f_keep[:, b], FBV[7][:, 0:D + 1],
                                                               ALU.mult, ALU.add).then_inc(sig["f_acc"], 1)

                    accumulate(0)
                    if st.on(2):
                        dve.wait_ge(sig["f_cT_hi"], st.done(2))
                        slot = bass.ds((k - 2) % 2, 1)
                        nc.vector.tensor_tensor(f_cT[:, slot, LO, :, :].rearrange("p o a b -> p (o a b)"), FBV[0][:, :],
                                                    f_cT[:, slot, HI, :, :].rearrange("p o a b -> p (o a b)"), ALU.subtract).then_inc(sig["f_cT_lo"], 1)
                    accumulate(1)
                    accumulate(2)
                    accumulate(3)
                    if st.on(3) and more:
                        dve_maxima(k - 3, (c + 1) * NQ + k - 2)
                    if st.on(1):
                        if later(k - 1):
                            dve.wait_ge(sig["f_cT_psum"], st.done(2))
                        b = bass.ds((k - 1) * Q4, Q4)
                        nc.vector.tensor_tensor(f_pair[:, COMBINE], logits[:, b, :], spread(f_rowmax[:, b], P), ALU.subtract).then_inc(sig["f_c_shifted"], 1)
                    if st.on(2):
                        for half in range(2):
                            dve.wait_ge(sig["f_y_hi"], st.done(2, 2) - 1 + half)
                            part = slice(2 * half, 2 * half + 2)
                            nc.vector.tensor_tensor(f_y[:, LO, part, 0:D], in3(FBV[5 + half][:, :], 2), f_y[:, HI, part, 0:D], ALU.subtract).then_inc(sig["f_y_lo"], 1)
                    if st.on(1):
                        for e in range(DT):
                            dve.wait_ge(sig["f_yT_psum"], st.done(1, 2) - 1 + e)
                            bias = f_bias[:, e, bass.ds(c * EC, EC)].unsqueeze(1).unsqueeze(3).broadcast_to([P, Q4, EC, SP_E])
                            nc.vector.tensor_tensor(f_yT[:, e].rearrange("p b (x s) -> p b x s", x=EC),
                                                        FBV[3 + e][:, :].rearrange("p (b x s) -> p b x s", b=Q4, x=EC), bias, ALU.add).then_inc(sig["f_yT"], 1)
                    if st.on(0):
                        for e in range(DT):
                            dve.wait_ge(sig["f_slots_hi"], st.done(0, 2) - 1 + e)
                            nc.vector.tensor_tensor(f_slT[:, LO, e], in3(FBV[1 + e][:, :], Q4), f_slT[:, HI, e], ALU.subtract).then_inc(sig["f_slots_lo"], 1)
                quads(dve, c, body)

            dve.wait_ge(sig["f_bias_in"], DMA)
            chunks(dve, dve_chunk)
            dve.wait_ge(sig["f_acc"], NCH * B + 1)
            nc.vector.reciprocal(n_rsum, acc[:, :, D]).then_inc(sig["f_n_rsum"], 1)
            dve.wait_ge(sig["f_n_rsum"], 1)
            for g in range(NQ):
                dve.wait_ge(sig[f"f_res{g % 4}"], DMA * (g // 4 + 1))
                for b in range(g * Q4, (g + 1) * Q4):
                    nc.vector.scalar_tensor_tensor(acc[:, b, 0:D], acc[:, b, 0:D], n_rsum[:, b:b + 1], res_ring[:, g % 4, b % Q4],
                                                       ALU.mult, ALU.add, accum_out=n_total[:, b:b + 1]).then_inc(sig["f_added"], 1)
            dve.wait_ge(sig["f_added"], B)
            for g in range(B // NORM_GROUP):
                cols = slice(g * NORM_GROUP, (g + 1) * NORM_GROUP)
                nc.vector.tensor_scalar(n_negmean[:, cols], n_total[:, cols], -1.0 / D, None, ALU.mult).then_inc(sig["f_negmean"], 1)
            for g in range(B // NORM_GROUP):
                cols = slice(g * NORM_GROUP, (g + 1) * NORM_GROUP)
                dve.wait_ge(sig["f_squares"], NORM_GROUP * (g + 1))
                nc.vector.tensor_scalar(n_veps[:, cols], n_squares[:, cols], 1.0 / D, LN_EPS, ALU.mult, ALU.add).then_inc(sig["f_veps"], 1)
            for g in range(B // NORM_GROUP):
                dve.wait_ge(sig["f_rstd"], g + 1)
                with dve.Fori(g * NORM_GROUP, (g + 1) * NORM_GROUP) as b:
                    b1 = bass.ds(b, 1)
                    nc.vector.tensor_scalar(one(acc[:, b1, 0:D]), one(acc[:, b1, 0:D]), n_negmean[:, b1], n_rstd[:, b1], ALU.add, ALU.mult).then_inc(sig["f_normed"], 1)

        @block.gpsimd
        def _(pool):
            pool.memset(minus_half, -0.5).then_inc(sig["zeros"], 1)
            pool.memset(c_rms, 0.0).then_inc(sig["zeros"], 1)
            pool.memset(s_kbd[:, :, :, :, :, :].rearrange("p a b c d e -> p (a b c d e)"), 0.0).then_inc(sig["s_kbd_zero"], 1)
            pool.memset(c_kbd.rearrange("p a b c d -> p (a b c d)"), 0.0).then_inc(sig["c_kbd_zero"], 1)
            pool.wait_ge(sig["zeros"], 2)

            def body(st):
                def reciprocal_root(name, ready, b, dst, src):
                    pool.wait_ge(sig[ready], b + 1)
                    pool.tensor_tensor(dst, src, minus_half[:, 0:src.shape[1]], ALU.pow).then_inc(sig[name], 1)

                if st.on("s_tail"):
                    reciprocal_root("s_rstd", "s_veps", st.b("s_tail"), s_rstd, s_veps)
                if st.on("c_tail"):
                    reciprocal_root("c_rstd", "c_veps", st.b("c_tail"), c_rstd, c_veps)
                if st.on("c_late"):
                    b = st.b("c_late")
                    pool.wait_ge(sig["c_value_read"], b + 1)
                    pool.tensor_tensor(c_sq, c_oraw, c_oraw, ALU.mult).then_inc(sig["c_sq"], 1)
                if st.on("c_tail"):
                    b = st.b("c_tail")
                    pool.wait_ge(sig["x2_hi"], b + 1)
                    if later(b):
                        pool.wait_ge(sig["x2_parts_stored"], DMA * b)
                    pool.tensor_tensor(x2_parts[:, LO, :], x2, x2_parts[:, HI, :], ALU.subtract).then_inc(sig["x2_parts"], 1)
                if st.on("c_late"):
                    reciprocal_root("c_rms", "c_ms", st.b("c_late"), c_rms, c_ms)

            steps(pool, body)

            pool.memset(fence[:, 2:3], 0.0).then_inc(sig["f_cleared"], 1)
            pool.wait_ge(sig["f_cleared"], 3)
            pool.wait_ge(sig["x2_parts_stored"], DMA * B)
            pool.wait_ge(sig["x2_stored"], DMA * B)
            pool.memset(acc[:, B // 2:B, :], 0.0).then_inc(sig["f_zero"], 1)
            pool.memset(f_y[:, HI, :, D:YW], 1.0).then_inc(sig["f_ones"], 1)
            pool.memset(f_y[:, LO, :, D:YW], 0.0).then_inc(sig["f_ones"], 1)
            pool.memset(n_half, -0.5).then_inc(sig["f_ones"], 1)

            pool.wait_ge(sig["f_ones"], 3)

            def pool_chunk(c, more):
                f_max_b = f_max.unsqueeze(1).broadcast_to([P, Q4, P])
                f_rsum_b = f_rsum.unsqueeze(1).broadcast_to([P, Q4, P])
                pool.wait_ge(sig["f_max"], c + 1)
                for g in range(2):
                    pool.tensor_tensor(f_pair[:, g], logits[:, g * Q4:(g + 1) * Q4, :], f_max_b, ALU.subtract).then_inc(sig["f_shifted"], 1)
                with pool.Fori(2, NQ) as g:
                    pool.wait_ge(sig["f_sum4"], c * NQ + g - 1)
                    pool.tensor_tensor(one4(f_pair[:, bass.ds(g % 2, 1), :, :]), logits[:, bass.ds(g * Q4, Q4), :], f_max_b, ALU.subtract).then_inc(sig["f_shifted"], 1)
                pool.wait_ge(sig["f_rsum"], c + 1)

                def body(st):
                    k = st.k
                    if st.on(0):
                        if later(k):
                            pool.wait_ge(sig["f_dispatch_lo"], st.done(1))
                        pool.tensor_tensor(f_pair[:, DISPATCH], logits[:, bass.ds(k * Q4, Q4), :], f_max_b, ALU.subtract).then_inc(sig["f_d_shifted"], 1)
                        pool.wait_ge(sig["f_d_exp"], st.done(0))
                        pool.tensor_tensor(f_pair[:, DISPATCH], f_pair[:, DISPATCH], f_rsum_b, ALU.mult).then_inc(sig["f_dispatch"], 1)
                        pool.wait_ge(sig["f_dispatch_hi"], st.done(0))
                        pool.tensor_tensor(f_dp[:, LO], f_pair[:, DISPATCH], f_dp[:, HI], ALU.subtract).then_inc(sig["f_dispatch_lo"], 1)
                quads(pool, c, body)

            chunks(pool, pool_chunk)
            for g in range(B // NORM_GROUP):
                cols = slice(g * NORM_GROUP, (g + 1) * NORM_GROUP)
                pool.wait_ge(sig["f_veps"], g + 1)
                pool.tensor_tensor(n_rstd[:, cols], n_veps[:, cols], n_half, ALU.pow).then_inc(sig["f_rstd"], 1)


def _layout(inputs):
    a = {k: np.asarray(v) for k, v in inputs.items()}
    d = a["x"].shape[2]
    s = a["x"].shape[1]
    p = 128
    weights = np.concatenate([a["L0_attn_Wq"].T, a["L0_attn_Wk"].T, a["L0_attn_Wv"].T, a["L0_attn_Wo"].T,
                              a["L0_xattn_W_q"], a["L0_xattn_W_k"], a["L0_xattn_W_v"], a["L0_xattn_W_o"]], axis=1)
    heads = a["L0_xattn_lambda_q1"].shape[0]
    lambdas = np.stack([a[f"L0_xattn_lambda_{n}"] for n in ("q1", "k1", "q2", "k2")]).reshape(1, -1)
    idx = np.arange(s)
    seen = np.abs(idx[:, None] - idx[None, :]) <= 32
    seen[0, :] = True
    seen[:, 0] = True
    return {
        "x": a["x"], "ctx": a["ctx_1024"], "mask": a["mask_Bx16xSxS2_ff0"],
        "w_all": weights.reshape(d // p, p, -1).transpose(1, 0, 2),
        "w_scale": np.tile(a["L0_xattn_rms_scale"], heads).reshape(d // p, p).T,
        "lambdas": np.broadcast_to(lambdas, (p, lambdas.size)),
        "phi": a["L0_ffn_phi"].reshape(d // p, p, -1).transpose(1, 0, 2),
        "w_ffn": a["L0_ffn_W"].reshape(-1, d // p, p, d).transpose(0, 2, 1, 3),
        "b_ffn": a["L0_ffn_b"].T.reshape(d // p, p, -1).transpose(1, 0, 2),
        "ident": np.eye(p, dtype=np.float32),
        "band": np.where(seen, np.float32(0), np.float32(-1)).astype(np.float32),
    }


def kernel(**inputs):
    import concourse.bacc as _bacc
    from concourse.bass_utils import run_bass_kernel_spmd as _run

    nc = _bacc.Bacc("TRN2", target_bir_lowering=False, num_devices=1)
    arrays, args = {}, []
    for name, a in _layout(inputs).items():
        a = np.ascontiguousarray(a)
        arrays[f"in_{name}_dram"] = a
        args.append(nc.dram_tensor(f"in_{name}_dram", a.shape, mybir.dt.from_np(a.dtype), kind="ExternalInput").ap())
    out = nc.dram_tensor("out_dram", inputs["x"].shape, mybir.dt.float32, kind="ExternalOutput").ap()
    decoder_layer(nc, *args, out)
    return _run(nc, [arrays], core_ids=[0]).results[0]["out_dram"]
```

```python
import numpy as np
import concourse.bass as bass
from concourse import mybir
from contextlib import ExitStack

HI, LO = 0, 1
PASSES = ((HI, HI), (HI, LO), (LO, HI))


def decoder_layer(nc, x, ctx_in, mask, w_all, w_scale, lambdas, phi, w_ffn, b_ffn, ident_in, band_in, out):
    F32, F16 = mybir.dt.float32, mybir.dt.float16
    ALU, ACT, AX = mybir.AluOpType, mybir.ActivationFunctionType, mybir.AxisListType

    B, S, D = x.shape
    H = mask.shape[1]
    DH = D // H
    P = 128
    DT = D // P
    NP = phi.shape[2]
    E = w_ffn.shape[0]
    SP_E = NP // E
    EC = P // SP_E
    NCH = NP // P
    Q4 = 4
    NQ = B // Q4
    HIGHEST = 3e38
    LN_EPS, RMS_EPS = 1e-5, 1e-5
    LAMBDA_INIT = 0.8
    OUT_SCALE = 1.0 - LAMBDA_INIT
    FAR = 32768.0
    SCORE_SCALE = 1.0 / float(np.sqrt(DH))
    SQ, SK, SV, SO, CQ, CK, CV, CO, W_END = (int(c) for c in np.cumsum([0, D, D, D, D, 2 * D, 2 * D, D, D]))

    scratch_x2 = nc.dram_tensor("scratch_x2", [B, S, D], F32).ap()
    scratch_x2_parts = nc.dram_tensor("scratch_x2_parts", [B, S, 2 * D], F16).ap()

    es = ExitStack()
    with es:
        def sb(name, shape, dt=F32):
            return es.enter_context(nc.sbuf_tensor(name, shape, dt))

        def sem(name):
            return es.enter_context(nc.semaphore(name))

        bank = {n: es.enter_context(nc.psum_tensor(f"bank_{n}", [P, 512], F32))
                for n in ("turn0", "turn1", "score_a", "score_b", "score_s", "prob_c", "prob_s", "value")}

        xT = sb("xT", [P, 2, DT, B * S], F16)
        ident = sb("ident", [P, P])
        ARENA = (207 * 1024 - 2 * DT * B * S * 2 - P * 4) // 4
        arena = sb("arena", [P, ARENA])
        used = [0]

        def carve(shape, dt=F32):
            n = int(np.prod(shape))
            words = n if dt == F32 else (n + 1) // 2
            part = arena[:, used[0]:used[0] + words]
            used[0] += words
            assert used[0] <= ARENA, (used[0], ARENA)
            if dt != F32:
                part = part.bitcast(dt)
            if len(shape) > 1:
                names = "abcdef"[:len(shape)]
                part = part.rearrange(f"p ({' '.join(names)}) -> p {' '.join(names)}", **dict(zip(names, shape)))
            return part

        w_parts = carve([2, DT, W_END], F16)
        c_mask = carve([H, S])
        c_prob = carve([2 * H, S])
        s_prob = carve([H, S])
        STAGES = 5
        w_stage = c_prob.rearrange("p a b -> p (a b)")[:, 0:STAGES * DT * D].rearrange("p (i k n) -> p i k n", i=STAGES, k=DT)
        band = carve([S])
        far16 = carve([S], F16)
        far_ident = carve([P], F16)
        lam_in = carve([4, H, DH])
        lam_prod = carve([2, H, DH])
        lam_sum = carve([2, H])
        lam_exp = carve([2, H])
        lam_dif = carve([H])
        neg_lam = carve([H])
        w_rows = carve([DT])
        w_rows2 = carve([DT])
        s_kbd = carve([2, 8, DT, 2, S], F16)
        c_kbd = carve([8, 2 * DT, 2, S], F16)
        s_in, s_res, c_in = carve([D]), carve([D]), carve([D])
        s_xT, s_oT, c_xT, c_cT, c_oT = (carve([DT, 2, S], F16) for _ in range(5))
        s_qk = carve([2, 4, 2, S], F16)
        c_q, c_k = carve([2, 4, 2, S], F16), carve([4, 2, S], F16)
        s_v, c_v = carve([2, 2, D], F16), carve([2, 2, D], F16)
        s_pT, c_pT = carve([2, 2, Q4, S], F16), carve([2, 2, Q4, S], F16)
        s_negmax, c_negmax = carve([H]), carve([2 * H])
        c_sum, s_expsum = carve([2, 2 * H]), carve([2, H])
        s_rsum, c_rsum, c_r2, c_ratio, c_blend = (carve([H]) for _ in range(5))
        s_o, c_o, c_oraw, c_sq = carve([D]), carve([D]), carve([D]), carve([D])
        c_ss, c_ms, c_rms = carve([H]), carve([H]), carve([H])
        s_sum, c_sumx = carve([D]), carve([D])
        s_total, c_total, s_negmean, c_negmean, s_sq, c_sqx = (carve([1]) for _ in range(6))
        s_junk, c_junk = carve([D]), carve([D])
        s_veps, c_veps, s_rstd, c_rstd = carve([1]), carve([1]), carve([1]), carve([1])
        x1, x2 = carve([D]), carve([D])
        X1_RING = 8
        x1_ring = carve([X1_RING, D])
        x2_parts = carve([2, D], F16)
        fence = carve([3])
        minus_half = carve([H])

        LAG = {"s_pre": 0, "s_proj": 1, "s_core": 2, "s_late": 3, "s_tail": 4,
               "c_pre": 4, "c_proj": 5, "c_core": 6, "c_late": 7, "c_tail": 8}
        STEPS = B + max(LAG.values())
        FIRST_FULL = max(LAG.values()) + 1
        UNITS = range(H // Q4)
        assert len(UNITS) == 4

        def earlier(slot, back):
            return (slot - back, "core") if slot >= back else (slot - back + 4, "late")

        def in_slots(back, *kinds):
            return [(f"{a}{earlier(i, back)[0]}", f"{a[0]}_{earlier(i, back)[1]}") for i in range(4) for a in kinds]

        TURN = [("s_oT", "s_tail"), ("c_oT", "c_tail"), ("s_qk", "s_proj"),
                ("s_wo", "s_tail"), ("c_wo", "c_tail"), ("c_q", "c_proj"),
                ("c_k", "c_proj"), ("s_v", "s_proj"), ("c_v", "c_proj"),
                ("s_xT", "s_pre"), ("c_cT", "c_pre"), ("x1T", "s_tail"), ("x2T", "c_tail")]
        ORDER = {
            "turn": TURN,
            "turn_hi": [e for e in TURN if e[0] not in ("s_wo", "c_wo")],
            "c_score": [(f"c{h}{u}", "c_core") for u in UNITS for h in "ab"],
            "s_score": in_slots(0, "s"),
            "blend": in_slots(1, "c"),
            "c_prob": in_slots(2, "c"),
            "s_prob": in_slots(2, "s"),
            "value": in_slots(3, "c", "s"),
        }

        class Step:

            def __init__(self, t, behind=0, multiples=None):
                self.t, self.behind, self.multiples = t, behind, {} if multiples is None else multiples
                self.known = isinstance(t, int)

            def on(self, part):
                return not self.known or 0 <= self.b(part) < B

            def b(self, part):
                return self.t - (self.behind + LAG[part])

            def slot(self, order, use):
                live = [u for u, part in ORDER[order] if self.on(part)]
                return live.index(use)

            def before(self, order, use, ring):
                uses = [u for u, _ in ORDER[order]]
                place = uses.index(use) % ring
                step = self
                ahead = uses[:uses.index(use)]
                while True:
                    live = [u for u, part in ORDER[order] if u in ahead and uses.index(u) % ring == place and step.on(part)]
                    if live:
                        return step.count(order, live[-1])
                    if step.known and step.t <= step.behind:
                        return 0
                    step, ahead = step.last(), uses

            def count(self, order, use):
                parts = [part for _, part in ORDER[order]]
                if self.known:
                    before = sum(min(max(self.b(p), 0), B) for p in parts)
                    return before + self.slot(order, use) + 1
                n = len(parts)
                if n not in self.multiples:
                    self.multiples[n] = self.t * n
                return self.multiples[n] + (self.slot(order, use) + 1 - self.behind * n - sum(LAG[p] for p in parts))

            def slot_of(self, part):
                b = self.b(part)
                return bass.ds(b % 2, 1)

            def made(self, order, use, kind):
                same = dict(ORDER[order])[use].endswith(kind)
                return (self if same else self.last()).count(order, use)

            def last(self):
                return Step(self.t, self.behind + 1, self.multiples)

        def steps(e, body):
            for t in range(min(FIRST_FULL, STEPS)):
                body(Step(t))
            if FIRST_FULL < B:
                with e.Fori(FIRST_FULL, B) as t:
                    body(Step(t))
            for t in range(max(B, FIRST_FULL), STEPS):
                body(Step(t))

        sig = {name: sem(name) for name in '''
            constants_in weights_in0 weights_in1 weights_in2 weights_in3 weights_in4 s_in s_res c_in c_mask0 c_mask1 c_mask2 c_mask3 far_ident far16 x2_stored x2_parts_stored
            lam_prod lam_sum lam_exp lam_dif neg_lam w_rows2 weights_scaled weights_hi weights_lo zeros
            turn_written turn_hi turn_read c_score_written c_score_read s_score_written
            c_prob_written c_prob_hi c_prob_read s_prob_written s_prob_hi s_prob_read value_written c_value_read
            s_kbd_zero c_kbd_zero s_kbd c_kbd0 c_kbd1 s_max s_exp c_exp c_r2 c_ratio c_blend scaled blended
            s_rsum s_o c_rsum c_sq c_ss c_ms c_rms c_o s_summed s_squares s_veps s_rstd x1 x1_kept
            c_summed c_squares c_veps c_rstd x2 x2_hi x2_parts
            f_cleared f_acc_zero f_zero f_half f_bias_in f_phi_in f_phi_hi f_phi_lo f_w_in0 f_w_in1 f_w_hi f_w_lo f_x0 f_x1 f_x2 f_x3
            f_logits f_logits_read f_max4 f_max4_reset f_chunkmax f_max f_newmax f_rowmax f_neg f_diff f_keep f_kept f_row_sum
            f_shifted_pool f_shifted_dve f_sum_exp f_sum4 f_sum f_rsum f_d_shifted f_d_exp f_dispatch f_dispatch_hi f_dispatch_lo
            f_slots0 f_slots1 f_slots2 f_slots_psum f_slots_hi f_slots_lo f_combine f_cT_psum f_cT_hi f_cT_lo
            f_yT_psum f_yT f_y_psum f_y_hi f_y_lo f_out f_acc
            f_res0 f_res1 f_res2 f_res3 f_n_rsum f_added f_negmean f_squares f_veps f_rstd f_normed out_stored'''.split()}

        def later(n):
            return not isinstance(n, int) or n > 0

        def in3(ap, a):
            return ap.rearrange("p (a n) -> p a n", a=a)

        def spread(ap, n):
            return ap.unsqueeze(2).broadcast_to([P, ap.shape[1], n])

        def batch(dram, b):
            return dram[bass.ds(b, 1), :, :].rearrange("o s d -> (o s) d")

        PIECE = D
        NPIECE = W_END // PIECE
        DMA = 16


        used[0] = 0
        acc = carve([B, D])
        logits = carve([B, S])
        f_w_stage = carve([2, DT, D])
        f_w = carve([2, DT, EC, D], F16)
        f_phi_stage = carve([DT, P])
        f_phi = carve([2, DT, P], F16)
        f_bias = carve([DT, NCH * EC])
        f_x = carve([Q4, 2, D], F16)
        f_dp = carve([2, Q4, P], F16)
        RING = 4
        f_ring = carve([RING, Q4, P])
        f_cT = carve([2, 2, Q4, S], F16)
        f_shared = carve([DT * Q4 * P])
        f_slT = f_shared.bitcast(F16).rearrange("p (h e q n) -> p h e q n", h=2, e=DT, q=Q4)
        f_sum4 = f_shared[:, 0:Q4 * P].rearrange("p (q n) -> p q n", q=Q4)
        assert RING == 2 + DT
        f_yT = f_ring[:, 2:RING]
        f_y = carve([2, Q4, D], F16)
        f_max4 = carve([Q4, P])
        f_max, f_sum, f_rsum = carve([P]), carve([P]), carve([P])
        f_chunkmax, f_rowmax, f_newmax, f_neg, f_diff, f_keep = (carve([B]) for _ in range(6))
        f_csum, f_kept, n_sum = (carve([B]) for _ in range(3))
        n_half = carve([16])
        F_LAST = NQ + 3
        ROUNDS = NQ // RING
        EARLY_EXPERTS = 2
        ROUND_EXPERTS = [[x_ for x_ in range(EARLY_EXPERTS, EC) if (x_ - EARLY_EXPERTS + 1) * ROUNDS // (EC - EARLY_EXPERTS) - 1 == i]
                         for i in range(ROUNDS)]

        class Quad:

            def __init__(self, c, k):
                self.c, self.k = c, k

            def on(self, lag):
                return not isinstance(self.k, int) or 0 <= self.k - lag < NQ

            def done(self, lag, each=1):
                return self.c * (NQ * each) + (self.k - lag + 1) * each

        def quads(e, c, body):
            for k in range(min(3, F_LAST)):
                body(Quad(c, k))
            if NQ > 3:
                with e.Fori(3, NQ) as k:
                    body(Quad(c, k))
            for k in range(max(NQ, 3), F_LAST):
                body(Quad(c, k))

        def chunks(e, body):
            if NCH > 1:
                with e.Fori(0, NCH - 1) as c:
                    body(c, True)
            body(NCH - 1, False)

        def one(ap):
            return ap.rearrange("p o n -> p (o n)")

        def one4(ap):
            return ap.rearrange("p o a b -> p (o a) b")

        DISPATCH, COMBINE = 0, 1
        names = ("turn0", "turn1", "score_a", "score_b", "score_s", "prob_c", "prob_s", "value")
        b_turn, b_slots, b_yT, b_y, b_out = (bank[names[0]], [bank[n] for n in names[1:3]], [bank[n] for n in names[3:5]],
                                             bank[names[5]], [bank[n] for n in names[6:8]])
        used[0] = B * D
        res_ring = carve([4, Q4, D])
        norm_junk = carve([2, D])
        n_rsum, n_total, n_negmean, n_squares, n_veps, n_rstd = (carve([B]) for _ in range(6))
        NORM_GROUP = 16

        block = es.enter_context(nc.Block())

        @block.sync
        def _(sp):
            for dst, src in ((ident[:, :], ident_in), (band, band_in), (w_rows, w_scale),
                             (lam_in.rearrange("p a b c -> p (a b c)"), lambdas)):
                sp.dma_start(dst, src).then_inc(sig["constants_in"], DMA)
            for i in range(NPIECE):
                if i >= STAGES:
                    sp.wait_ge(sig["weights_lo"], i - STAGES + 1)
                sp.dma_start(w_stage[:, i % STAGES], w_all[:, :, i * PIECE:(i + 1) * PIECE]).then_inc(sig[f"weights_in{i % STAGES}"], DMA)

            sp.wait_ge(sig["s_kbd_zero"], 1)
            sp.wait_ge(sig["c_kbd_zero"], 1)

            def load_mask(st, u):
                if st.on("c_proj"):
                    b = st.b("c_proj")
                    if later(b):
                        sp.wait_ge(sig["c_score_read"], st.count("c_score", f"cb{u}"))
                    sp.dma_start(c_mask[:, u * Q4:(u + 1) * Q4, :],
                                     mask[bass.ds(b, 1), u * Q4:(u + 1) * Q4, :, :].rearrange("o h q k -> q (o h) k")).then_inc(sig[f"c_mask{u}"], DMA)

            def cross_keys(half):
                tiles = slice(2 * half, 2 * half + 2)
                for r in range(8):
                    rows = slice(r * P // 8, (r + 1) * P // 8)
                    sp.dma_start(c_kbd[rows, r, tiles].rearrange("p a b s -> p (a b s)"),
                                     c_k[rows, tiles].rearrange("p a b s -> p (a b s)")).then_inc(sig[f"c_kbd{half}"], DMA)

            def body(st):
                if st.on("s_pre"):
                    b = st.b("s_pre")
                    if later(b):
                        sp.wait_ge(sig["turn_written"], st.last().count("turn", "s_xT"))
                    sp.dma_start(s_in, batch(x, b)).then_inc(sig["s_in"], DMA)
                if st.on("c_pre"):
                    b = st.b("c_pre")
                    if later(b):
                        sp.wait_ge(sig["turn_written"], st.last().count("turn", "c_cT"))
                    sp.dma_start(c_in, batch(ctx_in, b)).then_inc(sig["c_in"], DMA)
                if st.on("s_tail"):
                    b = st.b("s_tail")
                    if later(b):
                        sp.wait_ge(sig["s_summed"], b)
                    sp.dma_start(s_res, batch(x, b)).then_inc(sig["s_res"], DMA)
                load_mask(st, 0)
                if st.on("s_proj"):
                    sp.wait_ge(sig["turn_read"], st.count("turn", "s_qk"))
                    for r in range(8):
                        rows = slice(r * P // 8, (r + 1) * P // 8)
                        sp.dma_start(s_kbd[rows, st.slot_of("s_proj"), r].rearrange("p o a b s -> p (o a b s)"),
                                         s_qk[rows, st.slot_of("s_proj"), 2:4].rearrange("p o a b s -> p (o a b s)")).then_inc(sig["s_kbd"], DMA)
                load_mask(st, 1)
                if st.on("c_proj"):
                    sp.wait_ge(sig["turn_read"], st.count("turn", "c_k"))
                    cross_keys(0)
                load_mask(st, 2)
                if st.on("c_proj"):
                    if st.on("c_core"):
                        sp.wait_ge(sig["c_score_written"], st.count("c_score", "cb3"))
                    cross_keys(1)
                if st.on("c_tail"):
                    b = st.b("c_tail")
                    sp.wait_ge(sig["x2"], b + 1)
                    sp.dma_start(batch(scratch_x2, b), x2).then_inc(sig["x2_stored"], DMA)
                    sp.wait_ge(sig["x2_parts"], b + 1)
                    sp.dma_start(batch(scratch_x2_parts, b), x2_parts.rearrange("p a d -> p (a d)")).then_inc(sig["x2_parts_stored"], DMA)
                load_mask(st, 3)

            steps(sp, body)
            sp.wait_ge(sig["x2_stored"], DMA * B)
            sp.wait_ge(sig["x2_parts_stored"], DMA * B)

            sp.wait_ge(sig["f_cleared"], 3)
            sp.dma_start(f_bias, b_ffn).then_inc(sig["f_bias_in"], DMA)
            sp.dma_start(f_phi_stage, phi[:, :, 0:P]).then_inc(sig["f_phi_in"], DMA)

            def load_expert(n, slot):
                sp.dma_start(f_w_stage[:, slot], w_ffn[bass.ds(n, 1), :, :, :].rearrange("o p k e -> p (o k) e")).then_inc(sig[f"f_w_in{slot}"], DMA)

            def load_x(b, j):
                sp.dma_start(f_x[:, j].rearrange("p a d -> p (a d)"), batch(scratch_x2_parts, b)).then_inc(sig[f"f_x{j}"], DMA)

            load_expert(0, 0)
            load_expert(1, 1)
            for j in range(Q4):
                load_x(j, j)

            def sp_chunk(c, more):
                if more:
                    sp.wait_ge(sig["f_phi_lo"], c + 1)
                    sp.dma_start(f_phi_stage, phi[:, :, bass.ds((c + 1) * P, P)]).then_inc(sig["f_phi_in"], DMA)
                for j in range(EC if more else EC - 2):
                    sp.wait_ge(sig["f_w_lo"], c * EC + j + 1)
                    load_expert(c * EC + j + 2, j % 2)
                with sp.Fori(0, NQ if more else NQ - 1) as g:
                    for j in range(Q4):
                        if j < Q4 - 1:
                            sp.wait_ge(sig[f"f_slots{j}"], c * NQ + g + 1)
                        else:
                            sp.wait_ge(sig["f_slots_psum"], 2 * (c * NQ + g + 1))
                        load_x((g + 1) % NQ * Q4 + j, j)

            chunks(sp, sp_chunk)
            sp.wait_ge(sig["f_combine"], NCH * NQ)
            for g in range(NQ):
                if g >= 4:
                    sp.wait_ge(sig["f_added"], Q4 * (g - 3))
                sp.dma_start(res_ring[:, g % 4], scratch_x2[g * Q4:(g + 1) * Q4].rearrange("b s d -> s b d")).then_inc(sig[f"f_res{g % 4}"], DMA)
            for g in range(B // NORM_GROUP):
                sp.wait_ge(sig["f_normed"], NORM_GROUP * (g + 1))
                sp.dma_start(out[g * NORM_GROUP:(g + 1) * NORM_GROUP].rearrange("b s d -> s b d"),
                                 acc[:, g * NORM_GROUP:(g + 1) * NORM_GROUP, :]).then_inc(sig["out_stored"], DMA)
            sp.wait_ge(sig["out_stored"], DMA * (B // NORM_GROUP))

        @block.tensor
        def _(pe):
            pe.wait_ge(sig["weights_lo"], NPIECE)
            pe.wait_ge(sig["zeros"], 2)
            pe.wait_ge(sig["far_ident"], 1)
            pe.wait_ge(sig["far16"], 1)

            def body(st):
                s, c = "s", "c"

                def turn_bank(use, step=st):
                    others = step.before("turn", use, 2)
                    if later(others):
                        pe.wait_ge(sig["turn_read"], others)
                    return bank[f"turn{[u for u, _ in TURN].index(use) % 2}"]

                def turn(use, src, step=st):
                    dst = turn_bank(use, step)
                    for k in range(DT):
                        last = nc.tensor.transpose(dst[:, k * P:(k + 1) * P], src[:, k * P:(k + 1) * P], ident[:, :])
                    last.then_inc(sig["turn_written"], 1)

                def project_T(use, col, src):
                    dst = turn_bank(use)
                    for o in range(4):
                        for k in range(DT):
                            for n, (a, p) in enumerate(PASSES):
                                last = nc.tensor.matmul(dst[:, o * S:(o + 1) * S], w_parts[:, a, k, col + o * P:col + (o + 1) * P],
                                                        src[:, k, p, :], start=k + n == 0, stop=k == DT - 1 and n == 2)
                    last.then_inc(sig["turn_written"], 1)

                def project(use, col, src):
                    dst = turn_bank(use)
                    for k in range(DT):
                        for n, (a, p) in enumerate(PASSES):
                            last = nc.tensor.matmul(dst[:, 0:D], src[:, k, a, :], w_parts[:, p, k, col:col + D],
                                                    start=k + n == 0, stop=k == DT - 1 and n == 2)
                    last.then_inc(sig["turn_written"], 1)

                def self_scores(u):
                    if not st.on("s_core"):
                        return
                    before = st.before("s_score", f"s{u}", 1)
                    if later(before):
                        pe.wait_ge(sig["s_exp"], before)
                    if u == 0:
                        pe.wait_ge(sig["s_kbd"], 8 * DMA * (st.b("s_core") + 1))
                    slot, tile, r = st.slot_of("s_core"), u // 2, 4 * (u % 2)
                    for n, (a, p) in enumerate(PASSES):
                        nc.tensor.matmul(bank["score_s"][:, :], s_qk[:, slot, tile, a, :].rearrange("p o s -> p (o s)"),
                                         s_kbd[:, slot, r:r + 4, tile, p, :].rearrange("p o r k -> p (o r) k"), start=n == 0, stop=False)
                    nc.tensor.matmul(in3(bank["score_s"][:, :], Q4), far_ident, far16.unsqueeze(1).broadcast_to([P, Q4, S]),
                                     start=False, stop=True).then_inc(sig["s_score_written"], 1)

                def cross_scores(u, half):
                    if not st.on("c_core"):
                        return
                    use, name = (f"ca{u}", "score_a") if half == 0 else (f"cb{u}", "score_b")
                    before = st.before("c_score", use, 2)
                    if later(before):
                        pe.wait_ge(sig["c_score_read"], before)
                    if half == 0 and u % 2 == 0:
                        pe.wait_ge(sig[f"c_kbd{u // 2}"], 8 * DMA * (st.b("c_core") + 1))
                    for n, (a, p) in enumerate(PASSES):
                        last = nc.tensor.matmul(bank[name][:, :], c_q[:, st.slot_of("c_core"), u, a, :].rearrange("p o s -> p (o s)"),
                                                c_kbd[:, 4 * half:4 * half + 4, u, p, :], start=n == 0, stop=n == 2)
                    last.then_inc(sig["c_score_written"], 1)

                def turn_probs(which, slot):
                    u, kind = earlier(slot, 2)
                    if not st.on(f"{which}_{kind}"):
                        return
                    use = f"{which}{u}"
                    before = st.count(f"{which}_prob", use) - 1
                    if later(before):
                        pe.wait_ge(sig[f"{which}_prob_read"], before)
                    if which == c:
                        pe.wait_ge(sig["blended"], st.made("blend", use, kind))
                        src, stride = c_prob, 2
                    else:
                        pe.wait_ge(sig["s_exp"], st.made("s_score", use, kind))
                        src, stride = s_prob, 1
                    for j in range(Q4):
                        last = nc.tensor.transpose(bank[f"prob_{which}"][:, j * S:(j + 1) * S], src[:, (u * Q4 + j) * stride, :], ident[:, :])
                    last.then_inc(sig[f"{which}_prob_written"], 1)

                def values(slot):
                    u, kind = earlier(slot, 3)
                    if u == 0:
                        if st.on("c_late"):
                            pe.wait_ge(sig["c_value_read"], st.b("c_late") + 1)
                        if st.on("s_late"):
                            pe.wait_ge(sig["s_o"], st.b("s_late") + 1)
                    for which, pT, v, col in ((c, c_pT, c_v, 0), (s, s_pT, s_v, D)):
                        if not st.on(f"{which}_{kind}"):
                            continue
                        pe.wait_ge(sig[f"{which}_prob_read"], st.made(f"{which}_prob", f"{which}{u}", kind))
                        place = st.slot_of(f"{which}_{kind}")
                        for j in range(Q4):
                            h = u * Q4 + j
                            for n, (a, p) in enumerate(PASSES):
                                last = nc.tensor.matmul(bank["value"][:, col + h * DH:col + (h + 1) * DH], pT[:, u % 2, a, j, :],
                                                        v[:, place, p, h * DH:(h + 1) * DH].rearrange("p o d -> p (o d)"), start=n == 0, stop=n == 2)
                        last.then_inc(sig["value_written"], 1)

                def turn_normed(step):
                    if step.on("s_tail"):
                        pe.wait_ge(sig["x1"], step.b("s_tail") + 1)
                        turn("x1T", x1, step)
                    if step.on("c_tail"):
                        pe.wait_ge(sig["x2"], step.b("c_tail") + 1)
                        turn("x2T", x2, step)

                def slot_start(u):
                    turn_probs(c, u)
                    turn_probs(s, u)

                def first_scores(u):
                    self_scores(u)
                    cross_scores(u, 0)

                first_scores(0)
                turn_normed(st.last())
                slot_start(0)
                if st.on("s_tail"):
                    pe.wait_ge(sig["s_o"], st.b("s_tail") + 1)
                    turn("s_oT", s_o)
                cross_scores(0, 1)
                values(0)
                first_scores(1)
                if st.on("c_tail"):
                    pe.wait_ge(sig["c_o"], st.b("c_tail") + 1)
                    turn("c_oT", c_o)
                if st.on("s_proj"):
                    pe.wait_ge(sig["turn_read"], st.last().count("turn", "s_xT"))
                    project_T("s_qk", SQ, s_xT)
                slot_start(1)
                if st.on("s_tail"):
                    pe.wait_ge(sig["turn_read"], st.count("turn", "s_oT"))
                    project("s_wo", SO, s_oT)
                cross_scores(1, 1)
                values(1)
                first_scores(2)
                if st.on("c_tail"):
                    pe.wait_ge(sig["turn_read"], st.count("turn", "c_oT"))
                    project("c_wo", CO, c_oT)
                if st.on("c_proj"):
                    pe.wait_ge(sig["turn_read"], st.last().count("turn", "x1T"))
                    project_T("c_q", CQ, c_xT)
                slot_start(2)
                if st.on("c_proj"):
                    pe.wait_ge(sig["turn_read"], st.last().count("turn", "c_cT"))
                    project_T("c_k", CK, c_cT)
                cross_scores(2, 1)
                values(2)
                first_scores(3)
                if st.on("s_proj"):
                    project("s_v", SV, s_xT)
                if st.on("c_proj"):
                    project("c_v", CV, c_cT)
                slot_start(3)
                cross_scores(3, 1)
                if st.on("s_pre"):
                    pe.wait_ge(sig["s_in"], DMA * (st.b("s_pre") + 1))
                    turn("s_xT", s_in)
                if st.on("c_pre"):
                    pe.wait_ge(sig["c_in"], DMA * (st.b("c_pre") + 1))
                    turn("c_cT", c_in)
                values(3)

            steps(pe, body)
            body(Step(STEPS))

            mm = nc.tensor.matmul
            pe.wait_ge(sig["f_cleared"], 3)

            def pe_logits(g, js):
                for j in js:
                    for k in range(DT):
                        for n, (a, c_) in enumerate(PASSES):
                            last = mm(b_turn[:, j * P:(j + 1) * P], xT[:, a, k, bass.ds((g * Q4 + j) * S, S)], f_phi[:, c_, k, :],
                                      start=k + n == 0, stop=k == DT - 1 and n == 2)
                return last

            pe.wait_ge(sig["f_phi_lo"], 1)
            pe_logits(0, range(Q4)).then_inc(sig["f_logits"], 1)
            with pe.Fori(1, NQ) as g:
                pe.wait_ge(sig["f_logits_read"], g)
                pe_logits(g, range(Q4)).then_inc(sig["f_logits"], 1)

            def pe_chunk(c, more):
                pe.wait_ge(sig["f_w_lo"], c * EC + EC)
                if more:
                    pe.wait_ge(sig["f_phi_lo"], c + 2)

                def body(st):
                    k = st.k

                    def turn_y(half):
                        if st.on(3):
                            if half == 0:
                                pe.wait_ge(sig["f_yT"], st.done(3, 2))
                            else:
                                pe.wait_ge(sig["f_y_lo"], st.done(3, 2) - 1)
                            for j in (2 * half, 2 * half + 1):
                                for e in range(DT):
                                    col = (j % 2) * D + e * P
                                    last = nc.tensor.transpose(b_y[:, col:col + P], f_yT[:, e, j, :], ident[:, :])
                            last.then_inc(sig["f_y_psum"], 1)

                    def out_product(pair):
                        if not st.on(3):
                            return
                        if pair == 0:
                            pe.wait_ge(sig["f_y_lo"], st.done(3, 2))
                            pe.wait_ge(sig["f_cT_lo"], st.done(3))
                        pe.wait_ge(sig["f_acc"], st.done(3, 2) - 1 + pair)
                        slot = bass.ds((k - 3) % 2, 1)
                        for j in (2 * pair, 2 * pair + 1):
                            for n, (a, c_) in enumerate(PASSES):
                                last = mm(b_out[pair][:, (j % 2) * D:(j % 2 + 1) * D], one(f_cT[:, slot, a, j, :]), f_y[:, c_, j, :],
                                          start=n == 0, stop=n == 2)
                        last.then_inc(sig["f_out"], 1)

                    def experts(e):
                        if st.on(2):
                            pe.wait_ge(sig["f_slots_lo"], st.done(2, 2))
                            for x_ in range(EC):
                                for kk in range(DT):
                                    for n, (a, c_) in enumerate(PASSES):
                                        last = mm(b_yT[e][:, :].rearrange("p (b s) -> p b s", b=Q4)[:, :, x_ * SP_E:(x_ + 1) * SP_E],
                                                  f_w[:, a, kk, x_, e * P:(e + 1) * P], f_slT[:, c_, kk, :, x_ * SP_E:(x_ + 1) * SP_E],
                                                  start=kk + n == 0, stop=kk == DT - 1 and n == 2)
                            last.then_inc(sig["f_yT_psum"], 1)

                    turn_y(0)
                    experts(0)
                    if st.on(2):
                        pe.wait_ge(sig["f_combine"], st.done(2))
                        before = k - 2 if not isinstance(k, int) else max(k - 2, 0)
                        pe.wait_ge(sig["f_logits_read"], (c + 1) * NQ + (before if more else 0))
                        if st.on(3) and not more:
                            pe.wait_ge(sig["f_cT_lo"], st.done(3))
                        for j in range(Q4):
                            last = nc.tensor.transpose(b_turn[:, j * S:(j + 1) * S], f_ring[:, COMBINE, j, :], ident[:, :])
                        last.then_inc(sig["f_cT_psum"], 1)
                    turn_y(1)
                    experts(1)
                    if st.on(1):
                        pe.wait_ge(sig["f_dispatch_lo"], st.done(1))
                        for e in range(DT):
                            for j in range(Q4):
                                if e == 0:
                                    pe.wait_ge(sig[f"f_x{j}"], DMA * st.done(1))
                                for n, (a, c_) in enumerate(PASSES):
                                    last = mm(b_slots[e][:, j * P:(j + 1) * P], f_x[:, j, a, e * P:(e + 1) * P], f_dp[:, c_, j, :],
                                              start=n == 0, stop=n == 2)
                                if e == DT - 1 and j < Q4 - 1:
                                    last.then_inc(sig[f"f_slots{j}"], 1)
                            last.then_inc(sig["f_slots_psum"], 1)
                    if st.on(2) and more:
                        pe.wait_ge(sig["f_cT_lo"], st.done(2))
                        pe_logits(k - 2, range(Q4)).then_inc(sig["f_logits"], 1)
                    out_product(0)
                    out_product(1)
                quads(pe, c, body)

            chunks(pe, pe_chunk)

        @block.scalar
        def _(act):
            act.wait_ge(sig["constants_in"], DMA * 4)
            act.wait_ge(sig["lam_sum"], 1)
            nc.scalar.activation(lam_exp.rearrange("p a b -> p (a b)"), lam_sum.rearrange("p a b -> p (a b)"), ACT.Exp).then_inc(sig["lam_exp"], 1)
            for i in range(NPIECE):
                act.wait_ge(sig["weights_scaled"], i + 1)
                nc.scalar.activation(w_parts[:, HI, :, i * PIECE:(i + 1) * PIECE], w_stage[:, i % STAGES], ACT.Copy).then_inc(sig["weights_hi"], 1)

            def body(st):
                def hi_turn(use, dst, tiles):
                    src = bank[f"turn{[u for u, _ in TURN].index(use) % 2}"]
                    act.wait_ge(sig["turn_written"], st.count("turn", use))
                    nc.scalar.activation(dst, in3(src[:, 0:tiles * P], tiles), ACT.Copy).then_inc(sig["turn_hi"], 1)

                def squares(part, b, junk, summed, negmean, total):
                    act.wait_ge(sig[f"{part}_summed"], b + 1)
                    nc.scalar.activation(junk, summed, ACT.Square, bias=negmean, accum_out=total).then_inc(sig[f"{part}_squares"], 1)

                def cross_exps(u, half):
                    if st.on("c_core"):
                        act.wait_ge(sig["c_score_read"], st.count("c_score", f"c{'ab'[half]}{u}"))
                        g = 2 * u + half
                        for r in range(4 * g, 4 * g + 4):
                            last = nc.scalar.activation(c_prob[:, r, :], c_prob[:, r, :], ACT.Exp,
                                                        bias=c_negmax[:, r:r + 1], scale=-1.0, accum_out=one(c_sum[:, st.slot_of("c_core"), r:r + 1]))
                        last.then_inc(sig["c_exp"], 1)

                def self_exps(u):
                    if st.on("s_core"):
                        act.wait_ge(sig["s_max"], st.count("s_score", f"s{u}"))
                        for j in range(Q4):
                            h = u * Q4 + j
                            last = nc.scalar.activation(s_prob[:, h, :], bank["score_s"][:, j * S:(j + 1) * S], ACT.Exp,
                                                        bias=s_negmax[:, h:h + 1], accum_out=one(s_expsum[:, st.slot_of("s_core"), h:h + 1]))
                        last.then_inc(sig["s_exp"], 1)

                def prob_hi(which, slot):
                    u, kind = earlier(slot, 2)
                    if st.on(f"{which}_{kind}"):
                        pT = c_pT if which == "c" else s_pT
                        act.wait_ge(sig[f"{which}_prob_written"], st.count(f"{which}_prob", f"{which}{u}"))
                        nc.scalar.activation(pT[:, u % 2, HI, :, :], in3(bank[f"prob_{which}"][:, :], Q4), ACT.Copy).then_inc(sig[f"{which}_prob_hi"], 1)

                def q_like(buf, part):
                    return buf[:, st.slot_of(part), :, HI, :].rearrange("p o a s -> p (o a) s")

                def v_like(buf, part):
                    return in3(buf[:, st.slot_of(part), HI, :].rearrange("p o d -> p (o d)"), DT)

                def slot_start(u):
                    prob_hi("c", u)
                    self_exps(u)
                    prob_hi("s", u)
                    cross_exps(u, 0)

                slot_start(0)
                if st.on("s_tail"):
                    hi_turn("s_oT", s_oT[:, :, HI], DT)
                cross_exps(0, 1)
                if st.on("c_tail"):
                    hi_turn("c_oT", c_oT[:, :, HI], DT)
                if st.on("s_proj"):
                    hi_turn("s_qk", q_like(s_qk, "s_proj"), 4)
                slot_start(1)
                if st.on("s_tail"):
                    squares("s", st.b("s_tail"), s_junk, s_sum, s_negmean, s_sq)
                cross_exps(1, 1)
                if st.on("c_proj"):
                    hi_turn("c_q", q_like(c_q, "c_proj"), 4)
                slot_start(2)
                if st.on("c_tail"):
                    squares("c", st.b("c_tail"), c_junk, c_sumx, c_negmean, c_sqx)
                if st.on("c_proj"):
                    hi_turn("c_k", c_k[:, :, HI], 4)
                cross_exps(2, 1)
                if st.on("s_proj"):
                    hi_turn("s_v", v_like(s_v, "s_proj"), DT)
                if st.on("c_proj"):
                    hi_turn("c_v", v_like(c_v, "c_proj"), DT)
                prob_hi("c", 3)
                self_exps(3)
                if st.on("s_pre"):
                    hi_turn("s_xT", s_xT[:, :, HI], DT)
                if st.on("c_pre"):
                    hi_turn("c_cT", c_cT[:, :, HI], DT)
                prob_hi("s", 3)
                cross_exps(3, 0)
                if st.on("s_tail"):
                    b = st.b("s_tail")
                    act.wait_ge(sig["x1"], b + 1)
                    nc.scalar.activation(x1_ring[:, bass.ds(b % X1_RING, 1), :].rearrange("p o d -> p (o d)"), x1, ACT.Copy).then_inc(sig["x1_kept"], 1)
                cross_exps(3, 1)
                if st.on("c_tail"):
                    b = st.b("c_tail")
                    act.wait_ge(sig["x2"], b + 1)
                    if later(b):
                        act.wait_ge(sig["x2_parts_stored"], DMA * b)
                    nc.scalar.activation(x2_parts[:, HI, :], x2, ACT.Copy).then_inc(sig["x2_hi"], 1)
                if st.on("s_tail"):
                    hi_turn("x1T", c_xT[:, :, HI], DT)
                if st.on("c_tail"):
                    hi_turn("x2T", xT[:, HI, :, bass.ds(st.b("c_tail") * S, S)], DT)

            steps(act, body)

            EXP, COPY = ACT.Exp, ACT.Copy
            nc.scalar.activation(fence[:, 0:1], neg_lam[:, 0:1], COPY).then_inc(sig["f_cleared"], 1)

            def flat(ap):
                return ap.rearrange("p a b -> p (a b)")

            def act_phi(n):
                act.wait_ge(sig["f_phi_in"], DMA * n)
                nc.scalar.activation(f_phi[:, HI], f_phi_stage, COPY).then_inc(sig["f_phi_hi"], 1)

            def act_logits(g, n):
                act.wait_ge(sig["f_logits"], n)
                nc.scalar.activation(logits[:, bass.ds(g * Q4, Q4), :], in3(b_turn[:, :], Q4), COPY).then_inc(sig["f_logits_read"], 1)

            act.wait_ge(sig["f_cleared"], 3)
            act_phi(1)
            with act.Fori(0, NQ) as g:
                act_logits(g, g + 1)

            def expert_hi(c, x_):
                act.wait_ge(sig[f"f_w_in{x_ % 2}"], DMA * (c * (EC // 2) + x_ // 2 + 1))
                nc.scalar.activation(f_w[:, HI, :, x_, :], f_w_stage[:, x_ % 2], COPY).then_inc(sig["f_w_hi"], 1)

            for x_ in range(EARLY_EXPERTS):
                expert_hi(0, x_)

            def act_chunk(c, more):
                for i in range(ROUNDS):
                    for r in range(RING):
                        if r % 2 == 0:
                            act.wait_ge(sig["f_shifted_pool"], c * (NQ // 2) + (RING * i + r) // 2 + 1)
                        else:
                            act.wait_ge(sig["f_shifted_dve"], c * (NQ // 2) + (RING * i + r) // 2 + 1)
                        nc.scalar.activation(flat(f_ring[:, r]), flat(f_ring[:, r]), EXP).then_inc(sig["f_sum_exp"], 1)
                    for x_ in ROUND_EXPERTS[i]:
                        expert_hi(c, x_)
                if more:
                    act_phi(c + 2)
                act.wait_ge(sig["f_diff"], c + 1)
                nc.scalar.activation(f_keep, f_diff, EXP).then_inc(sig["f_keep"], 1)

                def body(st):
                    k = st.k

                    def y_hi(half):
                        if st.on(3):
                            act.wait_ge(sig["f_y_psum"], st.done(3, 2) - 1 + half)
                            nc.scalar.activation(f_y[:, HI, 2 * half:2 * half + 2, :], in3(b_y[:, :], 2), COPY).then_inc(sig["f_y_hi"], 1)

                    y_hi(0)
                    if st.on(0):
                        act.wait_ge(sig["f_d_shifted"], st.done(0))
                        nc.scalar.activation(flat(f_ring[:, DISPATCH]), flat(f_ring[:, DISPATCH]), EXP).then_inc(sig["f_d_exp"], 1)
                    if st.on(2):
                        act.wait_ge(sig["f_cT_psum"], st.done(2))
                        nc.scalar.activation(f_cT[:, bass.ds((k - 2) % 2, 1), HI, :, :].rearrange("p o a b -> p (o a b)"), b_turn[:, :], COPY).then_inc(sig["f_cT_hi"], 1)
                    if more and isinstance(k, int) and k == F_LAST - 1:
                        for x_ in range(EARLY_EXPERTS):
                            expert_hi(c + 1, x_)
                    y_hi(1)
                    if st.on(1):
                        act.wait_ge(sig["f_neg"], c + 1)
                        for j in range(Q4):
                            b = bass.ds((k - 1) * Q4 + j, 1)
                            last = nc.scalar.activation(f_ring[:, COMBINE, j], one(logits[:, b, :]), EXP, bias=f_neg[:, b], accum_out=f_csum[:, b])
                        last.then_inc(sig["f_combine"], 1)
                        for e in range(DT):
                            act.wait_ge(sig["f_slots_psum"], st.done(1, 2) - 1 + e)
                            nc.scalar.activation(f_slT[:, HI, e], in3(b_slots[e][:, :], Q4), COPY).then_inc(sig["f_slots_hi"], 1)
                    if st.on(0):
                        act.wait_ge(sig["f_dispatch"], st.done(0))
                        nc.scalar.activation(f_dp[:, HI], f_ring[:, DISPATCH], COPY).then_inc(sig["f_dispatch_hi"], 1)
                    if st.on(2) and more:
                        act_logits(k - 2, (c + 1) * NQ + k - 1)
                quads(act, c, body)

            chunks(act, act_chunk)
            for g in range(B // NORM_GROUP):
                act.wait_ge(sig["f_negmean"], g + 1)
                for b in range(g * NORM_GROUP, (g + 1) * NORM_GROUP):
                    if b:
                        act.wait_ge(sig["f_squares"], b)
                    nc.scalar.activation(norm_junk[:, b % 2], acc[:, b, :], ACT.Square, bias=n_negmean[:, b:b + 1],
                                             accum_out=n_squares[:, b:b + 1]).then_inc(sig["f_squares"], 1)

        @block.vector
        def _(dve):
            dve.wait_ge(sig["constants_in"], DMA * 4)
            nc.vector.tensor_scalar(far_ident, ident[:, :], FAR, None, ALU.mult).then_inc(sig["far_ident"], 1)
            nc.vector.tensor_scalar(far16, band, FAR, None, ALU.mult).then_inc(sig["far16"], 1)
            pairs = lam_in.rearrange("p (i two) b c -> p i two b c", two=2)
            nc.vector.tensor_tensor(lam_prod, pairs[:, :, 0], pairs[:, :, 1], ALU.mult).then_inc(sig["lam_prod"], 1)
            dve.wait_ge(sig["lam_prod"], 1)
            nc.vector.reduce_sum(lam_sum, lam_prod, AX.X).then_inc(sig["lam_sum"], 1)
            dve.wait_ge(sig["lam_exp"], 1)
            nc.vector.tensor_tensor(lam_dif, lam_exp[:, 1, :], lam_exp[:, 0, :], ALU.subtract).then_inc(sig["lam_dif"], 1)
            dve.wait_ge(sig["lam_dif"], 1)
            nc.vector.tensor_scalar(neg_lam, lam_dif, -LAMBDA_INIT, None, ALU.add).then_inc(sig["neg_lam"], 1)
            nc.vector.tensor_scalar(w_rows2, w_rows, OUT_SCALE, None, ALU.mult).then_inc(sig["w_rows2"], 1)
            dve.wait_ge(sig["neg_lam"], 1)
            dve.wait_ge(sig["w_rows2"], 1)
            def scale_piece(i):
                dve.wait_ge(sig[f"weights_in{i % STAGES}"], DMA * (i // STAGES + 1))
                col, stage = i * PIECE, w_stage[:, i % STAGES]
                scale = SCORE_SCALE if SQ <= col < SK or CQ <= col < CK else 1.0
                for k in range(DT):
                    last = nc.vector.tensor_scalar(stage[:, k], stage[:, k], w_rows2[:, k:k + 1] if CO <= col else scale, None, ALU.mult)
                last.then_inc(sig["weights_scaled"], 1)

            scale_piece(0)
            for i in range(NPIECE):
                if i + 1 < NPIECE:
                    scale_piece(i + 1)
                dve.wait_ge(sig["weights_hi"], i + 1)
                col = i * PIECE
                nc.vector.tensor_tensor(w_parts[:, LO, :, col:col + PIECE], w_stage[:, i % STAGES], w_parts[:, HI, :, col:col + PIECE], ALU.subtract).then_inc(sig["weights_lo"], 1)

            def body(st):
                def lo_turn(use, dst, hi, tiles, step=st):
                    src = bank[f"turn{[u for u, _ in TURN].index(use) % 2}"]
                    dve.wait_ge(sig["turn_hi"], step.count("turn_hi", use))
                    nc.vector.tensor_tensor(dst, in3(src[:, 0:tiles * P], tiles), hi, ALU.subtract).then_inc(sig["turn_read"], 1)

                def lo_T(use, parts, step=st):
                    lo_turn(use, parts[:, :, LO], parts[:, :, HI], parts.shape[1], step)

                def lo_q(use, buf, part):
                    at = [buf[:, st.slot_of(part), :, p, :].rearrange("p o a s -> p (o a) s") for p in (HI, LO)]
                    lo_turn(use, at[LO], at[HI], 4)

                def lo_v(use, buf, part):
                    at = [in3(buf[:, st.slot_of(part), p, :].rearrange("p o d -> p (o d)"), DT) for p in (HI, LO)]
                    lo_turn(use, at[LO], at[HI], DT)

                def self_max(u):
                    if st.on("s_core"):
                        n = st.count("s_score", f"s{u}")
                        dve.wait_ge(sig["s_score_written"], n)
                        nc.vector.reduce_max(s_negmax[:, u * Q4:(u + 1) * Q4], in3(bank["score_s"][:, :], Q4), AX.X, negate=True).then_inc(sig["s_max"], 1)

                def add_mask(g):
                    name = ["score_a", "score_b"][g % 2]
                    for i in range(4):
                        last = nc.vector.tensor_tensor_reduce(c_prob[:, 4 * g + i, :], bank[name][:, i * S:(i + 1) * S], c_mask[:, 2 * g + i // 2, :],
                                                              -1.0, HIGHEST, ALU.add, ALU.min, c_negmax[:, 4 * g + i:4 * g + i + 1])
                    last.then_inc(sig["c_score_read"], 1)

                def slot_start(slot):
                    if st.on("c_core"):
                        dve.wait_ge(sig[f"c_mask{slot}"], DMA * (st.b("c_core") + 1))
                        dve.wait_ge(sig["c_score_written"], st.count("c_score", f"ca{slot}"))
                    self_max(slot)
                    if st.on("c_core"):
                        add_mask(2 * slot)

                def slot_middle(slot, more=lambda: None):
                    v, kind = earlier(slot, 1)
                    core, blend = st.on("c_core"), st.on(f"c_{kind}")
                    heads = slice(v * Q4, (v + 1) * Q4)
                    if blend:
                        n = st.count("blend", f"c{v}")
                        sums = one(c_sum[:, st.slot_of(f"c_{kind}"), :]).rearrange("p (h i) -> p h i", i=2)
                        dve.wait_ge(sig["c_exp"], st.made("c_score", f"cb{v}", kind))
                        nc.vector.reciprocal(c_r2[:, heads], sums[:, heads, 1]).then_inc(sig["c_r2"], 1)
                    prob_lo("c", slot)
                    if core:
                        dve.wait_ge(sig["c_score_written"], st.count("c_score", f"cb{slot}"))
                    if blend:
                        dve.wait_ge(sig["c_r2"], n)
                        nc.vector.tensor_tensor(c_ratio[:, heads], c_r2[:, heads], sums[:, heads, 0], ALU.mult).then_inc(sig["c_ratio"], 1)
                    if core:
                        add_mask(2 * slot + 1)
                    if blend:
                        dve.wait_ge(sig["c_ratio"], n)
                        nc.vector.tensor_tensor(c_blend[:, heads], c_ratio[:, heads], neg_lam[:, heads], ALU.mult).then_inc(sig["c_blend"], 1)
                    more()
                    prob_lo("s", slot)

                def prob_lo(which, slot):
                    u, kind = earlier(slot, 2)
                    if st.on(f"{which}_{kind}"):
                        pT = c_pT if which == "c" else s_pT
                        dve.wait_ge(sig[f"{which}_prob_hi"], st.count(f"{which}_prob", f"{which}{u}"))
                        nc.vector.tensor_tensor(pT[:, u % 2, LO], in3(bank[f"prob_{which}"][:, :], Q4), pT[:, u % 2, HI], ALU.subtract).then_inc(sig[f"{which}_prob_read"], 1)

                def norm_mean(part, use, res, summed, total, negmean):
                    dve.wait_ge(sig["turn_written"], st.count("turn", use))
                    nc.vector.scalar_tensor_tensor(summed, bank[f"turn{[u for u, _ in TURN].index(use) % 2}"][:, 0:D], 1.0, res, ALU.mult, ALU.add,
                                                   accum_out=total).then_inc(sig["turn_read"], 1)
                    dve.wait_ge(sig["turn_read"], st.count("turn", use))
                    nc.vector.tensor_scalar(negmean, total, -1.0 / D, None, ALU.mult).then_inc(sig[f"{part}_summed"], 1)

                def norm_variance(part, b, squares, veps):
                    dve.wait_ge(sig[f"{part}_squares"], b + 1)
                    nc.vector.tensor_scalar(veps, squares, 1.0 / D, LN_EPS, ALU.mult, ALU.add).then_inc(sig[f"{part}_veps"], 1)

                def norm_apply(part, b, summed, negmean, rstd, dst, name):
                    dve.wait_ge(sig[f"{part}_rstd"], b + 1)
                    nc.vector.tensor_scalar(dst, summed, negmean, rstd, ALU.add, ALU.mult).then_inc(sig[name], 1)

                def turned_inputs():
                    if st.on("s_pre"):
                        lo_T("s_xT", s_xT)
                    if st.on("c_pre"):
                        lo_T("c_cT", c_cT)

                def turned_normed(step):
                    if step.on("s_tail"):
                        lo_T("x1T", c_xT, step)
                    if step.on("c_tail"):
                        at = xT[:, :, :, bass.ds(step.b("c_tail") * S, S)]
                        lo_turn("x2T", at[:, LO], at[:, HI], DT, step)

                slot_start(0)
                turned_normed(st.last())
                slot_middle(0)
                if st.on("s_tail"):
                    lo_T("s_oT", s_oT)
                if st.on("c_tail"):
                    dve.wait_ge(sig["c_rms"], st.b("c_tail") + 1)
                    nc.vector.tensor_tensor(in3(c_o, H), in3(c_oraw, H), spread(c_rms, DH), ALU.mult).then_inc(sig["c_o"], 1)
                slot_start(1)
                if st.on("c_tail"):
                    lo_T("c_oT", c_oT)
                if st.on("s_proj"):
                    lo_q("s_qk", s_qk, "s_proj")
                slot_middle(1)
                if st.on("s_tail"):
                    dve.wait_ge(sig["s_res"], DMA * (st.b("s_tail") + 1))
                    norm_mean("s", "s_wo", s_res, s_sum, s_total, s_negmean)
                slot_start(2)
                if st.on("c_tail"):
                    ctb = st.b("c_tail")
                    dve.wait_ge(sig["x1_kept"], ctb + 1)
                    norm_mean("c", "c_wo", x1_ring[:, bass.ds(ctb % X1_RING, 1), :].rearrange("p o d -> p (o d)"), c_sumx, c_total, c_negmean)
                if st.on("c_proj"):
                    lo_q("c_q", c_q, "c_proj")
                if st.on("s_tail"):
                    norm_variance("s", st.b("s_tail"), s_sq, s_veps)
                slot_middle(2)
                if st.on("c_proj"):
                    lo_T("c_k", c_k)
                if st.on("s_tail"):
                    if later(st.b("s_tail")):
                        dve.wait_ge(sig["x1_kept"], st.b("s_tail"))
                    norm_apply("s", st.b("s_tail"), s_sum, s_negmean, s_rstd, x1, "x1")
                if st.on("c_tail"):
                    norm_variance("c", st.b("c_tail"), c_sqx, c_veps)
                if st.on("s_late"):
                    b = st.b("s_late")
                    nc.vector.reciprocal(s_rsum, one(s_expsum[:, st.slot_of("s_late"), :])).then_inc(sig["s_rsum"], 1)
                if st.on("c_late"):
                    b = st.b("c_late")
                    sums = one(c_sum[:, st.slot_of("c_late"), :]).rearrange("p (h i) -> p h i", i=2)
                    nc.vector.reciprocal(c_rsum, sums[:, :, 0]).then_inc(sig["c_rsum"], 1)
                    dve.wait_ge(sig["value_written"], st.count("value", "s3" if st.on("s_late") else "c3"))
                    dve.wait_ge(sig["c_rsum"], b + 1)
                    nc.vector.tensor_tensor(in3(c_oraw, H), in3(bank["value"][:, 0:D], H), spread(c_rsum, DH), ALU.mult).then_inc(sig["c_value_read"], 1)
                if st.on("s_late"):
                    b = st.b("s_late")
                    dve.wait_ge(sig["value_written"], st.count("value", "s3"))
                    dve.wait_ge(sig["s_rsum"], b + 1)
                    nc.vector.tensor_tensor(in3(s_o, H), in3(bank["value"][:, D:2 * D], H), spread(s_rsum, DH), ALU.mult).then_inc(sig["s_o"], 1)
                slot_start(3)
                if st.on("s_proj"):
                    lo_v("s_v", s_v, "s_proj")
                if st.on("c_proj"):
                    lo_v("c_v", c_v, "c_proj")
                slot_middle(3, turned_inputs)
                if st.on("c_late"):
                    b = st.b("c_late")
                    dve.wait_ge(sig["c_sq"], b + 1)
                    nc.vector.reduce_sum(c_ss, in3(c_sq, H), AX.X).then_inc(sig["c_ss"], 1)
                if st.on("c_tail"):
                    ctb = st.b("c_tail")
                    if later(ctb):
                        dve.wait_ge(sig["x2_stored"], DMA * ctb)
                        dve.wait_ge(sig["x2_parts"], ctb)
                    norm_apply("c", ctb, c_sumx, c_negmean, c_rstd, x2, "x2")
                if st.on("c_late"):
                    dve.wait_ge(sig["c_ss"], b + 1)
                    nc.vector.tensor_scalar(c_ms, c_ss, 1.0 / DH, RMS_EPS, ALU.mult, ALU.add).then_inc(sig["c_ms"], 1)

            steps(dve, body)
            body(Step(STEPS))

            nc.vector.memset(fence[:, 1:2], 0.0).then_inc(sig["f_cleared"], 1)
            dve.wait_ge(sig["f_cleared"], 3)
            dve.wait_ge(sig["x2_parts_stored"], DMA * B)
            dve.wait_ge(sig["x2_stored"], DMA * B)
            nc.vector.memset(acc[:, 0:B // 4, :], 0.0).then_inc(sig["f_acc"], 1)
            nc.vector.memset(acc[:, B // 4:B // 2, :], 0.0).then_inc(sig["f_acc"], 1)
            nc.vector.memset(f_rowmax, -1e30).then_inc(sig["f_zero"], 1)
            nc.vector.memset(f_max4, -3e38).then_inc(sig["f_zero"], 1)
            nc.vector.memset(n_sum, 0.0).then_inc(sig["f_row_sum"], 1)

            def dve_phi(n):
                dve.wait_ge(sig["f_phi_hi"], n)
                nc.vector.tensor_tensor(f_phi[:, LO], f_phi_stage, f_phi[:, HI], ALU.subtract).then_inc(sig["f_phi_lo"], 1)

            def dve_maxima(g, n):
                dve.wait_ge(sig["f_logits_read"], n)
                dve.wait_ge(sig["f_max4"], n - 1)
                part = logits[:, bass.ds(g * Q4, Q4), :]
                nc.vector.tensor_tensor(f_max4, f_max4, part, ALU.max).then_inc(sig["f_max4"], 1)
                nc.vector.reduce_max(f_chunkmax[:, bass.ds(g * Q4, Q4)], part, AX.X).then_inc(sig["f_chunkmax"], 1)

            dve_phi(1)
            dve.wait_ge(sig["f_zero"], 2)
            dve.wait_ge(sig["f_acc_zero"], 1)
            dve.wait_ge(sig["f_logits_read"], 1)
            nc.vector.tensor_tensor(f_max4, f_max4, logits[:, 0:Q4, :], ALU.max).then_inc(sig["f_max4"], 1)
            nc.vector.reduce_max(f_chunkmax[:, 0:Q4], logits[:, 0:Q4, :], AX.X).then_inc(sig["f_chunkmax"], 1)
            with dve.Fori(1, NQ) as g:
                dve_maxima(g, g + 1)

            def shift(g):
                nc.vector.tensor_tensor(f_ring[:, g % RING], logits[:, g * Q4:(g + 1) * Q4, :], f_max.unsqueeze(1).broadcast_to([P, Q4, P]),
                                        ALU.subtract).then_inc(sig["f_shifted_dve"], 1)

            def slot_maxima(n):
                dve.wait_ge(sig["f_max4"], n * NQ)
                nc.vector.reduce_max(f_max, f_max4.rearrange("p q n -> p n q"), AX.X).then_inc(sig["f_max"], 1)
                dve.wait_ge(sig["f_max"], n)
                nc.vector.memset(f_max4, -3e38).then_inc(sig["f_max4_reset"], 1)
                shift(1)

            def add_exps(c, g):
                if g == 0:
                    return
                dve.wait_ge(sig["f_sum_exp"], c * NQ + g + 1)
                if g > 1:
                    dve.wait_ge(sig["f_sum4"], c * (NQ - 1) + g - 1)
                nc.vector.tensor_tensor(f_sum4, f_ring[:, 0] if g == 1 else f_sum4, f_ring[:, g % RING], ALU.add).then_inc(sig["f_sum4"], 1)

            def begin_sums(c):
                dve.wait_ge(sig["f_chunkmax"], (c + 1) * NQ)
                nc.vector.tensor_tensor(f_newmax, f_rowmax, f_chunkmax, ALU.max).then_inc(sig["f_newmax"], 1)
                shift(3)

            slot_maxima(1)
            begin_sums(0)

            def dve_chunk(c, more):
                dve.wait_ge(sig["f_newmax"], c + 1)
                nc.vector.tensor_tensor(f_diff, f_rowmax, f_newmax, ALU.subtract).then_inc(sig["f_diff"], 1)
                nc.vector.tensor_scalar(f_neg, f_newmax, -1.0, None, ALU.mult).then_inc(sig["f_neg"], 1)
                dve.wait_ge(sig["f_diff"], c + 1)
                nc.vector.tensor_copy(f_rowmax, f_newmax).then_inc(sig["f_rowmax"], 1)
                for i in range(ROUNDS):
                    for r in range(1, RING, 2):
                        g = RING * i + r
                        if i:
                            dve.wait_ge(sig["f_sum4"], c * (NQ - 1) + g - RING)
                        if i:
                            shift(g)
                    for r in range(RING):
                        add_exps(c, RING * i + r)
                dve.wait_ge(sig["f_sum4"], (c + 1) * (NQ - 1))
                nc.vector.reduce_sum(f_sum, f_sum4.rearrange("p q n -> p n q"), AX.X).then_inc(sig["f_sum"], 1)
                dve.wait_ge(sig["f_sum"], c + 1)
                nc.vector.reciprocal(f_rsum, f_sum).then_inc(sig["f_rsum"], 1)
                if more:
                    dve_phi(c + 2)
                dve.wait_ge(sig["f_keep"], c + 1)
                dve.wait_ge(sig["f_rowmax"], c + 1)
                dve.wait_ge(sig["f_max4_reset"], c + 1)
                dve.wait_ge(sig["f_row_sum"], c + 1)

                def body(st):
                    k = st.k

                    def y_lo(half):
                        if st.on(3):
                            dve.wait_ge(sig["f_y_hi"], st.done(3, 2) - 1 + half)
                            part = slice(2 * half, 2 * half + 2)
                            nc.vector.tensor_tensor(f_y[:, LO, part, :], in3(b_y[:, :], 2), f_y[:, HI, part, :], ALU.subtract).then_inc(sig["f_y_lo"], 1)

                    def accumulate(pair):
                        if st.on(3):
                            dve.wait_ge(sig["f_out"], st.done(3, 2) - 1 + pair)
                            for j in (2 * pair, 2 * pair + 1):
                                b = bass.ds((k - 3) * Q4 + j, 1)
                                last = nc.vector.scalar_tensor_tensor(one(acc[:, b, :]), one(acc[:, b, :]), f_keep[:, b],
                                                                      b_out[pair][:, (j % 2) * D:(j % 2 + 1) * D], ALU.mult, ALU.add)
                            last.then_inc(sig["f_acc"], 1)

                    final = isinstance(k, int) and k == F_LAST - 1
                    if not final:
                        y_lo(0)
                    if st.on(3) and more:
                        dve_maxima(k - 3, (c + 1) * NQ + k - 2)
                    if final:
                        if more:
                            slot_maxima(c + 2)
                        y_lo(0)
                    if st.on(2):
                        dve.wait_ge(sig["f_cT_hi"], st.done(2))
                        slot = bass.ds((k - 2) % 2, 1)
                        nc.vector.tensor_tensor(f_cT[:, slot, LO, :, :].rearrange("p o a b -> p (o a b)"), b_turn[:, :],
                                                    f_cT[:, slot, HI, :, :].rearrange("p o a b -> p (o a b)"), ALU.subtract).then_inc(sig["f_cT_lo"], 1)
                    y_lo(1)
                    if final and more:
                        begin_sums(c + 1)
                    if st.on(2):
                        if st.on(3):
                            dve.wait_ge(sig["f_y_psum"], st.done(3, 2))
                        for e in range(DT):
                            dve.wait_ge(sig["f_yT_psum"], st.done(2, 2) - 1 + e)
                            bias = f_bias[:, e, bass.ds(c * EC, EC)].unsqueeze(1).unsqueeze(3).broadcast_to([P, Q4, EC, SP_E])
                            nc.vector.tensor_tensor(f_yT[:, e].rearrange("p b (x s) -> p b x s", x=EC),
                                                        b_yT[e][:, :].rearrange("p (b x s) -> p b x s", b=Q4, x=EC), bias, ALU.add).then_inc(sig["f_yT"], 1)
                    if st.on(1):
                        for e in range(DT):
                            dve.wait_ge(sig["f_slots_hi"], st.done(1, 2) - 1 + e)
                            nc.vector.tensor_tensor(f_slT[:, LO, e], in3(b_slots[e][:, :], Q4), f_slT[:, HI, e], ALU.subtract).then_inc(sig["f_slots_lo"], 1)
                    accumulate(0)
                    accumulate(1)
                quads(dve, c, body)
                dve.wait_ge(sig["f_combine"], (c + 1) * NQ)
                nc.vector.tensor_tensor(f_kept, n_sum, f_keep, ALU.mult).then_inc(sig["f_kept"], 1)
                dve.wait_ge(sig["f_kept"], c + 1)
                nc.vector.tensor_tensor(n_sum, f_kept, f_csum, ALU.add).then_inc(sig["f_row_sum"], 1)

            dve.wait_ge(sig["f_bias_in"], DMA)
            chunks(dve, dve_chunk)
            dve.wait_ge(sig["f_acc"], NCH * NQ * 2 + 2)
            dve.wait_ge(sig["f_row_sum"], NCH + 1)
            nc.vector.reciprocal(n_rsum, n_sum).then_inc(sig["f_n_rsum"], 1)
            dve.wait_ge(sig["f_n_rsum"], 1)
            groups = range(B // NORM_GROUP)

            def add_residual(group):
                for b in range(group * NORM_GROUP, (group + 1) * NORM_GROUP):
                    g = b // Q4
                    if b % Q4 == 0:
                        dve.wait_ge(sig[f"f_res{g % 4}"], DMA * (g // 4 + 1))
                    nc.vector.scalar_tensor_tensor(acc[:, b, :], acc[:, b, :], n_rsum[:, b:b + 1], res_ring[:, g % 4, b % Q4],
                                                   ALU.mult, ALU.add, accum_out=n_total[:, b:b + 1]).then_inc(sig["f_added"], 1)
                cols = slice(group * NORM_GROUP, (group + 1) * NORM_GROUP)
                dve.wait_ge(sig["f_added"], NORM_GROUP * (group + 1))
                nc.vector.tensor_scalar(n_negmean[:, cols], n_total[:, cols], -1.0 / D, None, ALU.mult).then_inc(sig["f_negmean"], 1)

            def variances(group):
                cols = slice(group * NORM_GROUP, (group + 1) * NORM_GROUP)
                dve.wait_ge(sig["f_squares"], NORM_GROUP * (group + 1))
                nc.vector.tensor_scalar(n_veps[:, cols], n_squares[:, cols], 1.0 / D, LN_EPS, ALU.mult, ALU.add).then_inc(sig["f_veps"], 1)

            def norm(group):
                dve.wait_ge(sig["f_rstd"], group + 1)
                with dve.Fori(group * NORM_GROUP, (group + 1) * NORM_GROUP) as b:
                    b1 = bass.ds(b, 1)
                    nc.vector.tensor_scalar(one(acc[:, b1, :]), one(acc[:, b1, :]), n_negmean[:, b1], n_rstd[:, b1], ALU.add, ALU.mult).then_inc(sig["f_normed"], 1)

            add_residual(0)
            for group in groups:
                if group + 1 in groups:
                    add_residual(group + 1)
                variances(group)
                if group:
                    norm(group - 1)
            norm(groups[-1])

        @block.gpsimd
        def _(pool):
            pool.memset(minus_half, -0.5).then_inc(sig["zeros"], 1)
            pool.memset(c_rms, 0.0).then_inc(sig["zeros"], 1)
            pool.memset(s_kbd[:, :, :, :, :, :].rearrange("p a b c d e -> p (a b c d e)"), 0.0).then_inc(sig["s_kbd_zero"], 1)
            pool.memset(c_kbd.rearrange("p a b c d -> p (a b c d)"), 0.0).then_inc(sig["c_kbd_zero"], 1)
            pool.wait_ge(sig["zeros"], 2)

            def body(st):
                def reciprocal_root(name, ready, b, dst, src):
                    pool.wait_ge(sig[ready], b + 1)
                    pool.tensor_tensor(dst, src, minus_half[:, 0:src.shape[1]], ALU.pow).then_inc(sig[name], 1)

                def blend_unit(slot):
                    v, kind = earlier(slot, 1)
                    if not st.on(f"c_{kind}"):
                        return
                    n = st.count("blend", f"c{v}")
                    pool.wait_ge(sig["c_blend"], n)
                    pairs = c_prob[:, 2 * v * Q4:2 * (v + 1) * Q4, :].rearrange("p (h i) k -> p h i k", i=2)
                    first, second = pairs[:, :, 0], pairs[:, :, 1]
                    pool.tensor_tensor(second, second, spread(c_blend[:, v * Q4:(v + 1) * Q4], S), ALU.mult).then_inc(sig["scaled"], 1)
                    pool.wait_ge(sig["scaled"], n)
                    pool.tensor_tensor(first, first, second, ALU.add).then_inc(sig["blended"], 1)

                blend_unit(0)
                blend_unit(1)
                if st.on("s_tail"):
                    reciprocal_root("s_rstd", "s_veps", st.b("s_tail"), s_rstd, s_veps)
                blend_unit(2)
                if st.on("c_tail"):
                    reciprocal_root("c_rstd", "c_veps", st.b("c_tail"), c_rstd, c_veps)
                if st.on("c_late"):
                    b = st.b("c_late")
                    pool.wait_ge(sig["c_value_read"], b + 1)
                    pool.tensor_tensor(c_sq, c_oraw, c_oraw, ALU.mult).then_inc(sig["c_sq"], 1)
                blend_unit(3)
                if st.on("c_tail"):
                    b = st.b("c_tail")
                    pool.wait_ge(sig["x2_hi"], b + 1)
                    if later(b):
                        pool.wait_ge(sig["x2_parts_stored"], DMA * b)
                    pool.tensor_tensor(x2_parts[:, LO, :], x2, x2_parts[:, HI, :], ALU.subtract).then_inc(sig["x2_parts"], 1)
                if st.on("c_late"):
                    reciprocal_root("c_rms", "c_ms", st.b("c_late"), c_rms, c_ms)

            steps(pool, body)

            pool.memset(fence[:, 2:3], 0.0).then_inc(sig["f_cleared"], 1)
            pool.wait_ge(sig["f_cleared"], 3)
            pool.wait_ge(sig["x2_parts_stored"], DMA * B)
            pool.wait_ge(sig["x2_stored"], DMA * B)
            pool.memset(acc[:, B // 2:B, :], 0.0).then_inc(sig["f_acc_zero"], 1)
            pool.memset(n_half, -0.5).then_inc(sig["f_half"], 1)
            pool.wait_ge(sig["f_half"], 1)

            def expert_lo(c, x_):
                pool.wait_ge(sig["f_w_hi"], c * EC + x_ + 1)
                pool.tensor_tensor(f_w[:, LO, :, x_, :], f_w_stage[:, x_ % 2], f_w[:, HI, :, x_, :], ALU.subtract).then_inc(sig["f_w_lo"], 1)

            assert EARLY_EXPERTS == 2

            def pool_chunk(c, more):
                f_max_b = f_max.unsqueeze(1).broadcast_to([P, Q4, P])
                f_rsum_b = f_rsum.unsqueeze(1).broadcast_to([P, Q4, P])
                pool.wait_ge(sig["f_max"], c + 1)
                for i in range(ROUNDS):
                    for r in range(0, RING, 2):
                        g = RING * i + r
                        if g == 2:
                            pool.wait_ge(sig["f_shifted_dve"], c * (NQ // 2) + 2)
                        if i:
                            pool.wait_ge(sig["f_sum4"], c * (NQ - 1) + max(g - RING, 1))
                        pool.tensor_tensor(f_ring[:, r], logits[:, g * Q4:(g + 1) * Q4, :], f_max_b, ALU.subtract).then_inc(sig["f_shifted_pool"], 1)
                        if g in (0, 2):
                            expert_lo(c, g // 2)
                    for x_ in ROUND_EXPERTS[i]:
                        expert_lo(c, x_)

                def body(st):
                    k = st.k
                    if st.on(0):
                        if later(k):
                            pool.wait_ge(sig["f_dispatch_lo"], st.done(1))
                        else:
                            pool.wait_ge(sig["f_sum4"], c * (NQ - 1) + NQ - RING)
                        pool.tensor_tensor(f_ring[:, DISPATCH], logits[:, bass.ds(k * Q4, Q4), :], f_max_b, ALU.subtract).then_inc(sig["f_d_shifted"], 1)
                        if not later(k):
                            pool.wait_ge(sig["f_rsum"], c + 1)
                        pool.wait_ge(sig["f_d_exp"], st.done(0))
                        pool.tensor_tensor(f_ring[:, DISPATCH], f_ring[:, DISPATCH], f_rsum_b, ALU.mult).then_inc(sig["f_dispatch"], 1)
                        pool.wait_ge(sig["f_dispatch_hi"], st.done(0))
                        pool.tensor_tensor(f_dp[:, LO], f_ring[:, DISPATCH], f_dp[:, HI], ALU.subtract).then_inc(sig["f_dispatch_lo"], 1)
                quads(pool, c, body)

            chunks(pool, pool_chunk)
            for g in range(B // NORM_GROUP):
                cols = slice(g * NORM_GROUP, (g + 1) * NORM_GROUP)
                pool.wait_ge(sig["f_veps"], g + 1)
                pool.tensor_tensor(n_rstd[:, cols], n_veps[:, cols], n_half, ALU.pow).then_inc(sig["f_rstd"], 1)


def _layout(inputs):
    a = {k: np.asarray(v) for k, v in inputs.items()}
    d = a["x"].shape[2]
    s = a["x"].shape[1]
    p = 128
    weights = np.concatenate([a["L0_attn_Wq"].T, a["L0_attn_Wk"].T, a["L0_attn_Wv"].T, a["L0_attn_Wo"].T,
                              a["L0_xattn_W_q"], a["L0_xattn_W_k"], a["L0_xattn_W_v"], a["L0_xattn_W_o"]], axis=1)
    heads = a["L0_xattn_lambda_q1"].shape[0]
    lambdas = np.stack([a[f"L0_xattn_lambda_{n}"] for n in ("q1", "k1", "q2", "k2")]).reshape(1, -1)
    idx = np.arange(s)
    seen = np.abs(idx[:, None] - idx[None, :]) <= 32
    seen[0, :] = True
    seen[:, 0] = True
    return {
        "x": a["x"], "ctx": a["ctx_1024"], "mask": a["mask_Bx16xSxS2_ff0"],
        "w_all": weights.reshape(d // p, p, -1).transpose(1, 0, 2),
        "w_scale": np.tile(a["L0_xattn_rms_scale"], heads).reshape(d // p, p).T,
        "lambdas": np.broadcast_to(lambdas, (p, lambdas.size)),
        "phi": a["L0_ffn_phi"].reshape(d // p, p, -1).transpose(1, 0, 2),
        "w_ffn": a["L0_ffn_W"].reshape(-1, d // p, p, d).transpose(0, 2, 1, 3),
        "b_ffn": a["L0_ffn_b"].T.reshape(d // p, p, -1).transpose(1, 0, 2),
        "ident": np.eye(p, dtype=np.float32),
        "band": np.where(seen, np.float32(0), np.float32(-1)).astype(np.float32),
    }


def kernel(**inputs):
    import concourse.bacc as _bacc
    from concourse.bass_utils import run_bass_kernel_spmd as _run

    nc = _bacc.Bacc("TRN2", target_bir_lowering=False, num_devices=1)
    arrays, args = {}, []
    for name, a in _layout(inputs).items():
        a = np.ascontiguousarray(a)
        arrays[f"in_{name}_dram"] = a
        args.append(nc.dram_tensor(f"in_{name}_dram", a.shape, mybir.dt.from_np(a.dtype), kind="ExternalInput").ap())
    out = nc.dram_tensor("out_dram", inputs["x"].shape, mybir.dt.float32, kind="ExternalOutput").ap()
    decoder_layer(nc, *args, out)
    return _run(nc, [arrays], core_ids=[0]).results[0]["out_dram"]
```
